# Optimizing a Trainium2 kernel written in Bass

```python
import numpy as np
import jax
import jax.numpy as jnp

def _softmax(x, axis=-1):
    return jax.nn.softmax(x, axis=axis)

def _gelu(x):
    return jax.nn.gelu(x, approximate=True)

def _silu(x):
    return jax.nn.silu(x)

def _sigmoid(x):
    return jax.nn.sigmoid(x)

def _layernorm(x, axis=-1, eps=1e-05):
    m = jnp.mean(x, axis=axis, keepdims=True)
    v = jnp.var(x, axis=axis, keepdims=True)
    return (x - m) / jnp.sqrt(v + eps)

def _scatter_add(tgt, idx, src, axis=0):
    return tgt.at[idx].add(src)

def _segment_sum(src, seg, n):
    return jax.ops.segment_sum(src, seg, n)
kernel_name = 'mk_sandwich_d4_jaxref_r8_901afc'

def setup_inputs(seed: int=0):
    np.random.seed(seed)
    _w = jnp.asarray

    def _L0_attn_setup():
        import jax, jax.numpy as jnp
        import numpy as np
        D_MODEL, D_STATE, D_CONV, EXPAND = (128, 16, 4, 2)
        D_INNER = EXPAND * D_MODEL
        BATCH, SEQ = (2, 256)

        def _forward(x, in_proj_w, conv_w, conv_b, dt_w, dt_b, A_log, D, B_w, C_w, out_w):
            xz = x @ in_proj_w.T
            xc, z = jnp.split(xz, 2, axis=-1)
            h = jnp.transpose(xc, (0, 2, 1))
            h = jnp.pad(h, ((0, 0), (0, 0), (D_CONV - 1, 0)))
            h = jax.lax.conv_general_dilated(h, conv_w, (1,), 'VALID', dimension_numbers=('NCH', 'OIH', 'NCH'))
            h = h + conv_b[None, :, None]
            u = jnp.transpose(h, (0, 2, 1))
            dt = jnp.clip(jax.nn.sigmoid(u @ dt_w.T + dt_b), 0.0001, 1.0)
            A = -jnp.exp(A_log)
            Bm = u @ B_w.T
            Cm = u @ C_w.T
            u_t = jnp.transpose(u, (1, 0, 2))
            dt_t = jnp.transpose(dt, (1, 0, 2))
            B_t = jnp.transpose(Bm, (1, 0, 2))
            C_t = jnp.transpose(Cm, (1, 0, 2))

            def step(state, inp):
                ut, dtt, bt, ct = inp
                dA = jnp.exp(jnp.clip(dtt[:, :, None] * A, -5.0, 5.0))
                dB = dtt[:, :, None] * bt[:, None, :] * ut[:, :, None]
                state = dA * state + dB + 1e-06
                y = jnp.sum(state * ct[:, None, :], axis=-1) + D * ut
                return (state, y)
            state0 = jnp.zeros((x.shape[0], D_INNER, D_STATE), x.dtype)
            _, ys = jax.lax.scan(step, state0, (u_t, dt_t, B_t, C_t))
            y = jnp.transpose(ys, (1, 0, 2))
            y = y * jax.nn.silu(z)
            return y @ out_w.T
        key = jax.random.key(seed)
        ks = jax.random.split(key, 10)
        inv = lambda n: 1.0 / np.sqrt(n)
        return {'x': jax.random.normal(ks[0], (BATCH, SEQ, D_MODEL), jnp.float32), 'in_proj_w': jax.random.uniform(ks[1], (2 * D_INNER, D_MODEL), jnp.float32, -inv(D_MODEL), inv(D_MODEL)), 'conv_w': jax.random.uniform(ks[2], (D_INNER, D_INNER, D_CONV), jnp.float32, -inv(D_INNER * D_CONV), inv(D_INNER * D_CONV)), 'conv_b': jax.random.uniform(ks[3], (D_INNER,), jnp.float32, -inv(D_INNER * D_CONV), inv(D_INNER * D_CONV)), 'dt_w': jax.random.uniform(ks[4], (D_INNER, D_INNER), jnp.float32, -inv(D_INNER), inv(D_INNER)), 'dt_b': jax.random.uniform(ks[5], (D_INNER,), jnp.float32, -inv(D_INNER), inv(D_INNER)), 'A_log': jax.random.normal(ks[6], (D_INNER, D_STATE), jnp.float32) * 0.01, 'D': jnp.ones((D_INNER,), jnp.float32), 'B_w': jax.random.uniform(ks[7], (D_STATE, D_INNER), jnp.float32, -inv(D_INNER), inv(D_INNER)), 'C_w': jax.random.uniform(ks[8], (D_STATE, D_INNER), jnp.float32, -inv(D_INNER), inv(D_INNER)), 'out_w': jax.random.uniform(ks[9], (D_MODEL, D_INNER), jnp.float32, -inv(D_INNER), inv(D_INNER))}
    _L0_attn_in = _L0_attn_setup()

    def _L0_ffn_setup():
        import jax, jax.numpy as jnp
        import numpy as np
        B, T, C, H, E, K, F = (2, 256, 128, 16, 8, 2, 256)
        EPS = 1e-05

        def layernorm(x, w):
            m = x.mean(-1, keepdims=True)
            v = x.var(-1, keepdims=True)
            return (x - m) * jax.lax.rsqrt(v + EPS) * w

        def attention(x, c_attn_w, c_proj_w):
            b, t, c = x.shape
            hd = c // H
            q, k, v = jnp.split(x @ c_attn_w, 3, axis=-1)
            q = q.reshape(b, t, H, hd).transpose(0, 2, 1, 3)
            k = k.reshape(b, t, H, hd).transpose(0, 2, 1, 3)
            v = v.reshape(b, t, H, hd).transpose(0, 2, 1, 3)
            att = jnp.einsum('bhqd,bhkd->bhqk', q, k) / jnp.sqrt(jnp.asarray(hd, x.dtype))
            causal = jnp.tril(jnp.ones((t, t), bool))
            att = jnp.where(causal, att, jnp.asarray(-jnp.inf, att.dtype))
            att = jax.nn.softmax(att, axis=-1)
            y = jnp.einsum('bhqk,bhkd->bhqd', att, v)
            y = y.transpose(0, 2, 1, 3).reshape(b, t, c)
            return y @ c_proj_w

        def moe_mlp(x, router_w, w1, w2):
            b, t, c = x.shape
            xf = x.reshape(-1, c)
            router_logits = xf @ router_w
            probs = jax.nn.softmax(router_logits.astype(jnp.float32), axis=-1)
            rw, sel = jax.lax.top_k(probs, K)
            rw = rw / rw.sum(axis=-1, keepdims=True)
            rw = rw.astype(x.dtype)
            w1e = w1.reshape(c, E, F).transpose(1, 0, 2)
            w2e = w2.reshape(E, F, c)
            h = jax.nn.gelu(jnp.einsum('nc,ecf->enf', xf, w1e), approximate=False)
            y_all = jnp.einsum('enf,efc->nec', h, w2e)
            y_sel = jnp.take_along_axis(y_all, sel[:, :, None], axis=1)
            y = (y_sel * rw[:, :, None]).sum(axis=1)
            return y.reshape(b, t, c)
        key = jax.random.key(seed)
        ks = jax.random.split(key, 6)
        s = 0.02
        return {'x': jax.random.normal(ks[0], (B, T, C), jnp.float32), 'ln1_w': jnp.ones((C,), jnp.float32), 'c_attn_w': jax.random.normal(ks[1], (C, 3 * C), jnp.float32) * s, 'c_proj_w': jax.random.normal(ks[2], (C, C), jnp.float32) * s, 'ln2_w': jnp.ones((C,), jnp.float32), 'router_w': jax.random.normal(ks[3], (C, E), jnp.float32) * s, 'w1': jnp.clip(jax.random.normal(ks[4], (C, E * F), jnp.float32) * s, -0.06, 0.06), 'w2': jnp.clip(jax.random.normal(ks[5], (E * F, C), jnp.float32) * s, -0.06, 0.06)}
    _L0_ffn_in = _L0_ffn_setup()

    def _L1_attn_setup():
        import jax, jax.numpy as jnp
        import numpy as np
        B, T, C = (2, 256, 128)
        NH = 16
        HS = C // NH
        BD = max(HS // 4, 16)
        HORIZON = 32

        def _windows(t, delta):
            padded = jnp.pad(t, ((0, 0), (0, 0), (delta - 1, 0), (0, 0)))
            idx = jnp.arange(t.shape[2])[:, None] + jnp.arange(delta)[None, :]
            return padded[:, :, idx]
        key = jax.random.key(seed)
        ks = jax.random.split(key, 16)
        s = 0.02
        inp = {'x': jax.random.normal(ks[0], (B, T, C), dtype=jnp.float32), 'w_disp': jax.random.normal(ks[1], (C, NH * BD), dtype=jnp.float32) * s, 'b_disp': jnp.zeros((NH * BD,), dtype=jnp.float32), 'w_val': jax.random.normal(ks[2], (C, C), dtype=jnp.float32) * s, 'b_val': jnp.zeros((C,), dtype=jnp.float32), 'rel_pos_emb': jax.random.normal(ks[3], (HORIZON, BD), dtype=jnp.float32) * s, 'w_state': jax.random.normal(ks[4], (BD, BD), dtype=jnp.float32) * s, 'b_state': jnp.zeros((BD,), dtype=jnp.float32), 'w_strain': jax.random.normal(ks[5], (BD, BD), dtype=jnp.float32) * s, 'b_strain': jnp.zeros((BD,), dtype=jnp.float32), 'w_state_i': jax.random.normal(ks[6], (BD, BD), dtype=jnp.float32) * s, 'w_state_j': jax.random.normal(ks[7], (BD, BD), dtype=jnp.float32) * s, 'w_pos': jax.random.normal(ks[8], (BD, BD), dtype=jnp.float32) * s, 'w_bond_out': jax.random.normal(ks[9], (BD, 1), dtype=jnp.float32) * s, 'b_bond_out': jnp.zeros((1,), dtype=jnp.float32), 'w_damage': jax.random.normal(ks[10], (BD, BD), dtype=jnp.float32) * s, 'b_damage': jnp.zeros((BD,), dtype=jnp.float32), 'w_damage_out': jax.random.normal(ks[11], (BD, 1), dtype=jnp.float32) * s, 'b_damage_out': jnp.full((1,), -3.0, dtype=jnp.float32), 'w_cproj': jax.random.normal(ks[12], (C, C), dtype=jnp.float32) * s, 'b_cproj': jnp.zeros((C,), dtype=jnp.float32)}
        return inp
    _L1_attn_in = _L1_attn_setup()

    def _L1_ffn_setup():
        import jax, jax.numpy as jnp
        import numpy as np
        B, S, H, E, K = (2, 256, 128, 8, 2)
        FF = 4 * H
        EPS = 1e-05
        key = jax.random.key(seed)
        ks = jax.random.split(key, 5)
        rn = lambda k, shape, scale: jax.random.normal(k, shape, dtype=jnp.float32) * scale
        return {'x': rn(ks[0], (B, S, H), 1.0), 'router_W': rn(ks[1], (H, E), H ** (-0.5)), 'router_b': jnp.zeros((E,), jnp.float32), 'ln_g': jnp.ones((E, H), jnp.float32), 'ln_b': jnp.zeros((E, H), jnp.float32), 'W1': rn(ks[2], (E, H, FF), H ** (-0.5)), 'b1': jnp.zeros((E, FF), jnp.float32), 'W2': rn(ks[3], (E, FF, H), FF ** (-0.5)), 'b2': jnp.zeros((E, H), jnp.float32)}
    _L1_ffn_in = _L1_ffn_setup()

    def _L2_attn_setup():
        import jax, jax.numpy as jnp
        import numpy as np
        NUM_HEADS = 16
        EPS = 1e-12

        def _l2norm(t):
            n = jnp.linalg.norm(t, axis=-1, keepdims=True)
            return t / jnp.maximum(n, EPS)
        key = jax.random.key(seed)
        ks = jax.random.split(key, 5)
        N, C, d = (16, 128, 128)
        x = jax.random.normal(ks[0], (N, C, d), dtype=jnp.float32)
        Wq = jax.random.normal(ks[1], (d, d), dtype=jnp.float32) * 0.02
        Wk = jax.random.normal(ks[2], (d, d), dtype=jnp.float32) * 0.02
        Wv = jax.random.normal(ks[3], (d, d), dtype=jnp.float32) * 0.02
        Wo = jax.random.normal(ks[4], (d, d), dtype=jnp.float32) * 0.02
        norm_const = 0.5 * jnp.ones((1, NUM_HEADS, 1, 1), dtype=jnp.float32)
        return {'x': x, 'Wq': Wq, 'Wk': Wk, 'Wv': Wv, 'Wo': Wo, 'norm_const': norm_const}
    _L2_attn_in = _L2_attn_setup()

    def _L2_ffn_setup():
        import jax, jax.numpy as jnp
        import numpy as np
        DIM = 128
        DEPTH = 2
        HEADS = 8
        DIM_HEAD = 64
        WINDOW = 64
        INNER = HEADS * DIM_HEAD
        HID = int(DIM * 4 * 2 / 3)
        B, N = (2, 1024)
        QK_SCALE = 8.0

        def shift_token(t):
            t1, t2 = jnp.split(t, 2, axis=-1)
            t2 = jnp.pad(t2, ((0, 0), (1, 0), (0, 0)))[:, :-1]
            return jnp.concatenate([t1, t2], axis=-1)

        def l2norm(t):
            return t / jnp.clip(jnp.linalg.norm(t, axis=-1, keepdims=True), 1e-12)

        def rotate_half(x):
            x1, x2 = jnp.split(x, 2, axis=-1)
            return jnp.concatenate([-x2, x1], axis=-1)

        def rotary_xpos(q, k):
            n = q.shape[-2]
            half_idx = jnp.arange(0, DIM_HEAD, 2, dtype=jnp.float32)
            inv_freq = 1.0 / 10000.0 ** (half_idx / DIM_HEAD)
            t = jnp.arange(n, dtype=jnp.float32)
            freqs = t[:, None] * inv_freq[None, :]
            freqs = jnp.concatenate([freqs, freqs], axis=-1)
            base = (half_idx + 0.4 * DIM_HEAD) / (1.4 * DIM_HEAD)
            power = (t - n // 2) / float(WINDOW // 2)
            scale = base[None, :] ** power[:, None]
            scale = jnp.concatenate([scale, scale], axis=-1)
            cos, sin = (jnp.cos(freqs), jnp.sin(freqs))
            q = q * cos * scale + rotate_half(q) * sin * scale
            k = k * cos / scale + rotate_half(k) * sin / scale
            return (q, k)

        def local_attention(q, k, v):
            b, h, n, d = q.shape
            w = n // WINDOW
            bq = q.reshape(b, h, w, WINDOW, d) * QK_SCALE
            bk = k.reshape(b, h, w, WINDOW, d)
            bv = v.reshape(b, h, w, WINDOW, d)

            def look_around(t):
                p = jnp.pad(t, ((0, 0), (0, 0), (1, 0), (0, 0), (0, 0)))
                return jnp.concatenate([p[:, :, :w], p[:, :, 1:]], axis=3)
            bk, bv = (look_around(bk), look_around(bv))
            bt = jnp.arange(n).reshape(w, WINDOW)
            btp = jnp.pad(bt, ((1, 0), (0, 0)), constant_values=-1)
            btk = jnp.concatenate([btp[:w], btp[1:]], axis=1)
            sim = jnp.einsum('bhwid,bhwjd->bhwij', bq, bk)
            i = bt[:, :, None]
            j = btk[:, None, :]
            mask = (i < j) | (i > j + WINDOW) | (j == -1)
            sim = jnp.where(mask, -jnp.finfo(sim.dtype).max, sim)
            attn = jax.nn.softmax(sim, axis=-1)
            out = jnp.einsum('bhwij,bhwjd->bhwid', attn, bv)
            return out.reshape(b, h, n, d)

        def _layer(x, wqkv, qs, ksc, wo, lg, lb, w1, b1, w2, b2):
            b, n, _ = x.shape
            h = shift_token(x)
            qkv = h @ wqkv
            q, k, v = jnp.split(qkv, 3, axis=-1)
            to_heads = lambda t: t.reshape(b, n, HEADS, DIM_HEAD).transpose(0, 2, 1, 3)
            q, k, v = (to_heads(q), to_heads(k), to_heads(v))
            q = l2norm(q) * qs
            k = l2norm(k) * ksc
            q, k = rotary_xpos(q, k)
            o = local_attention(q, k, v)
            o = o.transpose(0, 2, 1, 3).reshape(b, n, INNER)
            x = x + o @ wo
            h = shift_token(x)
            mu = h.mean(-1, keepdims=True)
            var = h.var(-1, keepdims=True)
            h = (h - mu) / jnp.sqrt(var + 1e-05) * lg + lb
            h = h @ w1 + b1
            a, g = jnp.split(h, 2, axis=-1)
            h = a * jax.nn.gelu(g, approximate=False)
            x = x + h @ w2 + b2
            return x
        key = jax.random.key(seed)
        ks = jax.random.split(key, 6)
        return {'x': jax.random.normal(ks[0], (B, N, DIM), jnp.float32), 'wqkv': jax.random.normal(ks[1], (DEPTH, DIM, 3 * INNER), jnp.float32) * 0.02, 'q_scale': jnp.ones((DEPTH, DIM_HEAD), jnp.float32), 'k_scale': jnp.ones((DEPTH, DIM_HEAD), jnp.float32), 'wo': jax.random.normal(ks[2], (DEPTH, INNER, DIM), jnp.float32) * 0.02, 'ln_g': jnp.ones((DEPTH, DIM), jnp.float32), 'ln_b': jnp.zeros((DEPTH, DIM), jnp.float32), 'w1': jax.random.normal(ks[3], (DEPTH, DIM, 2 * HID), jnp.float32) * 0.02, 'b1': jnp.zeros((DEPTH, 2 * HID), jnp.float32), 'w2': jax.random.normal(ks[4], (DEPTH, HID, DIM), jnp.float32) * 0.02, 'b2': jnp.zeros((DEPTH, DIM), jnp.float32)}
    _L2_ffn_in = _L2_ffn_setup()

    def _L3_attn_setup():
        import jax, jax.numpy as jnp
        import numpy as np
        import math
        N_EMBD = 128
        NUM_HEADS = 16
        HEAD_DIM = N_EMBD // NUM_HEADS

        def alibi_slopes(num_heads):
            x = (2 ** 8) ** (1.0 / num_heads)
            return jnp.array([1.0 / x ** (i + 1) for i in range(num_heads)], dtype=jnp.float32)
        key = jax.random.key(seed)
        k1, k2 = jax.random.split(key)
        x = jax.random.normal(k1, (2, 256, N_EMBD), dtype=jnp.float32)
        W_kqv = jax.random.normal(k2, (3 * N_EMBD, N_EMBD), dtype=jnp.float32) * (1.0 / math.sqrt(N_EMBD))
        return {'x': x, 'W_kqv': W_kqv}
    _L3_attn_in = _L3_attn_setup()

    def _L3_ffn_setup():
        import jax, jax.numpy as jnp
        import numpy as np
        N_EMBD = 128
        N_STATE = 512
        key = jax.random.key(seed)
        k_x, k_w1, k_b1, k_w2, k_b2 = jax.random.split(key, 5)
        x = jax.random.normal(k_x, (4, 256, N_EMBD), dtype=jnp.float32)
        w1 = jax.random.normal(k_w1, (N_EMBD, N_STATE), dtype=jnp.float32) * (1.0 / np.sqrt(N_EMBD))
        b1 = jax.random.normal(k_b1, (N_STATE,), dtype=jnp.float32) * 0.02
        w2 = jax.random.normal(k_w2, (N_STATE, N_EMBD), dtype=jnp.float32) * (1.0 / np.sqrt(N_STATE))
        b2 = jax.random.normal(k_b2, (N_EMBD,), dtype=jnp.float32) * 0.02
        return {'x': x, 'w1': w1, 'b1': b1, 'w2': w2, 'b2': b2}
    _L3_ffn_in = _L3_ffn_setup()
    _d = {'L0_attn_x': _L0_attn_in['x'], 'L0_attn_in_proj_w': _L0_attn_in['in_proj_w'], 'L0_attn_conv_w': _L0_attn_in['conv_w'], 'L0_attn_conv_b': _L0_attn_in['conv_b'], 'L0_attn_dt_w': _L0_attn_in['dt_w'], 'L0_attn_dt_b': _L0_attn_in['dt_b'], 'L0_attn_A_log': _L0_attn_in['A_log'], 'L0_attn_D': _L0_attn_in['D'], 'L0_attn_B_w': _L0_attn_in['B_w'], 'L0_attn_C_w': _L0_attn_in['C_w'], 'L0_attn_out_w': _L0_attn_in['out_w'], 'L0_ffn_ln1_w': _L0_ffn_in['ln1_w'], 'L0_ffn_c_attn_w': _L0_ffn_in['c_attn_w'], 'L0_ffn_c_proj_w': _L0_ffn_in['c_proj_w'], 'L0_ffn_ln2_w': _L0_ffn_in['ln2_w'], 'L0_ffn_router_w': _L0_ffn_in['router_w'], 'L0_ffn_w1': _L0_ffn_in['w1'], 'L0_ffn_w2': _L0_ffn_in['w2'], 'L1_attn_w_disp': _L1_attn_in['w_disp'], 'L1_attn_b_disp': _L1_attn_in['b_disp'], 'L1_attn_w_val': _L1_attn_in['w_val'], 'L1_attn_b_val': _L1_attn_in['b_val'], 'L1_attn_rel_pos_emb': _L1_attn_in['rel_pos_emb'], 'L1_attn_w_state': _L1_attn_in['w_state'], 'L1_attn_b_state': _L1_attn_in['b_state'], 'L1_attn_w_strain': _L1_attn_in['w_strain'], 'L1_attn_b_strain': _L1_attn_in['b_strain'], 'L1_attn_w_state_i': _L1_attn_in['w_state_i'], 'L1_attn_w_state_j': _L1_attn_in['w_state_j'], 'L1_attn_w_pos': _L1_attn_in['w_pos'], 'L1_attn_w_bond_out': _L1_attn_in['w_bond_out'], 'L1_attn_b_bond_out': _L1_attn_in['b_bond_out'], 'L1_attn_w_damage': _L1_attn_in['w_damage'], 'L1_attn_b_damage': _L1_attn_in['b_damage'], 'L1_attn_w_damage_out': _L1_attn_in['w_damage_out'], 'L1_attn_b_damage_out': _L1_attn_in['b_damage_out'], 'L1_attn_w_cproj': _L1_attn_in['w_cproj'], 'L1_attn_b_cproj': _L1_attn_in['b_cproj'], 'L1_ffn_router_W': _L1_ffn_in['router_W'], 'L1_ffn_router_b': _L1_ffn_in['router_b'], 'L1_ffn_ln_g': _L1_ffn_in['ln_g'], 'L1_ffn_ln_b': _L1_ffn_in['ln_b'], 'L1_ffn_W1': _L1_ffn_in['W1'], 'L1_ffn_b1': _L1_ffn_in['b1'], 'L1_ffn_W2': _L1_ffn_in['W2'], 'L1_ffn_b2': _L1_ffn_in['b2'], 'L2_attn_Wq': _L2_attn_in['Wq'], 'L2_attn_Wk': _L2_attn_in['Wk'], 'L2_attn_Wv': _L2_attn_in['Wv'], 'L2_attn_Wo': _L2_attn_in['Wo'], 'L2_attn_norm_const': _L2_attn_in['norm_const'], 'L2_ffn_wqkv': _L2_ffn_in['wqkv'], 'L2_ffn_q_scale': _L2_ffn_in['q_scale'], 'L2_ffn_k_scale': _L2_ffn_in['k_scale'], 'L2_ffn_wo': _L2_ffn_in['wo'], 'L2_ffn_ln_g': _L2_ffn_in['ln_g'], 'L2_ffn_ln_b': _L2_ffn_in['ln_b'], 'L2_ffn_w1': _L2_ffn_in['w1'], 'L2_ffn_b1': _L2_ffn_in['b1'], 'L2_ffn_w2': _L2_ffn_in['w2'], 'L2_ffn_b2': _L2_ffn_in['b2'], 'L3_attn_W_kqv': _L3_attn_in['W_kqv'], 'L3_ffn_w1': _L3_ffn_in['w1'], 'L3_ffn_b1': _L3_ffn_in['b1'], 'L3_ffn_w2': _L3_ffn_in['w2'], 'L3_ffn_b2': _L3_ffn_in['b2']}
    _x0 = _d['L0_attn_x']
    _d['L0_attn_x'] = jax.random.normal(jax.random.fold_in(jax.random.key(seed), 1), (32, 256, 128), dtype=_x0.dtype)
    del _x0
    return _d

def reference(L0_attn_x, L0_attn_in_proj_w, L0_attn_conv_w, L0_attn_conv_b, L0_attn_dt_w, L0_attn_dt_b, L0_attn_A_log, L0_attn_D, L0_attn_B_w, L0_attn_C_w, L0_attn_out_w, L0_ffn_ln1_w, L0_ffn_c_attn_w, L0_ffn_c_proj_w, L0_ffn_ln2_w, L0_ffn_router_w, L0_ffn_w1, L0_ffn_w2, L1_attn_w_disp, L1_attn_b_disp, L1_attn_w_val, L1_attn_b_val, L1_attn_rel_pos_emb, L1_attn_w_state, L1_attn_b_state, L1_attn_w_strain, L1_attn_b_strain, L1_attn_w_state_i, L1_attn_w_state_j, L1_attn_w_pos, L1_attn_w_bond_out, L1_attn_b_bond_out, L1_attn_w_damage, L1_attn_b_damage, L1_attn_w_damage_out, L1_attn_b_damage_out, L1_attn_w_cproj, L1_attn_b_cproj, L1_ffn_router_W, L1_ffn_router_b, L1_ffn_ln_g, L1_ffn_ln_b, L1_ffn_W1, L1_ffn_b1, L1_ffn_W2, L1_ffn_b2, L2_attn_Wq, L2_attn_Wk, L2_attn_Wv, L2_attn_Wo, L2_attn_norm_const, L2_ffn_wqkv, L2_ffn_q_scale, L2_ffn_k_scale, L2_ffn_wo, L2_ffn_ln_g, L2_ffn_ln_b, L2_ffn_w1, L2_ffn_b1, L2_ffn_w2, L2_ffn_b2, L3_attn_W_kqv, L3_ffn_w1, L3_ffn_b1, L3_ffn_w2, L3_ffn_b2):

    def _L0_attn_ref(x, in_proj_w, conv_w, conv_b, dt_w, dt_b, A_log, D, B_w, C_w, out_w):
        import jax, jax.numpy as jnp
        import numpy as np
        D_MODEL, D_STATE, D_CONV, EXPAND = (128, 16, 4, 2)
        D_INNER = EXPAND * D_MODEL
        BATCH, SEQ = (2, 256)

        def _forward(x, in_proj_w, conv_w, conv_b, dt_w, dt_b, A_log, D, B_w, C_w, out_w):
            xz = x @ in_proj_w.T
            xc, z = jnp.split(xz, 2, axis=-1)
            h = jnp.transpose(xc, (0, 2, 1))
            h = jnp.pad(h, ((0, 0), (0, 0), (D_CONV - 1, 0)))
            h = jax.lax.conv_general_dilated(h, conv_w, (1,), 'VALID', dimension_numbers=('NCH', 'OIH', 'NCH'))
            h = h + conv_b[None, :, None]
            u = jnp.transpose(h, (0, 2, 1))
            dt = jnp.clip(jax.nn.sigmoid(u @ dt_w.T + dt_b), 0.0001, 1.0)
            A = -jnp.exp(A_log)
            Bm = u @ B_w.T
            Cm = u @ C_w.T
            u_t = jnp.transpose(u, (1, 0, 2))
            dt_t = jnp.transpose(dt, (1, 0, 2))
            B_t = jnp.transpose(Bm, (1, 0, 2))
            C_t = jnp.transpose(Cm, (1, 0, 2))

            def step(state, inp):
                ut, dtt, bt, ct = inp
                dA = jnp.exp(jnp.clip(dtt[:, :, None] * A, -5.0, 5.0))
                dB = dtt[:, :, None] * bt[:, None, :] * ut[:, :, None]
                state = dA * state + dB + 1e-06
                y = jnp.sum(state * ct[:, None, :], axis=-1) + D * ut
                return (state, y)
            state0 = jnp.zeros((x.shape[0], D_INNER, D_STATE), x.dtype)
            _, ys = jax.lax.scan(step, state0, (u_t, dt_t, B_t, C_t))
            y = jnp.transpose(ys, (1, 0, 2))
            y = y * jax.nn.silu(z)
            return y @ out_w.T
        return _forward(x, in_proj_w, conv_w, conv_b, dt_w, dt_b, A_log, D, B_w, C_w, out_w)

    def _L0_ffn_ref(x, ln1_w, c_attn_w, c_proj_w, ln2_w, router_w, w1, w2):
        import jax, jax.numpy as jnp
        import numpy as np
        B, T, C, H, E, K, F = (2, 256, 128, 16, 8, 2, 256)
        EPS = 1e-05

        def layernorm(x, w):
            m = x.mean(-1, keepdims=True)
            v = x.var(-1, keepdims=True)
            return (x - m) * jax.lax.rsqrt(v + EPS) * w

        def attention(x, c_attn_w, c_proj_w):
            b, t, c = x.shape
            hd = c // H
            q, k, v = jnp.split(x @ c_attn_w, 3, axis=-1)
            q = q.reshape(b, t, H, hd).transpose(0, 2, 1, 3)
            k = k.reshape(b, t, H, hd).transpose(0, 2, 1, 3)
            v = v.reshape(b, t, H, hd).transpose(0, 2, 1, 3)
            att = jnp.einsum('bhqd,bhkd->bhqk', q, k) / jnp.sqrt(jnp.asarray(hd, x.dtype))
            causal = jnp.tril(jnp.ones((t, t), bool))
            att = jnp.where(causal, att, jnp.asarray(-jnp.inf, att.dtype))
            att = jax.nn.softmax(att, axis=-1)
            y = jnp.einsum('bhqk,bhkd->bhqd', att, v)
            y = y.transpose(0, 2, 1, 3).reshape(b, t, c)
            return y @ c_proj_w

        def moe_mlp(x, router_w, w1, w2):
            b, t, c = x.shape
            xf = x.reshape(-1, c)
            router_logits = xf @ router_w
            probs = jax.nn.softmax(router_logits.astype(jnp.float32), axis=-1)
            rw, sel = jax.lax.top_k(probs, K)
            rw = rw / rw.sum(axis=-1, keepdims=True)
            rw = rw.astype(x.dtype)
            w1e = w1.reshape(c, E, F).transpose(1, 0, 2)
            w2e = w2.reshape(E, F, c)
            h = jax.nn.gelu(jnp.einsum('nc,ecf->enf', xf, w1e), approximate=False)
            y_all = jnp.einsum('enf,efc->nec', h, w2e)
            y_sel = jnp.take_along_axis(y_all, sel[:, :, None], axis=1)
            y = (y_sel * rw[:, :, None]).sum(axis=1)
            return y.reshape(b, t, c)
        x = x + attention(layernorm(x, ln1_w), c_attn_w, c_proj_w)
        x = x + moe_mlp(layernorm(x, ln2_w), router_w, w1, w2)
        return x

    def _L1_attn_ref(x, w_disp, b_disp, w_val, b_val, rel_pos_emb, w_state, b_state, w_strain, b_strain, w_state_i, w_state_j, w_pos, w_bond_out, b_bond_out, w_damage, b_damage, w_damage_out, b_damage_out, w_cproj, b_cproj):
        import jax, jax.numpy as jnp
        import numpy as np
        B, T, C = (2, 256, 128)
        NH = 16
        HS = C // NH
        BD = max(HS // 4, 16)
        HORIZON = 32

        def _windows(t, delta):
            padded = jnp.pad(t, ((0, 0), (0, 0), (delta - 1, 0), (0, 0)))
            idx = jnp.arange(t.shape[2])[:, None] + jnp.arange(delta)[None, :]
            return padded[:, :, idx]
        Bx, Tx, Cx = x.shape
        delta = min(HORIZON, Tx)
        gelu = lambda v: jax.nn.gelu(v, approximate=False)
        disp = (x @ w_disp + b_disp).reshape(Bx, Tx, NH, BD).transpose(0, 2, 1, 3)
        val = (x @ w_val + b_val).reshape(Bx, Tx, NH, HS).transpose(0, 2, 1, 3)
        disp_win = _windows(disp, delta)
        val_win = _windows(val, delta)
        cmask = jnp.arange(Tx)[:, None] - delta + 1 + jnp.arange(delta)[None, :] >= 0
        cmask_f = cmask.astype(x.dtype)
        strain = disp_win - disp[:, :, :, None, :]
        strain_for_state = strain @ w_state + b_state
        valid_counts = jnp.clip(cmask_f.sum(axis=-1), 1.0)
        state = (strain_for_state * cmask_f[None, None, :, :, None]).sum(axis=3) / valid_counts[None, None, :, None]
        state_win = _windows(state, delta)
        rel_emb = rel_pos_emb[:delta]
        bond_act = gelu(strain @ w_strain + b_strain + state[:, :, :, None, :] @ w_state_i + state_win @ w_state_j + rel_emb @ w_pos)
        bond_logits = (bond_act @ w_bond_out)[..., 0] + b_bond_out[0]
        damage_act = gelu(strain @ w_damage + b_damage)
        damage = jax.nn.sigmoid((damage_act @ w_damage_out)[..., 0] + b_damage_out[0])
        logits = bond_logits - damage * 10.0
        logits = jnp.where(cmask[None, None], logits, -jnp.inf)
        weights = jax.nn.softmax(logits, axis=-1)
        out = jnp.einsum('bntd,bntde->bnte', weights, val_win)
        out = out.transpose(0, 2, 1, 3).reshape(Bx, Tx, Cx)
        return out @ w_cproj + b_cproj

    def _L1_ffn_ref(x, router_W, router_b, ln_g, ln_b, W1, b1, W2, b2):
        import jax, jax.numpy as jnp
        import numpy as np
        B, S, H, E, K = (2, 256, 128, 8, 2)
        FF = 4 * H
        EPS = 1e-05
        logits = x @ router_W + router_b
        w, idx = jax.lax.top_k(logits, K)
        w = jax.nn.softmax(w, axis=-1)
        gates = jnp.einsum('bske,bsk->bse', jax.nn.one_hot(idx, E, dtype=x.dtype), w)
        mu = jnp.mean(x, axis=-1, keepdims=True)
        var = jnp.mean(jnp.square(x - mu), axis=-1, keepdims=True)
        xhat = (x - mu) * jax.lax.rsqrt(var + EPS)
        h = xhat[:, :, None, :] * ln_g + ln_b
        a = jax.nn.gelu(jnp.einsum('bseh,ehf->bsef', h, W1) + b1, approximate=False)
        y = jnp.einsum('bsef,efh->bseh', a, W2) + b2
        y = y + x[:, :, None, :]
        out = jnp.einsum('bseh,bse->bsh', y, gates)
        return out

    def _L2_attn_ref(x, Wq, Wk, Wv, Wo, norm_const):
        import jax, jax.numpy as jnp
        import numpy as np
        NUM_HEADS = 16
        EPS = 1e-12

        def _l2norm(t):
            n = jnp.linalg.norm(t, axis=-1, keepdims=True)
            return t / jnp.maximum(n, EPS)
        N, C, d = x.shape
        H = NUM_HEADS
        hd = d // H

        def proj(W):
            return (x @ W.T).reshape(N, C, H, hd).transpose(0, 2, 1, 3)
        q = _l2norm(proj(Wq))
        k = _l2norm(proj(Wk))
        v = proj(Wv)
        v = v / jnp.power(jnp.float32(C), jax.nn.sigmoid(norm_const))
        kv = jnp.einsum('nhcd,nhce->nhde', k, v)
        attn = jnp.einsum('nhcd,nhde->nhce', q, kv)
        out = attn.transpose(0, 2, 1, 3).reshape(N, C, d)
        return out @ Wo.T

    def _L2_ffn_ref(x, wqkv, q_scale, k_scale, wo, ln_g, ln_b, w1, b1, w2, b2):
        import jax, jax.numpy as jnp
        import numpy as np
        DIM = 128
        DEPTH = 2
        HEADS = 8
        DIM_HEAD = 64
        WINDOW = 64
        INNER = HEADS * DIM_HEAD
        HID = int(DIM * 4 * 2 / 3)
        B, N = (2, 1024)
        QK_SCALE = 8.0

        def shift_token(t):
            t1, t2 = jnp.split(t, 2, axis=-1)
            t2 = jnp.pad(t2, ((0, 0), (1, 0), (0, 0)))[:, :-1]
            return jnp.concatenate([t1, t2], axis=-1)

        def l2norm(t):
            return t / jnp.clip(jnp.linalg.norm(t, axis=-1, keepdims=True), 1e-12)

        def rotate_half(x):
            x1, x2 = jnp.split(x, 2, axis=-1)
            return jnp.concatenate([-x2, x1], axis=-1)

        def rotary_xpos(q, k):
            n = q.shape[-2]
            half_idx = jnp.arange(0, DIM_HEAD, 2, dtype=jnp.float32)
            inv_freq = 1.0 / 10000.0 ** (half_idx / DIM_HEAD)
            t = jnp.arange(n, dtype=jnp.float32)
            freqs = t[:, None] * inv_freq[None, :]
            freqs = jnp.concatenate([freqs, freqs], axis=-1)
            base = (half_idx + 0.4 * DIM_HEAD) / (1.4 * DIM_HEAD)
            power = (t - n // 2) / float(WINDOW // 2)
            scale = base[None, :] ** power[:, None]
            scale = jnp.concatenate([scale, scale], axis=-1)
            cos, sin = (jnp.cos(freqs), jnp.sin(freqs))
            q = q * cos * scale + rotate_half(q) * sin * scale
            k = k * cos / scale + rotate_half(k) * sin / scale
            return (q, k)

        def local_attention(q, k, v):
            b, h, n, d = q.shape
            w = n // WINDOW
            bq = q.reshape(b, h, w, WINDOW, d) * QK_SCALE
            bk = k.reshape(b, h, w, WINDOW, d)
            bv = v.reshape(b, h, w, WINDOW, d)

            def look_around(t):
                p = jnp.pad(t, ((0, 0), (0, 0), (1, 0), (0, 0), (0, 0)))
                return jnp.concatenate([p[:, :, :w], p[:, :, 1:]], axis=3)
            bk, bv = (look_around(bk), look_around(bv))
            bt = jnp.arange(n).reshape(w, WINDOW)
            btp = jnp.pad(bt, ((1, 0), (0, 0)), constant_values=-1)
            btk = jnp.concatenate([btp[:w], btp[1:]], axis=1)
            sim = jnp.einsum('bhwid,bhwjd->bhwij', bq, bk)
            i = bt[:, :, None]
            j = btk[:, None, :]
            mask = (i < j) | (i > j + WINDOW) | (j == -1)
            sim = jnp.where(mask, -jnp.finfo(sim.dtype).max, sim)
            attn = jax.nn.softmax(sim, axis=-1)
            out = jnp.einsum('bhwij,bhwjd->bhwid', attn, bv)
            return out.reshape(b, h, n, d)

        def _layer(x, wqkv, qs, ksc, wo, lg, lb, w1, b1, w2, b2):
            b, n, _ = x.shape
            h = shift_token(x)
            qkv = h @ wqkv
            q, k, v = jnp.split(qkv, 3, axis=-1)
            to_heads = lambda t: t.reshape(b, n, HEADS, DIM_HEAD).transpose(0, 2, 1, 3)
            q, k, v = (to_heads(q), to_heads(k), to_heads(v))
            q = l2norm(q) * qs
            k = l2norm(k) * ksc
            q, k = rotary_xpos(q, k)
            o = local_attention(q, k, v)
            o = o.transpose(0, 2, 1, 3).reshape(b, n, INNER)
            x = x + o @ wo
            h = shift_token(x)
            mu = h.mean(-1, keepdims=True)
            var = h.var(-1, keepdims=True)
            h = (h - mu) / jnp.sqrt(var + 1e-05) * lg + lb
            h = h @ w1 + b1
            a, g = jnp.split(h, 2, axis=-1)
            h = a * jax.nn.gelu(g, approximate=False)
            x = x + h @ w2 + b2
            return x
        for l in range(DEPTH):
            x = _layer(x, wqkv[l], q_scale[l], k_scale[l], wo[l], ln_g[l], ln_b[l], w1[l], b1[l], w2[l], b2[l])
        return x

    def _L3_attn_ref(x, W_kqv):
        import jax, jax.numpy as jnp
        import numpy as np
        import math
        N_EMBD = 128
        NUM_HEADS = 16
        HEAD_DIM = N_EMBD // NUM_HEADS

        def alibi_slopes(num_heads):
            x = (2 ** 8) ** (1.0 / num_heads)
            return jnp.array([1.0 / x ** (i + 1) for i in range(num_heads)], dtype=jnp.float32)
        B, S, E = x.shape
        H, D = (NUM_HEADS, HEAD_DIM)
        kqv = jnp.einsum('bse,fe->bsf', x, W_kqv)
        k, q, v = jnp.split(kqv, 3, axis=-1)
        q = q.reshape(B, S, H, D).transpose(0, 2, 1, 3)
        k = k.reshape(B, S, H, D).transpose(0, 2, 1, 3)
        v = v.reshape(B, S, H, D).transpose(0, 2, 1, 3)
        rel = jnp.arange(S)[None, :] - jnp.arange(S)[:, None]
        bias = alibi_slopes(H)[:, None, None] * rel.astype(jnp.float32)
        scale = math.sqrt(E)
        score = jnp.einsum('bhqd,bhkd->bhqk', q, k) / scale + bias[None]
        causal = jnp.tril(jnp.ones((S, S), dtype=bool))
        score = jnp.where(causal[None, None], score, -jnp.inf)
        attn = jax.nn.softmax(score, axis=-1)
        out = jnp.einsum('bhqk,bhkd->bhqd', attn, v)
        return out.transpose(0, 2, 1, 3).reshape(B, S, E)

    def _L3_ffn_ref(x, w1, b1, w2, b2):
        import jax, jax.numpy as jnp
        import numpy as np
        N_EMBD = 128
        N_STATE = 512
        h = jax.nn.gelu(jnp.einsum('bse,eh->bsh', x, w1) + b1, approximate=False)
        return jnp.einsum('bsh,he->bse', h, w2) + b2
    x = L0_attn_x
    x = x + _layernorm(_L0_attn_ref(_layernorm(x, axis=-1), L0_attn_in_proj_w, L0_attn_conv_w, L0_attn_conv_b, L0_attn_dt_w, L0_attn_dt_b, L0_attn_A_log, L0_attn_D, L0_attn_B_w, L0_attn_C_w, L0_attn_out_w), axis=-1)
    x = x + _layernorm(_L0_ffn_ref(_layernorm(x, axis=-1), L0_ffn_ln1_w, L0_ffn_c_attn_w, L0_ffn_c_proj_w, L0_ffn_ln2_w, L0_ffn_router_w, L0_ffn_w1, L0_ffn_w2), axis=-1)
    x = x + _layernorm(_L1_attn_ref(_layernorm(x, axis=-1), L1_attn_w_disp, L1_attn_b_disp, L1_attn_w_val, L1_attn_b_val, L1_attn_rel_pos_emb, L1_attn_w_state, L1_attn_b_state, L1_attn_w_strain, L1_attn_b_strain, L1_attn_w_state_i, L1_attn_w_state_j, L1_attn_w_pos, L1_attn_w_bond_out, L1_attn_b_bond_out, L1_attn_w_damage, L1_attn_b_damage, L1_attn_w_damage_out, L1_attn_b_damage_out, L1_attn_w_cproj, L1_attn_b_cproj), axis=-1)
    x = x + _layernorm(_L1_ffn_ref(_layernorm(x, axis=-1), L1_ffn_router_W, L1_ffn_router_b, L1_ffn_ln_g, L1_ffn_ln_b, L1_ffn_W1, L1_ffn_b1, L1_ffn_W2, L1_ffn_b2), axis=-1)
    x = x + _layernorm(_L2_attn_ref(_layernorm(x, axis=-1), L2_attn_Wq, L2_attn_Wk, L2_attn_Wv, L2_attn_Wo, L2_attn_norm_const), axis=-1)
    x = x + _layernorm(_L2_ffn_ref(_layernorm(x, axis=-1), L2_ffn_wqkv, L2_ffn_q_scale, L2_ffn_k_scale, L2_ffn_wo, L2_ffn_ln_g, L2_ffn_ln_b, L2_ffn_w1, L2_ffn_b1, L2_ffn_w2, L2_ffn_b2), axis=-1)
    x = x + _layernorm(_L3_attn_ref(_layernorm(x, axis=-1), L3_attn_W_kqv), axis=-1)
    x = x + _layernorm(_L3_ffn_ref(_layernorm(x, axis=-1), L3_ffn_w1, L3_ffn_b1, L3_ffn_w2, L3_ffn_b2), axis=-1)
    return x

_drawn_inputs = setup_inputs


def setup_inputs(seed=0):
    import zlib

    import numpy as np

    out = dict(_drawn_inputs(seed))
    spreads = {'L0_attn_D': (1.0, 0.2),
     'L0_ffn_ln1_w': (1.0, 0.6),
     'L0_ffn_ln2_w': (1.0, 0.6),
     'L1_attn_b_disp': (0.0, 2.0),
     'L1_attn_b_val': (0.0, 0.1),
     'L1_attn_b_state': (0.0, 2.0),
     'L1_attn_b_strain': (0.0, 2.0),
     'L1_attn_b_damage': (0.0, 2.0),
     'L1_attn_b_cproj': (0.0, 0.1),
     'L1_ffn_router_b': (0.0, 0.1),
     'L1_ffn_ln_g': (1.0, 0.553),
     'L1_ffn_ln_b': (0.0, 0.578),
     'L1_ffn_b1': (0.0, 0.557),
     'L1_ffn_b2': (0.0, 0.352),
     'L2_attn_norm_const': (0.5, 0.6),
     'L2_ffn_q_scale': (1.0, 0.6),
     'L2_ffn_k_scale': (1.0, 0.6),
     'L2_ffn_ln_g': (1.0, 0.6),
     'L2_ffn_ln_b': (0.0, 0.8),
     'L2_ffn_b1': (0.0, 0.8),
     'L2_ffn_b2': (0.0, 0.8)}
    factors = {'L0_attn_dt_w': 6.563,
     'L0_attn_dt_b': 8.0,
     'L0_attn_A_log': 37.013,
     'L0_ffn_c_attn_w': 8.0,
     'L0_ffn_c_proj_w': 8.0,
     'L0_ffn_router_w': 4.883,
     'L0_ffn_w1': 4.21,
     'L0_ffn_w2': 4.075,
     'L1_attn_w_disp': 8.0,
     'L1_attn_rel_pos_emb': 64.0,
     'L1_attn_w_state': 22.844,
     'L1_attn_w_strain': 8.0,
     'L1_attn_w_state_i': 30.513,
     'L1_attn_w_state_j': 8.0,
     'L1_attn_w_pos': 64.0,
     'L1_attn_w_bond_out': 8.0,
     'L1_attn_w_damage': 31.644,
     'L1_attn_w_damage_out': 8.0,
     'L2_ffn_wqkv': 4.336,
     'L2_ffn_wo': 4.483,
     'L2_ffn_w1': 8.0,
     'L2_ffn_w2': 8.0,
     'L3_ffn_b1': 8.0,
     'L3_ffn_b2': 8.0}
    for name, (base, spread) in spreads.items():
        noise = np.random.default_rng([zlib.crc32(name.encode()), seed]).standard_normal(out[name].shape)
        drawn = base * np.exp(spread * noise) if base else spread * noise
        out[name] = jnp.asarray(drawn.astype(out[name].dtype))
    for name, factor in factors.items():
        out[name] = (out[name] * factor).astype(out[name].dtype)
    return out
```

```python
from contextlib import ExitStack

import concourse.bass as bass
from concourse import mybir

F32 = mybir.dt.float32
BF16 = mybir.dt.bfloat16
ALU = mybir.AluOpType
ACT = mybir.ActivationFunctionType
AX = mybir.AxisListType

P = 128
SEQ = 256
TILES = SEQ // P
EPS = 1e-5


class Chain:

    def __init__(self, eng, sem):
        self.eng, self.sem, self.n = eng, sem, 0

    def link(self, ins):
        self.n += 1
        ins.then_inc(self.sem, 1)
        self.eng.wait_ge(self.sem, self.n)

    def restart(self):
        if self.n:
            self.eng.sem_clear(self.sem)
        self.n = 0


class Stage:

    def __init__(self, nc, ctx, name, lanes, core, tiles=2, src=None):
        self.nc, self.ctx, self.name, self.lanes, self.core = nc, ctx, name, lanes, core
        self.tiles = tiles
        self.sems = []
        self.turns = core.n_seq * TILES // (lanes * tiles)
        self.src = core.X if src is None else src
        self.mv_ready = self.sem("mv_ready")
        self.rstd_ready = self.sem("rstd_ready")
        self.xn_ready = self.sem("xn_ready")
        self.xt_in_psum = self.sem("xt_in_psum")
        self.xT_ready = self.sem("xT_ready")
        self.back_mv_ready = self.sem("back_mv_ready")
        self.back_rstd_ready = self.sem("back_rstd_ready")
        self.v_chain = self.sem("v_chain")
        self.a_chain = self.sem("a_chain")
        self.p_chain = self.sem("p_chain")
        self.stats = self.sb("stats", [P, lanes, tiles, 6])
        self.mv = self.sb("mv", [P, lanes, tiles, 2])
        self.rstd = self.sb("rstd", [P, lanes, tiles])
        self.back_stats = self.sb("back_stats", [P, lanes, tiles, 6])
        self.back_mv = self.sb("back_mv", [P, lanes, tiles, 2])
        self.back_rstd = self.sb("back_rstd", [P, lanes, tiles])
        self.xn = [self.sb(f"xn{k}", [P, tiles, P]) for k in range(lanes)]
        self.xT = [self.sb(f"xT{k}", [P, tiles * P]) for k in range(lanes)]
        self.r = [self.sb(f"r{k}", [P, tiles, P]) for k in range(lanes)]

    def sem(self, name):
        self.sems.append(self.ctx.enter_context(self.nc.semaphore(f"{self.name}_{name}")))
        return self.sems[-1]

    def clear_semaphores(self):
        with self.nc.Block() as block:
            @block.vector
            def _(eng):
                for sem in self.sems[0::3]:
                    eng.sem_clear(sem)

            @block.scalar
            def _(eng):
                for sem in self.sems[1::3]:
                    eng.sem_clear(sem)

            @block.gpsimd
            def _(eng):
                for sem in self.sems[2::3]:
                    eng.sem_clear(sem)

    def sb(self, name, shape, dt=F32):
        return self.ctx.enter_context(self.nc.sbuf_tensor(f"{self.name}_{name}", shape, dt))

    def ps(self, name, shape, dt=F32):
        return self.ctx.enter_context(self.nc.psum_tensor(f"{self.name}_{name}", shape, dt))

    def nth(self, i, lane, per=1, k=0):
        return i * (self.lanes * per) + (lane * per + k + 1)

    def rows(self, i, lane, tile):
        return self.of(self.src, i, lane, tile)

    def of(self, rows, i, lane, tile):
        return rows[:, i * (self.lanes * self.tiles) + (lane * self.tiles + tile), :]

    def front_stats(self, eng, chain, i, lane):
        for t in range(self.tiles):
            ins = eng.bn_stats(self.stats[:, lane, t, :], self.rows(i, lane, t))
        chain.link(ins)
        for t in range(self.tiles):
            ins = eng.bn_aggr(self.mv[:, lane, t, :], self.stats[:, lane, t, :])
        ins.then_inc(self.mv_ready, 1)

    def front_apply(self, eng, i, lane):
        eng.wait_ge(self.rstd_ready, self.nth(i, lane))
        for t in range(self.tiles):
            ins = eng.tensor_scalar(self.xn[lane][:, t, :], self.rows(i, lane, t), self.mv[:, lane, t, 0:1],
                                    self.rstd[:, lane, t:t + 1], ALU.subtract, ALU.mult)
        ins.then_inc(self.xn_ready, 1)

    def back_norm_stats(self, eng, chain, lane, src):
        for t in range(self.tiles):
            ins = eng.bn_stats(self.back_stats[:, lane, t, :], src[:, t, :])
        chain.link(ins)
        for t in range(self.tiles):
            ins = eng.bn_aggr(self.back_mv[:, lane, t, :], self.back_stats[:, lane, t, :])
        ins.then_inc(self.back_mv_ready, 1)

    def back_residual(self, eng, chain, i, lane, src):
        eng.wait_ge(self.back_rstd_ready, self.nth(i, lane))
        for t in range(self.tiles):
            ins = eng.tensor_scalar(self.r[lane][:, t, :], src[:, t, :],
                                    self.back_mv[:, lane, t, 0:1], self.back_rstd[:, lane, t:t + 1],
                                    ALU.subtract, ALU.mult)
        chain.link(ins)
        for t in range(self.tiles):
            x = self.of(self.core.X, i, lane, t)
            ins = eng.tensor_tensor(x, x, self.r[lane][:, t, :], ALU.add)
        chain.link(ins)

    def power(self, eng, chain, out, var, eps):
        n = out.shape[1]
        chain.link(eng.tensor_tensor(out, var, eps[:, 0:n], ALU.add))
        return eng.tensor_tensor(out, out, self.core.minus_half[:, 0:n], ALU.pow)

    def front_rstd(self, eng, chain, i, lane):
        eng.wait_ge(self.mv_ready, self.nth(i, lane))
        self.power(eng, chain, self.rstd[:, lane, :], self.mv[:, lane, :, 1], self.core.eps).then_inc(self.rstd_ready, 1)

    def back_rstd_step(self, eng, chain, i, lane):
        eng.wait_ge(self.back_mv_ready, self.nth(i, lane))
        self.power(eng, chain, self.back_rstd[:, lane, :], self.back_mv[:, lane, :, 1], self.core.eps)\
            .then_inc(self.back_rstd_ready, 1)

    def transpose_rows(self, eng, i, lane, out, src, ready, done):
        eng.wait_ge(ready, self.nth(i, lane))
        for t in range(self.tiles):
            ins = eng.transpose(out[:, t * P:(t + 1) * P], src[:, t, :], self.core.ident[:, :])
        ins.then_inc(done, 1)

    def front_transpose(self, eng, i, lane, out):
        self.transpose_rows(eng, i, lane, out, self.xn[lane], self.xn_ready, self.xt_in_psum)

    def front_copy(self, eng, i, lane, src):
        eng.wait_ge(self.xt_in_psum, self.nth(i, lane))
        eng.copy(self.xT[lane][:, :], src).then_inc(self.xT_ready, 1)


class Core:

    def __init__(self, nc, ctx, n_seq):
        self.n_seq = n_seq
        self.X = ctx.enter_context(nc.sbuf_tensor("rows", [P, n_seq * TILES, P], F32))
        self.ident = ctx.enter_context(nc.sbuf_tensor("ident", [P, P], F32))
        self.eps = ctx.enter_context(nc.sbuf_tensor("eps", [P, 8], F32))
        self.e = ctx.enter_context(nc.sbuf_tensor("e", [P, 64], F32))
        self.minus_half = ctx.enter_context(nc.sbuf_tensor("minus_half", [P, 64], F32))


def inner_rows(nc, ctx, core, name):
    core.Y = ctx.enter_context(nc.sbuf_tensor(name, [P, core.n_seq * TILES, P], F32))


def load_stage(nc, core, x):
    with ExitStack() as ctx:
        x_loaded = ctx.enter_context(nc.semaphore("x_loaded"))
        zeroed = ctx.enter_context(nc.semaphore("zeroed"))
        with nc.Block() as block:
            @block.sync
            def _(eng):
                eng.dma_start(core.X[:, :, :], x.rearrange("(n p) c -> p n c", p=P)).then_inc(x_loaded, 16)
                eng.wait_ge(x_loaded, 16)

            @block.gpsimd
            def _(eng):
                eng.memset(core.minus_half[:, :], -0.5).then_inc(zeroed, 1)
                eng.memset(core.eps[:, :], EPS).then_inc(zeroed, 1)
                eng.memset(core.e[:, :], 2.718281828459045).then_inc(zeroed, 1)
                eng.memset(core.ident[:, :], 0.0).then_inc(zeroed, 1)
                eng.wait_ge(zeroed, 4)
                eng.affine_select(out=core.ident[:, :], in_=core.ident[:, :], compare_op=ALU.not_equal, fill=1.0,
                                  base=0, pattern=[[-1, P]], channel_multiplier=1).then_inc(zeroed, 1)
                eng.wait_ge(zeroed, 5)

        with nc.Block() as block:
            @block.gpsimd
            def _(eng):
                eng.sem_clear(x_loaded)
                eng.sem_clear(zeroed)


def store_stage(nc, core, out):
    with ExitStack() as ctx:
        stored = ctx.enter_context(nc.semaphore("stored"))
        with nc.Block() as block:
            @block.sync
            def _(eng):
                eng.dma_start(out.rearrange("(n p) c -> p n c", p=P), core.X[:, :, :]).then_inc(stored, 16)
                eng.wait_ge(stored, 16)


def mamba_stage(nc, core, W):
    D_IN, STATES, TAPS = 256, 16, 4
    HALVES = D_IN // P
    GROUP = 4
    U = HALVES * STATES // GROUP
    LANES = 2
    with ExitStack() as ctx:
        S = Stage(nc, ctx, "l0a", LANES, core)
        w_in = S.sb("w_in", [P, 2 * D_IN])
        w_conv = S.sb("w_conv", [P, HALVES, TAPS, D_IN])
        w_dt = S.sb("w_dt", [P, HALVES, D_IN])
        w_bc = S.sb("w_bc", [P, HALVES, P])
        w_out = S.sb("w_out", [P, HALVES, P])
        pick = S.sb("pick", [P, 2 * STATES, P], BF16)
        conv_b = S.sb("conv_b", [P, HALVES])
        dt_b = S.sb("dt_b", [P, HALVES])
        skip = S.sb("skip", [P, HALVES])
        a_neg = S.sb("a_neg", [P, HALVES, STATES])
        tiny = S.sb("tiny", [P, 1])
        xc = [S.sb(f"xc{n}", [P, HALVES, TAPS - 1 + SEQ]) for n in range(LANES)]
        z_tanh = [S.sb(f"z_tanh{n}", [P, HALVES, SEQ]) for n in range(LANES)]
        z_gate = [S.sb(f"z_gate{n}", [P, HALVES, SEQ]) for n in range(LANES)]
        u_in = [S.sb(f"u{n}", [P, HALVES, SEQ]) for n in range(LANES)]
        dt = [S.sb(f"dt{n}", [P, HALVES, SEQ]) for n in range(LANES)]
        dtu = [S.sb(f"dtu{n}", [P, HALVES, SEQ]) for n in range(LANES)]
        bc = [S.sb(f"bc{n}", [P, SEQ], BF16) for n in range(LANES)]
        bc_rest = S.sb("bc_rest", [P, SEQ])
        y = [S.sb(f"y{n}", [P, HALVES, SEQ]) for n in range(LANES)]
        dta = [S.sb(f"dta{k}", [P, GROUP, SEQ]) for k in range(2)]
        decay = [S.sb(f"decay{k}", [P, GROUP, SEQ]) for k in range(2)]
        drive = [S.sb(f"drive{k}", [P, GROUP, SEQ]) for k in range(2)]
        state = [S.sb(f"state{k}", [P, GROUP, SEQ]) for k in range(2)]
        prod = [S.sb(f"prod{k}", [P, GROUP, SEQ]) for k in range(2)]
        pB = S.ps("pB", [P, GROUP, SEQ])
        pC = S.ps("pC", [P, GROUP, SEQ])
        pY = S.ps("pY", [P, HALVES, SEQ])
        p1 = S.ps("p1", [P, HALVES, SEQ])
        p2 = S.ps("p2", [P, HALVES, SEQ])
        pO = S.ps("pO", [P, 2, SEQ])
        out_rows = pO[:, 1, :].rearrange("p (t c) -> p t c", t=TILES)
        (weights_in, a_ready, const_ready, xc_in_psum, xc_ready, z_in_psum, z_tanh_ready, z_gate_ready,
         u_in_psum, u_ready, dt_in_psum, dt_tanh_ready, bc_in_psum, lane_ready, dta_ready, decay_ready,
         b_in_psum, drive_ready, drive_done, c_in_psum, prod_ready, y_in_psum, y_ready, out_in_psum) = (
             S.sem(s) for s in (
                 "weights_in", "a_ready", "const_ready", "xc_in_psum", "xc_ready", "z_in_psum", "z_tanh_ready",
                 "z_gate_ready", "u_in_psum", "u_ready", "dt_in_psum", "dt_tanh_ready", "bc_in_psum", "lane_ready",
                 "dta_ready", "decay_ready", "b_in_psum", "drive_ready", "drive_done", "c_in_psum", "prod_ready",
                 "y_in_psum", "y_ready", "out_in_psum"))
        N_LOADS = 10

        def unit(w):
            return w // U % LANES, w % U // (U // HALVES), w % (U // HALVES) * GROUP

        def at(i, w):
            return i * (LANES * U) + (w + 1)

        def turns(eng, turn):
            with eng.Fori(0, S.turns - 1) as i:
                turn(i, False)
            turn(S.turns - 1, True)

        with nc.Block() as block:
            @block.sync
            def _(eng):
                for dst, name in ((w_in, "in_proj"), (w_conv, "conv_w"), (w_dt, "dt_w"), (w_bc, "bc_w"), (w_out, "out_w"),
                                  (pick, "pick"), (conv_b, "conv_b"), (dt_b, "dt_b"), (skip, "D"), (a_neg, "A_log")):
                    src = W["bc_pick" if name == "pick" else f"L0_attn_{name}"]
                    eng.dma_start(dst[:], src).then_inc(weights_in, 16)
                eng.wait_ge(weights_in, 16 * N_LOADS)

            @block.vector
            def _(eng):
                chain = Chain(eng, S.v_chain)
                for n in range(LANES):
                    eng.memset(xc[n][:, :, 0:TAPS - 1], 0.0)
                for k in range(2):
                    eng.memset(dta[k][:, :, 0:1], -1e30)
                eng.memset(tiny[:, :], 1e-6)
                eng.wait_ge(a_ready, 1)
                eng.tensor_scalar(dt_b[:, :], dt_b[:, :], 0.5, None, ALU.mult)
                eng.tensor_scalar(a_neg[:, :, :], a_neg[:, :, :], -1.0, None, ALU.mult).then_inc(const_ready, 1)
                eng.wait_ge(const_ready, 1)

                def prepare(i, n, step):
                    if step == 0:
                        S.front_stats(eng, chain, i, n)
                    elif step == 1:
                        S.front_apply(eng, i, n)
                    elif step == 4:
                        eng.wait_ge(z_tanh_ready, S.nth(i, n))
                        eng.scalar_tensor_tensor(out=z_gate[n][:, :, :], in0=z_tanh[n][:, :, :], scalar=1.0,
                                                 in1=p2[:, :, :], op0=ALU.add, op1=ALU.mult).then_inc(z_gate_ready, 1)
                    elif step == 6:
                        eng.wait_ge(dt_tanh_ready, S.nth(i, n))
                        chain.link(eng.tensor_scalar(dt[n][:, :, :], dt[n][:, :, :], 0.5, 0.5, ALU.mult, ALU.add))
                        chain.link(eng.tensor_scalar(dt[n][:, :, :], dt[n][:, :, :], 1e-4, 1.0, ALU.max, ALU.min))
                        eng.tensor_tensor(dtu[n][:, :, :], dt[n][:, :, :], u_in[n][:, :, :], ALU.mult)
                        eng.wait_ge(bc_in_psum, S.nth(i, n))
                        chain.link(eng.tensor_copy(bc[n][:, :], pO[:, 0, :]))
                        chain.link(eng.tensor_tensor(bc_rest[64:128, :], pO[64:128, 0, :], bc[n][64:128, :], ALU.subtract))
                        chain.link(eng.tensor_copy(bc[n][64:128, :], bc_rest[64:128, :]))
                        chain.link(eng.tensor_tensor(bc_rest[96:128, :], bc_rest[96:128, :], bc[n][96:128, :], ALU.subtract))
                        chain.link(eng.tensor_copy(bc[n][96:128, :], bc_rest[96:128, :]))
                        eng.sem_inc(lane_ready, 1)

                def start_unit(i, w):
                    n, half, first = unit(w)
                    k = w % 2
                    for g in range(GROUP):
                        ins = eng.tensor_scalar(dta[k][:, g, 1:SEQ], dt[n][:, half, 1:SEQ],
                                                a_neg[:, half, first + g:first + g + 1], -5.0, ALU.mult, ALU.max)
                    ins.then_inc(dta_ready, 1)
                    eng.wait_ge(b_in_psum, at(i, w))
                    eng.tensor_tensor(drive[k][:, :, :], pB[:, :, :],
                                      dtu[n][:, half, :].unsqueeze(1).to_broadcast([P, GROUP, SEQ]), ALU.mult)\
                       .then_inc(drive_ready, 1)

                def finish_lane(i, n):
                    eng.wait_ge(y_in_psum, S.nth(i, n))
                    for h in range(HALVES):
                        ins = eng.scalar_tensor_tensor(out=y[n][:, h, :], in0=u_in[n][:, h, :], scalar=skip[:, h:h + 1],
                                                       in1=pY[:, h, :], op0=ALU.mult, op1=ALU.add)
                    chain.link(ins)
                    eng.scalar_tensor_tensor(out=y[n][:, :, :], in0=y[n][:, :, :], scalar=0.5, in1=z_gate[n][:, :, :],
                                             op0=ALU.mult, op1=ALU.mult).then_inc(y_ready, 1)

                def back_stats(i, n):
                    eng.wait_ge(out_in_psum, S.nth(i, n))
                    S.back_norm_stats(eng, chain, n, out_rows)

                def turn(i, last):
                    for w in range(LANES * U):
                        n, half, first = unit(w)
                        k = w % 2
                        if w + 1 < LANES * U:
                            start_unit(i, w + 1)
                        elif not last:
                            start_unit(i + 1, 0)
                        eng.wait_ge(decay_ready, at(i, w))
                        eng.wait_ge(drive_done, at(i, w))
                        chain.link(eng.tensor_tensor_scan(
                            out=state[k][:, :, :].rearrange("p g s -> p (g s)"),
                            data0=decay[k][:, :, :].rearrange("p g s -> p (g s)"),
                            data1=drive[k][:, :, :].rearrange("p g s -> p (g s)"), initial=0.0, op0=ALU.mult, op1=ALU.add))
                        eng.wait_ge(c_in_psum, at(i, w))
                        eng.tensor_tensor(prod[k][:, :, :], state[k][:, :, :], pC[:, :, :], ALU.mult).then_inc(prod_ready, 1)
                        if w < U:
                            prepare(i, 1, w)
                        elif not last:
                            prepare(i + 1, 0, w - U)
                        if w % U == U - 1:
                            finish_lane(i, n)
                        if w == U + 1:
                            back_stats(i, 0)
                        if w == U + 2:
                            S.back_residual(eng, chain, i, 0, out_rows)
                    back_stats(i, 1)
                    S.back_residual(eng, chain, i, 1, out_rows)
                    chain.restart()

                for step in range(U):
                    prepare(0, 0, step)
                start_unit(0, 0)
                chain.restart()
                turns(eng, turn)

            @block.gpsimd
            def _(eng):
                chain = Chain(eng, S.p_chain)

                def turn(i, last):
                    S.front_rstd(eng, chain, i, 1)
                    if not last:
                        S.front_rstd(eng, chain, i + 1, 0)
                    S.back_rstd_step(eng, chain, i, 0)
                    S.back_rstd_step(eng, chain, i, 1)
                    chain.restart()

                S.front_rstd(eng, chain, 0, 0)
                chain.restart()
                turns(eng, turn)

            @block.tensor
            def _(eng):
                eng.wait_ge(weights_in, 16 * N_LOADS)

                def prepare(i, n, step):
                    if step == 1:
                        S.front_transpose(eng, i, n, p1[:, 0, :])
                    elif step == 2:
                        eng.wait_ge(S.xT_ready, S.nth(i, n))
                        for h in range(HALVES):
                            ins = eng.matmul(p1[:, h, :], w_in[:, h * P:(h + 1) * P], S.xT[n][:, :], start=True, stop=True)
                        ins.then_inc(xc_in_psum, 1)
                        for h in range(HALVES):
                            ins = eng.matmul(p2[:, h, :], w_in[:, D_IN + h * P:D_IN + (h + 1) * P], S.xT[n][:, :],
                                             start=True, stop=True)
                        ins.then_inc(z_in_psum, 1)
                    elif step in (3, 4):
                        if step == 3:
                            eng.wait_ge(xc_ready, S.nth(i, n))
                        h = step - 3
                        for j in range(HALVES * TAPS):
                            c, tap = j // TAPS, j % TAPS
                            ins = eng.matmul(p1[:, h, :], w_conv[:, c, tap, h * P:(h + 1) * P], xc[n][:, c, tap:tap + SEQ],
                                             start=(j == 0), stop=(j == HALVES * TAPS - 1))
                        if h == 1:
                            ins.then_inc(u_in_psum, 1)
                    elif step == 5:
                        eng.wait_ge(u_ready, S.nth(i, n))
                        eng.wait_ge(z_gate_ready, S.nth(i, n))
                        for h in range(HALVES):
                            for c in range(HALVES):
                                ins = eng.matmul(p2[:, h, :], w_dt[:, c, h * P:(h + 1) * P], u_in[n][:, c, :],
                                                 start=(c == 0), stop=(c == HALVES - 1))
                        ins.then_inc(dt_in_psum, 1)
                        for c in range(HALVES):
                            ins = eng.matmul(pO[:, 0, :], w_bc[:, c, :], u_in[n][:, c, :], start=(c == 0), stop=(c == HALVES - 1))
                        ins.then_inc(bc_in_psum, 1)

                def spread_b(i, w):
                    n, half, first = unit(w)
                    if w % U == 0:
                        eng.wait_ge(lane_ready, S.nth(i, n))
                    for g in range(GROUP):
                        ins = eng.matmul(pB[:, g, :], pick[:, first + g, :], bc[n][:, :], start=True, stop=True)
                    ins.then_inc(b_in_psum, 1)

                def spread_c(i, w):
                    n, half, first = unit(w)
                    for g in range(GROUP):
                        ins = eng.matmul(pC[:, g, :], pick[:, STATES + first + g, :], bc[n][:, :], start=True, stop=True)
                    ins.then_inc(c_in_psum, 1)

                def sum_states(i, w):
                    n, half, first = unit(w)
                    eng.wait_ge(prod_ready, at(i, w))
                    for g in range(GROUP):
                        s = first + g
                        ins = eng.matmul(pY[:, half, :], core.ident[:, :], prod[w % 2][:, g, :], start=(s == 0),
                                         stop=(s == STATES - 1))
                    if w % U == U - 1:
                        ins.then_inc(y_in_psum, 1)

                def project_out(i, n):
                    eng.wait_ge(y_ready, S.nth(i, n))
                    for t in range(TILES):
                        for h in range(HALVES):
                            ins = eng.matmul(out_rows[:, t, :], y[n][:, h, t * P:(t + 1) * P], w_out[:, h, :],
                                             start=(h == 0), stop=(h == HALVES - 1))
                    ins.then_inc(out_in_psum, 1)

                def turn(i, last):
                    for w in range(LANES * U):
                        if w:
                            eng.wait_ge(prod_ready, at(i, w - 1))
                        spread_c(i, w)
                        if w + 1 < LANES * U:
                            eng.wait_ge(drive_ready, at(i, w))
                            spread_b(i, w + 1)
                        elif not last:
                            eng.wait_ge(drive_ready, at(i, w))
                            spread_b(i + 1, 0)
                        if w:
                            sum_states(i, w - 1)
                        if w < U:
                            prepare(i, 1, w)
                        elif not last:
                            prepare(i + 1, 0, w - U)
                        if w == U:
                            project_out(i, 0)
                    sum_states(i, LANES * U - 1)
                    project_out(i, 1)

                for step in range(U):
                    prepare(0, 0, step)
                spread_b(0, 0)
                turns(eng, turn)

            @block.scalar
            def _(eng):
                eng.wait_ge(weights_in, 16 * N_LOADS)
                eng.activation(a_neg[:, :, :], a_neg[:, :, :], ACT.Exp).then_inc(a_ready, 1)
                eng.wait_ge(const_ready, 1)

                def prepare(i, n, step):
                    if step == 1:
                        S.front_copy(eng, i, n, p1[:, 0, :])
                    elif step == 2:
                        eng.wait_ge(xc_in_psum, S.nth(i, n))
                        eng.copy(xc[n][:, :, TAPS - 1:], p1[:, :, :]).then_inc(xc_ready, 1)
                        eng.wait_ge(z_in_psum, S.nth(i, n))
                        eng.activation(z_tanh[n][:, :, :], p2[:, :, :], ACT.Tanh, scale=0.5).then_inc(z_tanh_ready, 1)
                    elif step == 4:
                        eng.wait_ge(u_in_psum, S.nth(i, n))
                        for h in range(HALVES):
                            ins = eng.activation(u_in[n][:, h, :], p1[:, h, :], ACT.Identity, bias=conv_b[:, h:h + 1])
                        ins.then_inc(u_ready, 1)
                    elif step == 5:
                        eng.wait_ge(dt_in_psum, S.nth(i, n))
                        for h in range(HALVES):
                            ins = eng.activation(dt[n][:, h, :], p2[:, h, :], ACT.Tanh, bias=dt_b[:, h:h + 1], scale=0.5)
                        ins.then_inc(dt_tanh_ready, 1)

                def start_unit(i, w):
                    k = w % 2
                    eng.wait_ge(dta_ready, at(i, w))
                    eng.activation(decay[k][:, :, :], dta[k][:, :, :], ACT.Exp).then_inc(decay_ready, 1)
                    eng.wait_ge(drive_ready, at(i, w))
                    eng.activation(drive[k][:, :, :], drive[k][:, :, :], ACT.Identity, bias=tiny[:, 0:1]).then_inc(drive_done, 1)

                def turn(i, last):
                    for w in range(LANES * U):
                        if w + 1 < LANES * U:
                            start_unit(i, w + 1)
                        elif not last:
                            start_unit(i + 1, 0)
                        if w < U:
                            prepare(i, 1, w)
                        elif not last:
                            prepare(i + 1, 0, w - U)

                for step in range(U):
                    prepare(0, 0, step)
                start_unit(0, 0)
                turns(eng, turn)
        S.clear_semaphores()


EXPERTS = 8


def moe_stage(nc, core, name, FC, src, setup, load, has_bias):
    T = 4
    N = T * P
    E = EXPERTS
    with ExitStack() as ctx:
        S = Stage(nc, ctx, name, 1, core, tiles=T, src=src)
        w1 = S.sb("w1", [P, E, FC * P])
        w2 = S.sb("w2", [P, E * FC, P])
        router = S.sb("router", [P, E])
        router_b = S.sb("router_b", [P, E])
        channel = S.sb("channel", [P, E])
        scale = S.sb("scale", [P, E])
        shift = S.sb("shift", [P, E])
        b1 = S.sb("b1", [P, E * FC])
        b2 = S.sb("b2", [E, P])
        hT = [S.sb(f"hT{k}", [P, FC, N]) for k in range(2)]
        logits = S.sb("logits", [P, T, E])
        top = S.sb("top", [P, T, 8])
        top_at = S.sb("top_at", [P, T, 8], mybir.dt.uint32)
        below_top = S.sb("below_top", [P, T, E])
        expd = S.sb("expd", [P, T, E])
        first = S.sb("first", [P, T, E])
        chosen = S.sb("chosen", [P, T, E])
        gate_sum = S.sb("gate_sum", [P, T])
        gates = S.sb("gates", [P, T, E])
        gT = S.sb("gT", [E, N])
        acc = S.r[0]
        pX = S.ps("pX", [P, N])
        pL = S.ps("pL", [P, N])
        pH = [S.ps(f"pH{k}", [P, N]) for k in range(4)]
        pY = [S.ps(f"pY{k}", [P, N]) for k in range(2)]
        logits3 = pL[:, 0:T * E].rearrange("p (t e) -> p t e", t=T)
        (weights_in, scaled, b1_in_psum, weights_ready, logits_in_psum, below_ready, expd_ready, gates_ready,
         gT_in_psum, gT_ready, b2_in_psum, acc_started, h_in_psum, h_ready, y_in_psum, y_used) = (S.sem(n) for n in (
             "weights_in", "scaled", "b1_in_psum", "weights_ready", "logits_in_psum", "below_ready", "expd_ready",
             "gates_ready", "gT_in_psum", "gT_ready", "b2_in_psum", "acc_started", "h_in_psum", "h_ready",
             "y_in_psum", "y_used"))

        def to_tiles(ap):
            return ap.unsqueeze(2).to_broadcast([P, T, E])

        with nc.Block() as block:
            @block.sync
            def _(eng):
                n = load(eng, weights_in, dict(w1=w1, w2=w2, router=router, router_b=router_b, scale=scale,
                                               shift=shift, b1=b1, b2=b2, channel=channel))
                eng.wait_ge(weights_in, 16 * n)

            n_loads = len(setup)

            @block.vector
            def _(eng):
                chain = Chain(eng, S.v_chain)
                eng.wait_ge(weights_in, 16 * n_loads)
                if has_bias:
                    eng.wait_ge(b1_in_psum, 1)
                    eng.tensor_tensor(b1[:, :], b1[:, :], pL[:, 0:E * FC], ALU.add)
                else:
                    eng.tensor_scalar(router[:, :], router[:, :], scale[:, 0:1], None, ALU.mult)
                for e in range(E):
                    ins = eng.tensor_scalar(w1[:, e, :], w1[:, e, :], scale[:, e:e + 1], None, ALU.mult)
                ins.then_inc(weights_ready, 1)

                def front(i):
                    S.front_stats(eng, chain, i, 0)
                    S.front_apply(eng, i, 0)

                def route(i):
                    eng.wait_ge(logits_in_psum, i + 1)
                    chain.link(eng.tensor_tensor(logits[:, :, :], logits3, router_b[:, :].unsqueeze(1)
                                                 .to_broadcast([P, T, E]), ALU.add))
                    for t in range(T):
                        ins = eng.max(top[:, t, :], logits[:, t, :])
                    chain.link(ins)
                    eng.tensor_tensor(below_top[:, :, :], logits[:, :, :], to_tiles(top[:, :, 0]),
                                      ALU.subtract).then_inc(below_ready, 1)
                    for t in range(T):
                        ins = eng.max_index(top_at[:, t, :], top[:, t, :], logits[:, t, :])
                    chain.link(ins)
                    eng.tensor_tensor(first[:, :, :], channel[:, :].unsqueeze(1).to_broadcast([P, T, E]),
                                      to_tiles(top_at[:, :, 0]), ALU.is_equal)
                    chain.link(eng.tensor_tensor(chosen[:, :, :], channel[:, :].unsqueeze(1).to_broadcast([P, T, E]),
                                                 to_tiles(top_at[:, :, 1]), ALU.is_equal))
                    chain.link(eng.tensor_tensor(chosen[:, :, :], chosen[:, :, :], first[:, :, :], ALU.add))
                    eng.wait_ge(expd_ready, i + 1)
                    chain.link(eng.tensor_tensor(expd[:, :, :], expd[:, :, :], chosen[:, :, :], ALU.mult))
                    chain.link(eng.tensor_reduce(gate_sum[:, :], expd[:, :, :], AX.X, ALU.add))
                    chain.link(eng.reciprocal(gate_sum[:, :], gate_sum[:, :]))
                    eng.tensor_tensor(gates[:, :, :], expd[:, :, :], to_tiles(gate_sum[:, :]), ALU.mult)\
                       .then_inc(gates_ready, 1)
                    eng.wait_ge(gates_ready, i + 1)

                def experts(i, after_first):
                    if has_bias:
                        eng.wait_ge(b2_in_psum, i + 1)
                        chain.link(eng.tensor_tensor(acc[:, :, :], S.xn[0][:, :, :],
                                                     pX[:, :].rearrange("p (t c) -> p t c", t=T), ALU.add))
                    else:
                        for t in range(T):
                            ins = eng.tensor_copy(acc[:, t, :], S.rows(i, 0, t))
                        chain.link(ins)
                    for e in range(E):
                        eng.wait_ge(y_in_psum, i * E + (e + 1))
                        for t in range(T):
                            ins = eng.scalar_tensor_tensor(out=acc[:, t, :], in0=pY[e % 2][:, t * P:(t + 1) * P],
                                                           scalar=gates[:, t, e:e + 1], in1=acc[:, t, :],
                                                           op0=ALU.mult, op1=ALU.add)
                        ins.then_inc(y_used, 1)
                        eng.wait_ge(y_used, i * E + (e + 3))
                        if e == 0:
                            after_first()

                def turn(i, after_first):
                    route(i)
                    experts(i, after_first)
                    S.back_norm_stats(eng, chain, 0, acc)
                    S.back_residual(eng, chain, i, 0, acc)
                    chain.restart()

                eng.sem_inc(y_used, 2)
                front(0)
                chain.restart()
                with eng.Fori(0, S.turns - 1) as i:
                    turn(i, lambda: front(i + 1))
                turn(S.turns - 1, lambda: None)

            @block.gpsimd
            def _(eng):
                chain = Chain(eng, S.p_chain)

                def front(i):
                    S.front_rstd(eng, chain, i, 0)

                def turn(i, between):
                    eng.wait_ge(below_ready, i + 1)
                    eng.tensor_tensor(expd[:, :, :], core.e[:, 0:T * E].rearrange("p (t e) -> p t e", t=T),
                                      below_top[:, :, :], ALU.pow).then_inc(expd_ready, 1)
                    between()
                    S.back_rstd_step(eng, chain, i, 0)
                    chain.restart()

                front(0)
                chain.restart()
                with eng.Fori(0, S.turns - 1) as i:
                    turn(i, lambda: front(i + 1))
                turn(S.turns - 1, lambda: None)

            @block.tensor
            def _(eng):
                eng.wait_ge(weights_in, 16 * n_loads)
                if has_bias:
                    for e in range(E):
                        for c in range(FC):
                            ins = eng.matmul(pL[:, e * FC + c:e * FC + c + 1], w1[:, e, c * P:(c + 1) * P],
                                             shift[:, e:e + 1], start=True, stop=True)
                    ins.then_inc(b1_in_psum, 1)
                eng.wait_ge(weights_ready, 1)

                def hidden(i, e):
                    for c in range(FC):
                        k = e * FC + c
                        if k >= 4:
                            eng.wait_ge(h_ready, i * (E * FC) + (k + 1 - 4))
                        eng.matmul(pH[k % 4][:, :], w1[:, e, c * P:(c + 1) * P], S.xT[0][:, :],
                                   start=True, stop=True).then_inc(h_in_psum, 1)

                def back_to_rows(i, e):
                    eng.wait_ge(h_ready, i * (E * FC) + (e + 1) * FC)
                    eng.wait_ge(y_used, i * E + (e + 1))
                    for t in range(T):
                        for c in range(FC):
                            ins = eng.matmul(pY[e % 2][:, t * P:(t + 1) * P], hT[e % 2][:, c, t * P:(t + 1) * P],
                                             w2[:, e * FC + c, :], start=(c == 0), stop=(c == FC - 1))
                    ins.then_inc(y_in_psum, 1)

                def turn(i):
                    S.front_transpose(eng, i, 0, pX)
                    eng.wait_ge(S.xT_ready, i + 1)
                    for t in range(T):
                        ins = eng.matmul(pL[:, t * E:(t + 1) * E], S.xT[0][:, t * P:(t + 1) * P], router[:, :],
                                         start=True, stop=True)
                    ins.then_inc(logits_in_psum, 1)
                    hidden(i, 0)
                    hidden(i, 1)
                    if has_bias:
                        eng.wait_ge(gates_ready, i + 1)
                        for t in range(T):
                            ins = eng.transpose(pL[0:E, t * P:(t + 1) * P], gates[:, t, :], core.ident[:, :])
                        ins.then_inc(gT_in_psum, 1)
                    for e in range(E):
                        back_to_rows(i, e)
                        if e + 2 < E:
                            hidden(i, e + 2)
                        if has_bias and e == 0:
                            eng.wait_ge(gT_ready, i + 1)
                            for t in range(T):
                                ins = eng.matmul(pX[:, t * P:(t + 1) * P], gT[:, t * P:(t + 1) * P], b2[:, :],
                                                 start=True, stop=True)
                            ins.then_inc(b2_in_psum, 1)

                with eng.Fori(0, S.turns) as i:
                    turn(i)

            @block.scalar
            def _(eng):
                eng.wait_ge(weights_in, 16 * n_loads)
                eng.wait_ge(weights_ready, 1)
                with eng.Fori(0, S.turns) as i:
                    S.front_copy(eng, i, 0, pX[:, :])
                    for e in range(E):
                        for c in range(FC):
                            k = e * FC + c
                            eng.wait_ge(h_in_psum, i * (E * FC) + (k + 1))
                            if c == 0 and e >= 2:
                                eng.wait_ge(y_in_psum, i * E + (e - 1))
                            eng.activation(hT[e % 2][:, c, :], pH[k % 4][:, :], ACT.Gelu,
                                           bias=b1[:, k:k + 1] if has_bias else 0.0).then_inc(h_ready, 1)
                            if has_bias and e == 1 and c == FC - 1:
                                eng.wait_ge(gT_in_psum, i + 1)
                                eng.copy(gT[:, :], pL[0:E, :]).then_inc(gT_ready, 1)
        S.clear_semaphores()


def expert_ffn_stage(nc, core, W):
    names = ["router", "router_b", "scale", "shift", "b1", "b2", "channel", "w1", "w2"]

    def load(eng, done, sb):
        eng.dma_start(sb["router"][:, :], W["L1_ffn_router_W"]).then_inc(done, 16)
        eng.dma_start(sb["router_b"][:, :], W["L1_ffn_router_b"].partition_broadcast(P)).then_inc(done, 16)
        eng.dma_start(sb["scale"][:, :], W["L1_ffn_ln_g"]).then_inc(done, 16)
        eng.dma_start(sb["shift"][:, :], W["L1_ffn_ln_b"]).then_inc(done, 16)
        eng.dma_start(sb["b1"][:, :], W["L1_ffn_b1"]).then_inc(done, 16)
        eng.dma_start(sb["b2"][:, :], W["L1_ffn_b2"]).then_inc(done, 16)
        eng.dma_start(sb["channel"][:, :], W["expert_index"].partition_broadcast(P)).then_inc(done, 16)
        eng.dma_start(sb["w1"][:, :, :], W["L1_ffn_W1"].rearrange("e p f -> p e f")).then_inc(done, 16)
        eng.dma_start(sb["w2"][:, :, :], W["L1_ffn_W2"].rearrange("(k p) n -> p k n", p=P)).then_inc(done, 16)
        return len(names)

    moe_stage(nc, core, "l1f", 4, core.X, names, load, True)


def routed_ffn_stage(nc, core, W):
    names = ["router", "router_b", "scale", "channel", "w1", "w2"]

    def load(eng, done, sb):
        eng.dma_start(sb["router"][:, :], W["L0_ffn_router_w"]).then_inc(done, 16)
        eng.dma_start(sb["router_b"][:, :], W["expert_zero"].partition_broadcast(P)).then_inc(done, 16)
        eng.dma_start(sb["scale"][:, :], W["L0_ffn_ln2_w"]).then_inc(done, 16)
        eng.dma_start(sb["channel"][:, :], W["expert_index"].partition_broadcast(P)).then_inc(done, 16)
        eng.dma_start(sb["w1"][:, :, :], W["L0_ffn_w1"].rearrange("p (e f) -> p e f", e=EXPERTS)).then_inc(done, 16)
        eng.dma_start(sb["w2"][:, :, :], W["L0_ffn_w2"].rearrange("(k p) n -> p k n", p=P)).then_inc(done, 16)
        return len(names)

    moe_stage(nc, core, "l0f", 2, core.Y, names, load, False)


HEADS = 16
HEAD = P // HEADS
GROUPS = HEADS // 4
KEYS = 3 * P


def causal_attn_stage(nc, core, name, scale, load, n_loads, alibi, inner):
    with ExitStack() as ctx:
        S = Stage(nc, ctx, name, 2, core)
        wq = S.sb("wq", [P, GROUPS, P])
        wk = S.sb("wk", [P, GROUPS, P])
        wv = S.sb("wv", [P, P])
        wo = S.sb("wo", [P, P])
        ln_w = S.sb("ln_w", [P, 1])
        mask = S.sb("mask", [P, P], BF16)
        ident16 = S.sb("ident16", [P, P], BF16)
        q_bias = S.sb("q_bias", [P, GROUPS, SEQ]) if alibi else None
        k_bias = S.sb("k_bias", [P, GROUPS, SEQ]) if alibi else None
        qT = [S.sb(f"qT{n}", [P, GROUPS, SEQ]) for n in range(2)]
        kT = [S.sb(f"kT{n}", [P, GROUPS, SEQ]) for n in range(2)]
        v = [S.sb(f"v{n}", [P, TILES, HEADS, HEAD + 1]) for n in range(2)]
        prob = [S.sb(f"prob{n}", [P, 4, KEYS]) for n in range(2)]
        probT = [S.sb(f"probT{n}", [P, 3, 4 * P]) for n in range(2)]
        highest = [S.sb(f"highest{n}", [P, 2, 4]) for n in range(2)]
        rden = [S.sb(f"rden{n}", [P, TILES, HEADS]) for n in range(2)]
        oT = [S.sb(f"oT{n}", [P, SEQ]) for n in range(2)]
        pS = S.ps("pS", [P, 4, 512])
        pT = [S.ps(f"pT{n}", [P, 512]) for n in range(2)]
        pO = [S.ps(f"pO{n}", [P, 512]) for n in range(2)]
        o3 = [pO[n][:, 0:TILES * HEADS * (HEAD + 1)].rearrange("p (t h d) -> p t h d", t=TILES, h=HEADS) for n in range(2)]
        units = [(g, n) for g in range(GROUPS) for n in range(2)]
        U = len(units)
        (weights_in, weights_ready, inner_xn, proj_in_psum, proj_copied, v_ready, scores_in_psum, scores_used,
         below_ready, prob_ready, probT_in_psum, probT_ready, o_in_psum, o_ready, oT_in_psum, oT_ready,
         y_in_psum) = (S.sem(s) for s in (
             "weights_in", "weights_ready", "inner_xn", "proj_in_psum", "proj_copied", "v_ready", "scores_in_psum",
             "scores_used", "below_ready", "prob_ready", "probT_in_psum", "probT_ready", "o_in_psum", "o_ready",
             "oT_in_psum", "oT_ready", "y_in_psum"))

        with nc.Block() as block:
            @block.sync
            def _(eng):
                load(eng, weights_in, dict(wq=wq, wk=wk, wv=wv, wo=wo, ln_w=ln_w, mask=mask, ident16=ident16,
                                           q_bias=q_bias, k_bias=k_bias))
                eng.wait_ge(weights_in, 16 * n_loads)

            @block.vector
            def _(eng):
                chain = Chain(eng, S.v_chain)
                for n in range(2):
                    eng.memset(v[n][:, :, :, HEAD:HEAD + 1], 1.0)
                eng.wait_ge(weights_in, 16 * n_loads)
                if inner:
                    eng.tensor_scalar(wv[:, :], wv[:, :], ln_w[:, 0:1], None, ALU.mult)
                    eng.tensor_scalar(wk[:, :, :], wk[:, :, :], ln_w[:, 0:1], None, ALU.mult)
                eng.tensor_scalar(wq[:, :, :], wq[:, :, :], ln_w[:, 0:1] if inner else 1.0, None, ALU.mult)\
                   .then_inc(weights_ready, 1)
                with eng.Fori(0, S.turns) as i:
                    for n in range(2):
                        S.front_stats(eng, chain, i, n)
                    for n in range(2):
                        S.front_apply(eng, i, n)
                        if inner:
                            eng.wait_ge(S.xn_ready, S.nth(i, n))
                            S.back_norm_stats(eng, chain, n, S.xn[n])
                    for n in range(2):
                        if inner:
                            eng.wait_ge(S.back_rstd_ready, S.nth(i, n))
                            for t in range(TILES):
                                ins = eng.tensor_scalar(S.r[n][:, t, :], S.xn[n][:, t, :], S.back_mv[:, n, t, 0:1],
                                                        S.back_rstd[:, n, t:t + 1], ALU.subtract, ALU.mult)
                            ins.then_inc(inner_xn, 1)
                    for n in range(2):
                        for b in range(4):
                            eng.wait_ge(proj_in_psum, S.nth(i, n, 5, b))
                            dst = (qT if b < 2 else kT)[n][:, 2 * (b % 2):2 * (b % 2) + 2, :]
                            src = pT[b % 2][:, :].rearrange("p (g s) -> p g s", g=2)
                            if alibi:
                                bias = (q_bias if b < 2 else k_bias)[:, 2 * (b % 2):2 * (b % 2) + 2, :]
                                eng.tensor_tensor(dst, src, bias, ALU.add).then_inc(proj_copied, 1)
                            else:
                                eng.tensor_copy(dst, src).then_inc(proj_copied, 1)
                        eng.wait_ge(proj_in_psum, S.nth(i, n, 5, 4))
                        eng.tensor_copy(v[n][:, :, :, 0:HEAD],
                                        pT[0][:, 0:SEQ].rearrange("p (t h d) -> p t h d", t=TILES, h=HEADS))\
                           .then_inc(proj_copied, 1)
                    for u, (g, n) in enumerate(units):
                        eng.wait_ge(scores_in_psum, i * U + (u + 1))
                        eng.tensor_reduce(highest[u % 2][:, 0, :], pS[:, :, 0:P], AX.X, ALU.max)
                        chain.link(eng.tensor_reduce(highest[u % 2][:, 1, :], pS[:, :, P:KEYS], AX.X, ALU.max))
                        for a, (lo, hi) in enumerate(((0, P), (P, KEYS))):
                            ins = eng.tensor_tensor(prob[u % 2][:, :, lo:hi], pS[:, :, lo:hi],
                                                    highest[u % 2][:, a, :].unsqueeze(2).to_broadcast([P, 4, hi - lo]),
                                                    ALU.subtract)
                        ins.then_inc(below_ready, 1)
                    for n in range(2):
                        eng.wait_ge(o_in_psum, S.nth(i, n))
                        chain.link(eng.reciprocal(rden[n][:, :, :], o3[n][:, :, :, HEAD]))
                        eng.tensor_tensor(S.r[n][:, :, :].rearrange("p t (h d) -> p t h d", h=HEADS),
                                          o3[n][:, :, :, 0:HEAD],
                                          rden[n][:, :, :].unsqueeze(3).to_broadcast([P, TILES, HEADS, HEAD]),
                                          ALU.mult).then_inc(o_ready, 1)
                        if not inner:
                            eng.wait_ge(o_ready, S.nth(i, n))
                            S.back_norm_stats(eng, chain, n, S.r[n])
                    for n in range(2):
                        if inner:
                            eng.wait_ge(y_in_psum, S.nth(i, n))
                            for t in range(TILES):
                                eng.tensor_tensor(S.of(core.Y, i, n, t), S.xn[n][:, t, :],
                                                  pO[n][:, t * P:(t + 1) * P], ALU.add)
                        else:
                            S.back_residual(eng, chain, i, n, S.r[n])
                    chain.restart()

            @block.gpsimd
            def _(eng):
                chain = Chain(eng, S.p_chain)
                with eng.Fori(0, S.turns) as i:
                    for n in range(2):
                        S.front_rstd(eng, chain, i, n)
                    for n in range(2):
                        S.back_rstd_step(eng, chain, i, n)
                    chain.restart()

            @block.tensor
            def _(eng):
                eng.wait_ge(weights_in, 16 * n_loads)
                eng.wait_ge(weights_ready, 1)

                def scores(i, u):
                    g, n = units[u]
                    eng.wait_ge(proj_copied, S.nth(i, n, 5, 4))
                    if u > 0:
                        eng.wait_ge(below_ready, i * U + u)
                    for r in range(4):
                        q = qT[n][32 * r:32 * r + 32, g, :]
                        k = kT[n][32 * r:32 * r + 32, g, :]
                        eng.matmul(pS[:, r, 0:P], q[:, 0:P], k[:, 0:P], start=True, stop=True)
                        eng.matmul(pS[:, r, P:KEYS], q[:, P:SEQ], k, start=False, stop=True, skip_group_check=True)
                    for r in range(4):
                        eng.matmul(pS[:, r, 0:P], ident16[:, :], mask[:, :], start=False, stop=True,
                                   skip_group_check=True)
                        ins = eng.matmul(pS[:, r, 2 * P:3 * P], ident16[:, :], mask[:, :], start=False, stop=True,
                                         skip_group_check=True)
                    ins.then_inc(scores_in_psum, 1)

                def weigh(i, u):
                    g, n = units[u]
                    eng.wait_ge(prob_ready, i * U + (u + 1))
                    for c in range(3):
                        k = 3 * u + c
                        if k >= 2:
                            eng.wait_ge(probT_ready, i * (3 * U) + (k - 1))
                        for r in range(4):
                            ins = eng.transpose(pT[k % 2][:, r * P:(r + 1) * P],
                                                prob[u % 2][:, r, c * P:(c + 1) * P], core.ident[:, :])
                        ins.then_inc(probT_in_psum, 1)
                    for c, (t, kt) in enumerate(((0, 0), (1, 0), (1, 1))):
                        eng.wait_ge(probT_ready, i * (3 * U) + (3 * u + c + 1))
                        for r in range(4):
                            ins = eng.matmul(o3[n][:, t, 4 * g + r, :], probT[u % 2][:, c, r * P:(r + 1) * P],
                                             v[n][:, kt, 4 * g + r, :], start=(g == 0 and c == 0 and r == 0),
                                             stop=True, skip_group_check=True)
                    if g == GROUPS - 1:
                        ins.then_inc(o_in_psum, 1)

                with eng.Fori(0, S.turns) as i:
                    for n in range(2):
                        S.transpose_rows(eng, i, n, pO[n], S.r[n] if inner else S.xn[n],
                                         inner_xn if inner else S.xn_ready, S.xt_in_psum)
                    for n in range(2):
                        eng.wait_ge(S.xT_ready, S.nth(i, n))
                        for b in range(5):
                            if n or b >= 2:
                                eng.wait_ge(proj_copied, i * 10 + (5 * n + b - {0: 0, 1: 2}.get(b, 1)))
                            if b < 4:
                                for h in range(2):
                                    ins = eng.matmul(pT[b % 2][:, h * SEQ:(h + 1) * SEQ],
                                                     (wq if b < 2 else wk)[:, 2 * (b % 2) + h, :], S.xT[n][:, :],
                                                     start=True, stop=True)
                            else:
                                for t in range(TILES):
                                    ins = eng.matmul(pT[0][:, t * P:(t + 1) * P], S.xT[n][:, t * P:(t + 1) * P],
                                                     wv[:, :], start=True, stop=True)
                            ins.then_inc(proj_in_psum, 1)
                    scores(i, 0)
                    for u in range(U):
                        if u + 1 < U:
                            scores(i, u + 1)
                        weigh(i, u)
                    if inner:
                        for n in range(2):
                            S.transpose_rows(eng, i, n, pO[n], S.r[n], o_ready, oT_in_psum)
                        for n in range(2):
                            eng.wait_ge(oT_ready, S.nth(i, n))
                            for t in range(TILES):
                                ins = eng.matmul(pO[n][:, t * P:(t + 1) * P], oT[n][:, t * P:(t + 1) * P], wo[:, :],
                                                 start=True, stop=True)
                            ins.then_inc(y_in_psum, 1)

            @block.scalar
            def _(eng):
                with eng.Fori(0, S.turns) as i:
                    for n in range(2):
                        S.front_copy(eng, i, n, pO[n][:, 0:SEQ])

                    def exps(u):
                        eng.wait_ge(below_ready, i * U + (u + 1))
                        eng.activation(prob[u % 2][:, :, :], prob[u % 2][:, :, :], ACT.Exp, scale=scale)\
                           .then_inc(prob_ready, 1)

                    for u in range(U):
                        exps(u)
                        for c in range(3):
                            k = 3 * u + c
                            eng.wait_ge(probT_in_psum, i * (3 * U) + (k + 1))
                            eng.copy(probT[u % 2][:, c, :], pT[k % 2][:, :]).then_inc(probT_ready, 1)
                    if inner:
                        for n in range(2):
                            eng.wait_ge(oT_in_psum, S.nth(i, n))
                            eng.copy(oT[n][:, :], pO[n][:, 0:SEQ]).then_inc(oT_ready, 1)
        S.clear_semaphores()


def alibi_attn_stage(nc, core, W):
    def load(eng, done, sb):
        for n in ("wq", "wk", "wv"):
            dst = sb[n][:, :] if n == "wv" else sb[n][:, :, :]
            eng.dma_start(dst, W[f"L3_attn_{n}"]).then_inc(done, 16)
        eng.dma_start(sb["q_bias"][:, :, :], W["alibi_q"]).then_inc(done, 16)
        eng.dma_start(sb["k_bias"][:, :, :], W["alibi_k"]).then_inc(done, 16)
        eng.dma_start(sb["mask"][:, :], W["causal_mask"]).then_inc(done, 16)
        eng.dma_start(sb["ident16"][:, :], W["ident16"]).then_inc(done, 16)

    causal_attn_stage(nc, core, "l3a", float(P) ** -0.5, load, 7, True, False)


def routed_block_stage(nc, core, W):
    def load(eng, done, sb):
        for n in ("wq", "wk", "wv", "wo"):
            dst = sb[n][:, :] if n in ("wv", "wo") else sb[n][:, :, :]
            eng.dma_start(dst, W[f"L0_ffn_{n}"]).then_inc(done, 16)
        eng.dma_start(sb["ln_w"][:, :], W["L0_ffn_ln1_w"]).then_inc(done, 16)
        eng.dma_start(sb["mask"][:, :], W["causal_mask"]).then_inc(done, 16)
        eng.dma_start(sb["ident16"][:, :], W["ident16"]).then_inc(done, 16)

    with ExitStack() as ctx:
        inner_rows(nc, ctx, core, "l0f_rows")
        causal_attn_stage(nc, core, "l0t", float(HEAD) ** -0.5, load, 7, False, True)
        routed_ffn_stage(nc, core, W)


def bond_attn_stage(nc, core, W):
    H, BD, K = 16, 16, 32
    HALVES = 2
    T = 4
    N = T * P
    SEQS = 2
    PAD = K - 1
    BATCH = 4
    RUN = 16
    BATCHES = HALVES * K // BATCH
    RUNS = HALVES * K // RUN
    RING = 2
    HG = 8
    scratch = nc.dram_tensor("val_rows", [SEQS, PAD + SEQ, P], F32).ap()
    with ExitStack() as ctx:
        S = Stage(nc, ctx, "l1a", 1, core, tiles=T)
        w_disp = S.sb("w_disp", [P, 2 * P])
        w_val = S.sb("w_val", [P, P])
        w_cproj = S.sb("w_cproj", [P, P])
        w_small = S.sb("w_small", [P, 6, P])
        w_bond = S.sb("w_bond", [P, RUN, P])
        w_damage_out = S.sb("w_damage_out", [P, RUN, P])
        biases = S.sb("biases", [P, 6])
        w_pos = S.sb("w_pos", [BD, P])
        rel_emb = S.sb("rel_emb", [BD, K])
        pos = S.sb("pos", [P, K])
        b_val = S.sb("b_val", [P, P])
        b_cproj = S.sb("b_cproj", [P, P])
        b_bond = S.sb("b_bond", [P, 1])
        mask = S.sb("mask", [P, TILES, K])
        mean_w = S.sb("mean_w", [P, TILES, SEQ])
        zeros = S.sb("zeros", [PAD, P])
        diff = S.sb("diff", [P, N])
        disp = S.sb("disp", [P, N])
        disp_diff = S.sb("disp_diff", [P, N])
        state = S.sb("state", [P, N])
        a_bond = S.sb("a_bond", [P, HALVES, SEQS, PAD + SEQ])
        b_bond_in = S.sb("b_bond_in", [P, HALVES, SEQS, SEQ])
        a_dmg = S.sb("a_dmg", [P, HALVES, SEQS, PAD + SEQ])
        b_dmg = S.sb("b_dmg", [P, HALVES, SEQS, SEQ])
        bond = [S.sb(f"bond{k}", [P, BATCH, SEQS, SEQ]) for k in range(RING)]
        dmg = [S.sb(f"dmg{k}", [P, BATCH, SEQS, SEQ]) for k in range(RING)]
        logit = S.sb("logit", [P, RUNS, N])
        damage = S.sb("damage", [P, RUNS, N])
        weight = S.sb("weight", [P, T, H, K])
        highest = S.sb("highest", [P, T * H])
        total = S.sb("total", [P, T * H])
        val = S.sb("val", [P, T, P])
        window = S.sb("window", [P, K, P])
        prod = S.sb("prod", [P, HG, P // H, K])
        o = S.r[0]
        oT = S.sb("oT", [P, N])
        p1 = S.ps("p1", [P, N])
        p2 = S.ps("p2", [P, N])
        p3 = S.ps("p3", [P, N])
        p4 = S.ps("p4", [P, N])
        pBond = [S.ps(f"pBond{k}", [P, N]) for k in range(2)]
        pDmg = [S.ps(f"pDmg{k}", [P, N]) for k in range(2)]
        (weights_in, pad_ready, setup_psum, setup_ready, pad_stored, mean_in_psum, diff_ready, lin_in_psum, lin_ready,
         val_in_psum, val_ready, val_stored, window_in, window_used, bond_in, dmg_in, bond_act, dmg_act, bond_used,
         dmg_used, run_in_psum, run_copied, tanh_ready, logits_ready, logits_in_psum, below_ready, exp_ready,
         o_ready, oT_in_psum, oT_ready, y_in_psum) = (S.sem(s) for s in (
             "weights_in", "pad_ready", "setup_psum", "setup_ready", "pad_stored", "mean_in_psum", "diff_ready",
             "lin_in_psum", "lin_ready", "val_in_psum", "val_ready", "val_stored", "window_in", "window_used",
             "bond_in", "dmg_in", "bond_act", "dmg_act", "bond_used", "dmg_used", "run_in_psum", "run_copied",
             "tanh_ready", "logits_ready", "logits_in_psum", "below_ready", "exp_ready", "o_ready", "oT_in_psum",
             "oT_ready", "y_in_psum"))
        LIN = 7
        N_LOADS = 14

        def batch(b):
            return b // (K // BATCH), b % (K // BATCH) * BATCH

        def two(ap):
            return ap.rearrange("p (n s) -> p n s", n=SEQS)

        with nc.Block() as block:
            @block.sync
            def _(eng):
                loads = [(w_disp, "w_disp"), (w_val, "w_val"), (w_cproj, "w_cproj"), (w_small, "w_small"),
                         (w_bond, "w_bond"), (w_damage_out, "w_damage_out"), (biases, "biases"), (w_pos, "w_pos"),
                         (rel_emb, "rel_emb"), (mask, "mask"), (mean_w, "mean_w")]
                for dst, name in loads:
                    eng.dma_start(dst[:], W[f"L1_attn_{name}"]).then_inc(weights_in, 16)
                for dst, name in ((b_val, "b_val"), (b_cproj, "b_cproj"), (b_bond, "b_bond_out")):
                    eng.dma_start(dst[:, :], W[f"L1_attn_{name}"].partition_broadcast(P)).then_inc(weights_in, 16)
                eng.wait_ge(weights_in, 16 * N_LOADS)
                eng.wait_ge(pad_ready, 1)
                for n in range(SEQS):
                    eng.dma_start(scratch[n, 0:PAD, :], zeros[:, :]).then_inc(pad_stored, 16)
                eng.wait_ge(pad_stored, 16 * SEQS)
                with eng.Fori(0, S.turns) as i:
                    eng.wait_ge(val_ready, i + 1)
                    for n in range(SEQS):
                        eng.dma_start(scratch[n, PAD:, :].rearrange("(t p) c -> p t c", p=P),
                                      val[:, n * TILES:(n + 1) * TILES, :]).then_inc(val_stored, 16)
                    eng.wait_ge(val_stored, i * (16 * SEQS) + 16 * SEQS)
                    for t in range(T):
                        eng.wait_ge(window_used, i * T + (t + 1))
                        rows = scratch[t // TILES]
                        src = bass.AP(tensor=rows.tensor, offset=rows.offset + t % TILES * P * P, ap=[[P, P], [1, K * P]])
                        eng.dma_start(window[:, :, :].rearrange("p k c -> p (k c)"), src).then_inc(window_in, 16)

            @block.vector
            def _(eng):
                chain = Chain(eng, S.v_chain)
                eng.memset(zeros[:, :], 0.0).then_inc(pad_ready, 1)
                eng.memset(a_bond[:, :, :, 0:PAD], 0.0)
                eng.memset(a_dmg[:, :, :, 0:PAD], 0.0)
                eng.wait_ge(weights_in, 16 * N_LOADS)
                eng.wait_ge(setup_psum, 1)
                eng.tensor_copy(pos[:, :], p1[:, 0:K])
                chain.link(eng.tensor_scalar(b_bond[:, :], b_bond[:, :], -5.0, None, ALU.add))
                eng.tensor_scalar(mask[:, :, :], mask[:, :, :], b_bond[:, 0:1], None, ALU.add)
                eng.tensor_scalar(biases[:, 5:6], biases[:, 5:6], 0.5, None, ALU.mult)
                eng.tensor_scalar(w_small[:, 5, :], w_small[:, 5, :], -1.0, None, ALU.mult).then_inc(setup_ready, 1)
                eng.wait_ge(setup_ready, 1)
                eng.sem_inc(window_used, 1)
                chain.restart()

                with eng.Fori(0, S.turns) as i:
                    S.front_stats(eng, chain, i, 0)
                    S.front_apply(eng, i, 0)
                    eng.wait_ge(mean_in_psum, i + 1)
                    eng.wait_ge(S.xT_ready, i + 1)
                    eng.tensor_tensor(diff[:, :], p2[:, :], S.xT[0][:, :], ALU.subtract).then_inc(diff_ready, 1)
                    eng.wait_ge(val_in_psum, i + 1)
                    eng.tensor_tensor(val[:, :, :], p2[:, :].rearrange("p (t c) -> p t c", t=T),
                                      b_val[:, :].unsqueeze(1).to_broadcast([P, T, P]), ALU.add).then_inc(val_ready, 1)
                    for b in range(BATCHES):
                        half, k0 = batch(b)
                        eng.wait_ge(lin_ready, i * (HALVES * LIN) + (half * LIN + LIN))
                        eng.wait_ge(bond_used, i * BATCHES + (b + 1))
                        for j in range(BATCH):
                            k = k0 + j
                            ins = eng.scalar_tensor_tensor(out=bond[b % RING][:, j, :, :],
                                                           in0=a_bond[:, half, :, k:k + SEQ], scalar=pos[:, k:k + 1],
                                                           in1=b_bond_in[:, half, :, :], op0=ALU.add, op1=ALU.add)
                        ins.then_inc(bond_in, 1)
                    eng.wait_ge(tanh_ready, i + 1)
                    eng.scalar_tensor_tensor(out=logit[:, :, :], in0=damage[:, :, :], scalar=-5.0, in1=logit[:, :, :],
                                             op0=ALU.mult, op1=ALU.add).then_inc(logits_ready, 1)
                    for t in range(T):
                        eng.wait_ge(logits_in_psum, i * T + (t + 1))
                        src = (p1, p2, p3, p4)[t][:, :].rearrange("p (a b h k) -> p a b h k", a=HALVES, b=2, h=8)
                        dst = weight[:, t, :, :].rearrange("p (a h) (b k) -> p a b h k", a=HALVES, b=2)
                        for a in range(HALVES):
                            m = mask[:, t % TILES, :].rearrange("p (b k) -> p b k", b=2).unsqueeze(2)\
                                .to_broadcast([P, 2, 8, RUN])
                            ins = eng.tensor_tensor(dst[:, a], src[:, a], m, ALU.add)
                    chain.link(ins)
                    rows3 = weight[:, :, :, :].rearrange("p t h k -> p (t h) k")
                    chain.link(eng.tensor_reduce(highest[:, :], rows3, AX.X, ALU.max))
                    eng.tensor_tensor(rows3, rows3, highest[:, :].unsqueeze(2).to_broadcast([P, T * H, K]), ALU.subtract)\
                       .then_inc(below_ready, 1)
                    eng.wait_ge(exp_ready, i + 1)
                    chain.link(eng.tensor_reduce(total[:, :], rows3, AX.X, ALU.add))
                    chain.link(eng.reciprocal(total[:, :], total[:, :]))
                    for t in range(T):
                        eng.wait_ge(window_in, i * (16 * T) + 16 * (t + 1))
                        for g in range(H // HG):
                            v = window[:, :, g * HG * 8:(g + 1) * HG * 8].rearrange("p k (h e) -> p h e k", h=HG)
                            wgt = weight[:, t, g * HG:(g + 1) * HG, :]
                            mul = eng.tensor_tensor(prod[:, :, :, :], v, wgt.unsqueeze(2).to_broadcast([P, HG, 8, K]), ALU.mult)
                            if g == H // HG - 1:
                                mul.then_inc(window_used, 1)
                                eng.wait_ge(window_used, i * T + (t + 2))
                            else:
                                chain.link(mul)
                            chain.link(eng.tensor_reduce(o[:, t, g * HG * 8:(g + 1) * HG * 8].rearrange("p (h e) -> p h e", h=HG),
                                                         prod[:, :, :, :], AX.X, ALU.add))
                    eng.tensor_tensor(o[:, :, :].rearrange("p t (h e) -> p (t h) e", h=H),
                                      o[:, :, :].rearrange("p t (h e) -> p (t h) e", h=H),
                                      total[:, :].unsqueeze(2).to_broadcast([P, T * H, P // H]), ALU.mult).then_inc(o_ready, 1)
                    eng.wait_ge(y_in_psum, i + 1)
                    chain.link(eng.tensor_tensor(o[:, :, :], p2[:, :].rearrange("p (t c) -> p t c", t=T),
                                                 b_cproj[:, :].unsqueeze(1).to_broadcast([P, T, P]), ALU.add))
                    S.back_norm_stats(eng, chain, 0, o)
                    S.back_residual(eng, chain, i, 0, o)
                    chain.restart()

            @block.gpsimd
            def _(eng):
                chain = Chain(eng, S.p_chain)
                eng.wait_ge(setup_ready, 1)
                with eng.Fori(0, S.turns) as i:
                    S.front_rstd(eng, chain, i, 0)
                    for b in range(BATCHES):
                        half, k0 = batch(b)
                        eng.wait_ge(lin_ready, i * (HALVES * LIN) + (half * LIN + LIN))
                        eng.wait_ge(dmg_used, i * BATCHES + (b + 1))
                        for j in range(BATCH):
                            k = k0 + j
                            ins = eng.tensor_tensor(dmg[b % RING][:, j, :, :], a_dmg[:, half, :, k:k + SEQ],
                                                    b_dmg[:, half, :, :], ALU.add)
                        ins.then_inc(dmg_in, 1)
                    S.back_rstd_step(eng, chain, i, 0)
                    chain.restart()

            @block.tensor
            def _(eng):
                eng.wait_ge(weights_in, 16 * N_LOADS)
                eng.matmul(p1[:, 0:K], w_pos[:, :], rel_emb[:, :], start=True, stop=True).then_inc(setup_psum, 1)
                eng.wait_ge(setup_ready, 1)
                eng.sem_inc(bond_used, RING)
                eng.sem_inc(dmg_used, RING)
                STATE, STRAIN, STATE_I, STATE_J, DAMAGE, MINUS_STRAIN = range(6)
                with eng.Fori(0, S.turns) as i:
                    S.front_transpose(eng, i, 0, p1)
                    for n in range(SEQS):
                        for t in range(TILES):
                            ins = eng.matmul(p2[:, n * SEQ:(n + 1) * SEQ], S.xn[0][:, n * TILES + t, :], mean_w[:, t, :],
                                             start=(t == 0), stop=(t == TILES - 1))
                    ins.then_inc(mean_in_psum, 1)
                    eng.wait_ge(diff_ready, i + 1)
                    for t in range(T):
                        ins = eng.matmul(p2[:, t * P:(t + 1) * P], S.xT[0][:, t * P:(t + 1) * P], w_val[:, :],
                                         start=True, stop=True)
                    ins.then_inc(val_in_psum, 1)
                    for half in range(HALVES):
                        base = half * LIN
                        if half:
                            eng.wait_ge(lin_ready, i * (HALVES * LIN) + base)
                        cols = slice(half * P, (half + 1) * P)
                        eng.matmul(p1[:, :], w_disp[:, cols], S.xT[0][:, :], start=True, stop=True).then_inc(lin_in_psum, 1)
                        eng.matmul(p3[:, :], w_disp[:, cols], diff[:, :], start=True, stop=True).then_inc(lin_in_psum, 1)
                        eng.wait_ge(lin_ready, i * (HALVES * LIN) + (base + 2))
                        eng.matmul(p4[:, :], w_small[:, STATE, :], disp_diff[:, :], start=True, stop=True).then_inc(lin_in_psum, 1)
                        eng.matmul(p1[:, :], w_small[:, DAMAGE, :], disp[:, :], start=True, stop=True).then_inc(lin_in_psum, 1)
                        eng.wait_ge(lin_ready, i * (HALVES * LIN) + (base + 3))
                        eng.matmul(p3[:, :], w_small[:, STRAIN, :], disp[:, :], start=True, stop=False)
                        eng.matmul(p3[:, :], w_small[:, STATE_J, :], state[:, :], start=False, stop=True).then_inc(lin_in_psum, 1)
                        eng.matmul(p4[:, :], w_small[:, STATE_I, :], state[:, :], start=True, stop=False)
                        eng.matmul(p4[:, :], w_small[:, MINUS_STRAIN, :], disp[:, :], start=False, stop=True).then_inc(lin_in_psum, 1)
                    for b in range(BATCHES):
                        half, k0 = batch(b)
                        run = b * BATCH // RUN
                        if b * BATCH % RUN == 0 and run >= 2:
                            eng.wait_ge(run_copied, i * RUNS + (run - 1))
                        for act, used, w, bank, buf in ((bond_act, bond_used, w_bond, pBond, bond),
                                                        (dmg_act, dmg_used, w_damage_out, pDmg, dmg)):
                            eng.wait_ge(act, i * BATCHES + (b + 1))
                            for j in range(BATCH):
                                k = (k0 + j) % RUN
                                ins = eng.matmul(two(bank[run % 2][:, :]), w[:, k, :], buf[b % RING][:, j, :, :],
                                                 start=(k == 0), stop=(k == RUN - 1))
                            ins.then_inc(used, 1)
                        if (b + 1) * BATCH % RUN == 0:
                            eng.wait_ge(dmg_used, i * BATCHES + (b + 1 + RING))
                            eng.sem_inc(run_in_psum, 1)
                    eng.wait_ge(logits_ready, i + 1)
                    for t in range(T):
                        for r in range(RUNS):
                            ins = eng.transpose((p1, p2, p3, p4)[t][:, r * P:(r + 1) * P], logit[:, r, t * P:(t + 1) * P],
                                                core.ident[:, :])
                        ins.then_inc(logits_in_psum, 1)
                    S.transpose_rows(eng, i, 0, p1, o, o_ready, oT_in_psum)
                    eng.wait_ge(oT_ready, i + 1)
                    for t in range(T):
                        ins = eng.matmul(p2[:, t * P:(t + 1) * P], oT[:, t * P:(t + 1) * P], w_cproj[:, :],
                                         start=True, stop=True)
                    ins.then_inc(y_in_psum, 1)

            @block.scalar
            def _(eng):
                eng.wait_ge(weights_in, 16 * N_LOADS)
                eng.wait_ge(setup_ready, 1)
                with eng.Fori(0, S.turns) as i:
                    S.front_copy(eng, i, 0, p1[:, :])

                    def lin(k, copies):
                        eng.wait_ge(lin_in_psum, i * (HALVES * (LIN - 1)) + k)
                        for out, src, bias, sign in copies:
                            eng.activation(out, src, ACT.Identity, bias=bias, scale=sign).then_inc(lin_ready, 1)

                    for half in range(HALVES):
                        base = half * (LIN - 1)
                        lin(base + 1, [(disp[:, :], p1[:, :], biases[:, half:half + 1], 1.0)])
                        lin(base + 2, [(disp_diff[:, :], p3[:, :], 0.0, 1.0)])
                        lin(base + 3, [(state[:, :], p4[:, :], biases[:, 2:3], 1.0)])
                        lin(base + 4, [(a_dmg[:, half, :, PAD:], two(p1[:, :]), 0.0, 1.0),
                                       (b_dmg[:, half, :, :], two(p1[:, :]), biases[:, 4:5], -1.0)])
                        lin(base + 5, [(a_bond[:, half, :, PAD:], two(p3[:, :]), 0.0, 1.0)])
                        lin(base + 6, [(b_bond_in[:, half, :, :], two(p4[:, :]), biases[:, 3:4], 1.0)])

                    def copy_run(run):
                        eng.wait_ge(run_in_psum, i * RUNS + (run + 1))
                        eng.copy(logit[:, run, :], pBond[run % 2][:, :])
                        eng.copy(damage[:, run, :], pDmg[run % 2][:, :]).then_inc(run_copied, 1)

                    for b in range(BATCHES):
                        for came, act, buf in ((bond_in, bond_act, bond), (dmg_in, dmg_act, dmg)):
                            eng.wait_ge(came, i * BATCHES + (b + 1))
                            eng.activation(buf[b % RING][:], buf[b % RING][:], ACT.Gelu).then_inc(act, 1)
                        if b and b * BATCH % RUN == 0:
                            copy_run(b * BATCH // RUN - 1)
                    copy_run(RUNS - 1)
                    eng.wait_ge(run_copied, i * RUNS + RUNS)
                    eng.activation(damage[:, :, :], damage[:, :, :], ACT.Tanh, bias=biases[:, 5:6], scale=0.5)\
                       .then_inc(tanh_ready, 1)
                    eng.wait_ge(below_ready, i + 1)
                    eng.activation(weight[:, :, :, :], weight[:, :, :, :], ACT.Exp).then_inc(exp_ready, 1)
                    eng.wait_ge(oT_in_psum, i + 1)
                    eng.copy(oT[:, :], p1[:, :]).then_inc(oT_ready, 1)
        S.clear_semaphores()


def linear_attn_stage(nc, core, W):
    HD = 8
    HEADS = P // HD
    LOG_C = 5.545177444479562
    with ExitStack() as ctx:
        S = Stage(nc, ctx, "l2a", 2, core)
        wqkv = S.sb("wqkv", [P, 3 * P])
        wo = S.sb("wo", [P, P])
        norm_const = S.sb("norm_const", [P, P])
        v_factor = S.sb("v_factor", [P, P])
        same_head = S.sb("same_head", [P, P])
        sq = [S.sb(f"sq{k}", [P, TILES, 2 * P]) for k in range(2)]
        n2 = [S.sb(f"n2{k}", [P, TILES * 2 * HEADS]) for k in range(2)]
        qk = [S.sb(f"qk{k}", [P, TILES, 2 * P]) for k in range(2)]
        v = [S.sb(f"v{k}", [P, TILES, P]) for k in range(2)]
        qT = [S.sb(f"qT{k}", [P, SEQ]) for k in range(2)]
        kv = [S.sb(f"kv{k}", [P, P]) for k in range(2)]
        oT = [S.sb(f"oT{k}", [P, SEQ]) for k in range(2)]
        pT = [S.ps(f"pT{k}", [P, 512]) for k in range(2)]
        pQ = [S.ps(f"pQ{k}", [P, TILES, 512]) for k in range(2)]
        pM = [S.ps(f"pM{k}", [P, 512]) for k in range(2)]
        y = [pT[k][:, 256:512].rearrange("p (t c) -> p t c", t=TILES) for k in range(2)]
        (weights_in, qkv_in_psum, sq_ready, n2_ready, norm_ready, qkv_ready, kv_in_psum, kv_ready, qT_ready,
         oT_in_psum, oT_ready, y_in_psum, factor, mask_ready) = (S.sem(n) for n in (
            "weights_in", "qkv_in_psum", "sq_ready", "n2_ready", "norm_ready", "qkv_ready", "kv_in_psum",
            "kv_ready", "qT_ready", "oT_in_psum", "oT_ready", "y_in_psum", "factor", "mask_ready"))
        with nc.Block() as block:
            @block.sync
            def _(eng):
                eng.dma_start(wqkv[:, :], W["L2_attn_Wqkv"]).then_inc(weights_in, 16)
                eng.dma_start(wo[:, :], W["L2_attn_Wo"]).then_inc(weights_in, 16)
                eng.dma_start(norm_const[:, :], W["L2_attn_norm_const"].partition_broadcast(P)).then_inc(weights_in, 16)
                eng.dma_start(same_head[:, :], W["same_head"]).then_inc(weights_in, 16)
                eng.wait_ge(weights_in, 64)

            @block.vector
            def _(eng):
                chain = Chain(eng, S.v_chain)
                eng.wait_ge(factor, 1)
                eng.tensor_scalar(v_factor[:, :], v_factor[:, :], 1.0, -0.5 * LOG_C, ALU.add, ALU.mult).then_inc(mask_ready, 1)
                eng.wait_ge(factor, 2)
                with eng.Fori(0, S.turns) as i:
                    for n in range(2):
                        S.front_stats(eng, chain, i, n)
                    for n in range(2):
                        S.front_apply(eng, i, n)
                    for n in range(2):
                        eng.wait_ge(sq_ready, S.nth(i, n))
                        chain.link(eng.tensor_reduce(n2[n][:, :].rearrange("p (t h) -> p t h", t=TILES),
                                                     sq[n][:, :, :].rearrange("p t (h d) -> p t h d", d=HD), AX.X, ALU.add))
                        eng.tensor_scalar(n2[n][:, :], n2[n][:, :], 1e-24, None, ALU.max).then_inc(n2_ready, 1)
                    for n in range(2):
                        for t in range(TILES):
                            ins = eng.tensor_tensor(v[n][:, t, :], pQ[n][:, t, 2 * P:3 * P], v_factor[:, :], ALU.mult)
                        eng.wait_ge(norm_ready, S.nth(i, n))
                        chain.link(eng.reciprocal(n2[n][:, :], n2[n][:, :]))
                        eng.tensor_tensor(qk[n][:, :, :].rearrange("p t (h d) -> p t h d", d=HD),
                                          pQ[n][:, :, 0:2 * P].rearrange("p t (h d) -> p t h d", d=HD),
                                          n2[n][:, :].rearrange("p (t h) -> p t h", t=TILES).unsqueeze(3)
                                          .to_broadcast([P, TILES, 2 * HEADS, HD]), ALU.mult).then_inc(qkv_ready, 1)
                    for n in range(2):
                        eng.wait_ge(kv_in_psum, S.nth(i, n))
                        eng.tensor_tensor(kv[n][:, :], pM[n][:, 0:P], same_head[:, :], ALU.mult).then_inc(kv_ready, 1)
                    for n in range(2):
                        eng.wait_ge(y_in_psum, S.nth(i, n))
                        S.back_norm_stats(eng, chain, n, y[n])
                    for n in range(2):
                        S.back_residual(eng, chain, i, n, y[n])
                    chain.restart()

            @block.gpsimd
            def _(eng):
                chain = Chain(eng, S.p_chain)
                with eng.Fori(0, S.turns) as i:
                    for n in range(2):
                        S.front_rstd(eng, chain, i, n)
                    for n in range(2):
                        S.back_rstd_step(eng, chain, i, n)
                    chain.restart()

            @block.tensor
            def _(eng):
                eng.wait_ge(weights_in, 64)
                with eng.Fori(0, S.turns) as i:
                    for n in range(2):
                        S.front_transpose(eng, i, n, pT[n][:, 0:256])
                    for n in range(2):
                        eng.wait_ge(S.xT_ready, S.nth(i, n))
                        for t in range(TILES):
                            ins = eng.matmul(pQ[n][:, t, 0:3 * P], S.xT[n][:, t * P:(t + 1) * P], wqkv[:, :],
                                             start=True, stop=True)
                        ins.then_inc(qkv_in_psum, 1)
                    for n in range(2):
                        eng.wait_ge(qkv_ready, S.nth(i, n))
                        for t in range(TILES):
                            eng.transpose(pT[n][:, t * P:(t + 1) * P], qk[n][:, t, 0:P], core.ident[:, :])
                        for t in range(TILES):
                            ins = eng.matmul(pM[n][:, 0:P], qk[n][:, t, P:2 * P], v[n][:, t, :],
                                             start=(t == 0), stop=(t == TILES - 1))
                        ins.then_inc(kv_in_psum, 1)
                    for n in range(2):
                        eng.wait_ge(kv_ready, S.nth(i, n))
                        eng.wait_ge(qT_ready, S.nth(i, n))
                        eng.matmul(pM[n][:, P:P + SEQ], kv[n][:, :], qT[n][:, :], start=True, stop=True)\
                           .then_inc(oT_in_psum, 1)
                    for n in range(2):
                        eng.wait_ge(oT_ready, S.nth(i, n))
                        for t in range(TILES):
                            ins = eng.matmul(y[n][:, t, :], oT[n][:, t * P:(t + 1) * P], wo[:, :], start=True, stop=True)
                        ins.then_inc(y_in_psum, 1)

            @block.scalar
            def _(eng):
                eng.wait_ge(weights_in, 64)
                eng.activation(v_factor[:, :], norm_const[:, :], ACT.Tanh, scale=0.5).then_inc(factor, 1)
                eng.wait_ge(mask_ready, 1)
                eng.activation(v_factor[:, :], v_factor[:, :], ACT.Exp).then_inc(factor, 1)
                with eng.Fori(0, S.turns) as i:
                    for n in range(2):
                        S.front_copy(eng, i, n, pT[n][:, 0:256])
                    for n in range(2):
                        eng.wait_ge(qkv_in_psum, S.nth(i, n))
                        eng.activation(sq[n][:, :, :], pQ[n][:, :, 0:2 * P], ACT.Square).then_inc(sq_ready, 1)
                    for n in range(2):
                        eng.wait_ge(n2_ready, S.nth(i, n))
                        eng.activation(n2[n][:, :], n2[n][:, :], ACT.Sqrt).then_inc(norm_ready, 1)
                    for n in range(2):
                        eng.wait_ge(kv_in_psum, S.nth(i, n))
                        eng.copy(qT[n][:, :], pT[n][:, 0:SEQ]).then_inc(qT_ready, 1)
                    for n in range(2):
                        eng.wait_ge(oT_in_psum, S.nth(i, n))
                        eng.copy(oT[n][:, :], pM[n][:, P:P + SEQ]).then_inc(oT_ready, 1)
        S.clear_semaphores()


L2_HEADS = 8
L2_HEAD = 64
L2_INNER = L2_HEADS * L2_HEAD
WINDOW = 64


def local_attn_stage(nc, core, W, depth):
    first = depth == 0
    H, D, HALF = L2_HEADS, L2_HEAD, L2_HEAD // 2
    with ExitStack() as ctx:
        S = Stage(nc, ctx, f"l2t{depth}", 2, core, src=None if first else core.Y)
        wqkv = S.sb("wqkv", [P, 3 * L2_INNER])
        wo = S.sb("wo", [P, 4, P])
        cos_f = S.sb("cos_f", [P, TILES, 2, D])
        sin_f = S.sb("sin_f", [P, TILES, 2, D])
        qk_scale = S.sb("qk_scale", [P, 2, D])
        qk_scale_rot = S.sb("qk_scale_rot", [P, 2, D])
        band = S.sb("band", [P, 128 + 192], BF16)
        ident16 = S.sb("ident16", [P, P], BF16)
        sq = [S.sb(f"sq{k}", [P, 2, L2_INNER]) for k in range(2)]
        n2 = [S.sb(f"n2{k}", [P, 2 * H]) for k in range(2)]
        inv = [S.sb(f"inv{k}", [P, 2 * H]) for k in range(2)]
        direct = [S.sb(f"direct{k}", [P, 2, L2_INNER]) for k in range(2)]
        rotated = [S.sb(f"rotated{k}", [P, 2, L2_INNER]) for k in range(2)]
        qkT = [S.sb(f"qkT{k}", [P, 2, 4, SEQ]) for k in range(2)]
        v = [S.sb(f"v{k}", [P, 3, H, D + 1]) for k in range(2)]
        prob = [S.sb(f"prob{k}", [P, 4, 192]) for k in range(2)]
        highest = [S.sb(f"highest{k}", [P, 4]) for k in range(2)]
        probT = [S.sb(f"probT{k}", [P, 2, 4 * P]) for k in range(2)]
        rden = [S.sb(f"rden{k}", [P, H]) for k in range(2)]
        o = [S.sb(f"o{k}", [P, L2_INNER]) for k in range(2)]
        oT = [S.sb(f"oT{k}", [P, 4, P]) for k in range(2)]
        pQ = S.ps("pQ", [P, 2, 512])
        pT = [S.ps(f"pT{k}", [P, 512]) for k in range(2)]
        pS = S.ps("pS", [P, 2, 2, 256])
        pO = S.ps("pO", [P, 2, 512])
        tiles = [(n, t) for n in range(2) for t in range(TILES)]
        units = [(n, t, g) for n, t in tiles for g in range(2)]
        U = len(units)
        (weights_in, tables_ready, qk_in_psum, sq_ready, n2_ready, inv_ready, parts_ready, sum_ready, qk_ready,
         qkT_in_psum, qkT_ready, v_in_psum, v_ready, scores_in_psum, below_ready, prob_ready, probT_in_psum,
         probT_ready, o_in_psum, o_ready, oT_in_psum, oT_ready, y_in_psum) = (S.sem(s) for s in (
             "weights_in", "tables_ready", "qk_in_psum", "sq_ready", "n2_ready", "inv_ready", "parts_ready",
             "sum_ready", "qk_ready", "qkT_in_psum", "qkT_ready", "v_in_psum", "v_ready", "scores_in_psum",
             "below_ready", "prob_ready", "probT_in_psum", "probT_ready", "o_in_psum", "o_ready", "oT_in_psum",
             "oT_ready", "y_in_psum"))

        def heads(ap):
            return ap.rearrange("p a (h s d) -> p (a h) s d", h=H, s=2)

        with nc.Block() as block:
            @block.sync
            def _(eng):
                eng.dma_start(wqkv[:, :], W["L2_ffn_wqkv"][depth]).then_inc(weights_in, 16)
                eng.dma_start(wo[:, :, :], W["L2_ffn_wo"][depth].rearrange("(k p) n -> p k n", p=P)).then_inc(weights_in, 16)
                eng.dma_start(cos_f[:, :, :, :], W["xpos_cos"]).then_inc(weights_in, 16)
                eng.dma_start(sin_f[:, :, :, :], W["xpos_sin"]).then_inc(weights_in, 16)
                eng.dma_start(qk_scale[:, :, :], W["L2_ffn_qk_scale"][depth].partition_broadcast(P)).then_inc(weights_in, 16)
                eng.dma_start(qk_scale_rot[:, :, :], W["L2_ffn_qk_scale_rot"][depth].partition_broadcast(P))\
                   .then_inc(weights_in, 16)
                eng.dma_start(band[:, :], W["band_mask"]).then_inc(weights_in, 16)
                eng.dma_start(ident16[:, :], W["ident16"]).then_inc(weights_in, 16)
                eng.wait_ge(weights_in, 128)

            @block.vector
            def _(eng):
                chain = Chain(eng, S.v_chain)
                for n in range(2):
                    eng.memset(v[n][:, :, :, D:D + 1], 1.0)
                    eng.memset(S.xT[n][64:128, 0:1], 0.0)
                eng.wait_ge(weights_in, 128)
                for t in range(TILES):
                    eng.tensor_tensor(cos_f[:, t, :, :], cos_f[:, t, :, :], qk_scale[:, :, :], ALU.mult)
                    ins = eng.tensor_tensor(sin_f[:, t, :, :], sin_f[:, t, :, :], qk_scale_rot[:, :, :], ALU.mult)
                ins.then_inc(tables_ready, 1)
                eng.wait_ge(tables_ready, 1)

                def outputs(k, eng, i, chain):
                    eng.wait_ge(o_in_psum, i * 4 + (k + 1))
                    o4 = pO[:, :, 0:4 * (D + 1)].rearrange("p b (h d) -> p b h d", h=4)
                    chain.link(eng.reciprocal(rden[k % 2][:, :].rearrange("p (b h) -> p b h", b=2), o4[:, :, :, D]))
                    eng.tensor_tensor(o[k % 2][:, :].rearrange("p (b h d) -> p b h d", b=2, h=4), o4[:, :, :, 0:D],
                                      rden[k % 2][:, :].rearrange("p (b h) -> p b h", b=2).unsqueeze(3)
                                      .to_broadcast([P, 2, 4, D]), ALU.mult).then_inc(o_ready, 1)

                with eng.Fori(0, S.turns) as i:
                    if first:
                        for n in range(2):
                            S.front_stats(eng, chain, i, n)
                        for n in range(2):
                            S.front_apply(eng, i, n)
                    else:
                        for n in range(2):
                            for t in range(TILES):
                                ins = eng.tensor_copy(S.xn[n][:, t, :], S.rows(i, n, t))
                            ins.then_inc(S.xn_ready, 1)

                    def parts(k):
                        n, t = tiles[k]
                        eng.wait_ge(sq_ready, i * 4 + (k + 1))
                        chain.link(eng.tensor_reduce(n2[k % 2][:, :], sq[k % 2][:, :, :].rearrange("p a (h d) -> p (a h) d", h=H),
                                                     AX.X, ALU.add))
                        eng.tensor_scalar(n2[k % 2][:, :], n2[k % 2][:, :], 1e-24, None, ALU.max).then_inc(n2_ready, 1)
                        for a in range(2):
                            q4 = pQ[:, a, :].rearrange("p (h s d) -> p h s d", h=H, s=2)
                            r4 = rotated[k % 2][:, a, :].rearrange("p (h s d) -> p h s d", h=H, s=2)
                            for s in range(2):
                                eng.tensor_tensor(r4[:, :, s, :], q4[:, :, 1 - s, :],
                                                  sin_f[:, t, a, s * HALF:(s + 1) * HALF].unsqueeze(1).to_broadcast([P, H, HALF]),
                                                  ALU.mult)
                            ins = eng.tensor_tensor(direct[k % 2][:, a, :].rearrange("p (h d) -> p h d", h=H),
                                                    pQ[:, a, :].rearrange("p (h d) -> p h d", h=H),
                                                    cos_f[:, t, a, :].unsqueeze(1).to_broadcast([P, H, D]), ALU.mult)
                        ins.then_inc(parts_ready, 1)

                    def normed(k):
                        eng.wait_ge(sum_ready, i * 4 + (k + 1))
                        eng.wait_ge(inv_ready, i * 4 + (k + 1))
                        eng.tensor_tensor(direct[k % 2][:, :, :].rearrange("p a (h d) -> p (a h) d", h=H),
                                          direct[k % 2][:, :, :].rearrange("p a (h d) -> p (a h) d", h=H),
                                          inv[k % 2][:, :].unsqueeze(2).to_broadcast([P, 2 * H, D]), ALU.mult)\
                           .then_inc(qk_ready, 1)

                    parts(0)
                    for k in range(4):
                        if k + 1 < 4:
                            if k + 1 >= 2:
                                eng.wait_ge(qkT_in_psum, (i * 16) + 4 * k)
                            parts(k + 1)
                        normed(k)
                    for u, (n, t, g) in enumerate(units):
                        K = 128 + 64 * t
                        eng.wait_ge(scores_in_psum, i * U + (u + 1))
                        s4 = pS[:, :, :, 0:K].rearrange("p a j k -> p (a j) k")
                        chain.link(eng.tensor_reduce(highest[u % 2][:, :], s4, AX.X, ALU.max))
                        eng.tensor_tensor(prob[u % 2][:, :, 0:K], s4,
                                          highest[u % 2][:, :].unsqueeze(2).to_broadcast([P, 4, K]),
                                          ALU.subtract).then_inc(below_ready, 1)
                        if u % 2 == 0 and u >= 2:
                            outputs(u // 2 - 1, eng, i, chain)
                    outputs(3, eng, i, chain)
                    eng.wait_ge(y_in_psum, i + 1)
                    for k, (n, t) in enumerate(tiles):
                        ins = eng.tensor_tensor(S.of(core.Y, i, n, t), S.xn[n][:, t, :], pQ[:, 1, k * P:(k + 1) * P], ALU.add)
                    chain.link(ins)
                    chain.restart()

            @block.gpsimd
            def _(eng):
                chain = Chain(eng, S.p_chain)
                with eng.Fori(0, S.turns) as i:
                    if first:
                        for n in range(2):
                            S.front_rstd(eng, chain, i, n)
                    for k in range(4):
                        eng.wait_ge(n2_ready, i * 4 + (k + 1))
                        eng.tensor_tensor(inv[k % 2][:, :], n2[k % 2][:, :], core.minus_half[:, 0:2 * H], ALU.pow)\
                           .then_inc(inv_ready, 1)
                        eng.wait_ge(parts_ready, i * 4 + (k + 1))
                        eng.tensor_tensor(direct[k % 2][:, :, :], direct[k % 2][:, :, :], rotated[k % 2][:, :, :],
                                          ALU.add).then_inc(sum_ready, 1)
                    chain.restart()

            @block.tensor
            def _(eng):
                eng.wait_ge(weights_in, 128)
                with eng.Fori(0, S.turns) as i:
                    for n in range(2):
                        S.front_transpose(eng, i, n, pT[n][:, 0:SEQ])

                    def project(k):
                        n, t = tiles[k]
                        if k == 0:
                            eng.wait_ge(S.xT_ready, S.nth(i, 1))
                        if k:
                            eng.wait_ge(parts_ready, i * 4 + k)
                        for a in range(2):
                            ins = eng.matmul(pQ[:, a, :], S.xT[n][:, t * P:(t + 1) * P],
                                             wqkv[:, a * L2_INNER:(a + 1) * L2_INNER], start=True, stop=True)
                        ins.then_inc(qk_in_psum, 1)

                    def values(n):
                        for j, (lo, hi) in enumerate(((0, 128), (64, 128), (128, 256))):
                            c = 3 * n + j
                            if c >= 2:
                                eng.wait_ge(v_ready, i * 6 + (c - 1))
                            eng.matmul(pO[0:hi - lo, c % 2, :], S.xT[n][:, lo:hi], wqkv[:, 2 * L2_INNER:3 * L2_INNER],
                                       start=True, stop=True).then_inc(v_in_psum, 1)

                    def turn_qk(k):
                        eng.wait_ge(qk_ready, i * 4 + (k + 1))
                        for a in range(2):
                            for half in range(2):
                                c = 4 * k + 2 * a + half
                                if c >= 2:
                                    eng.wait_ge(qkT_ready, i * 16 + (c - 1))
                                for j in range(2):
                                    ch = 2 * half + j
                                    ins = eng.transpose(pT[c % 2][:, j * P:(j + 1) * P],
                                                        direct[k % 2][:, a, ch * P:(ch + 1) * P], core.ident[:, :])
                                ins.then_inc(qkT_in_psum, 1)

                    project(0)
                    values(0)
                    project(1)
                    turn_qk(0)
                    project(2)
                    values(1)
                    turn_qk(1)
                    project(3)
                    turn_qk(2)
                    turn_qk(3)
                    eng.wait_ge(qkT_ready, i * 16 + 16)
                    eng.wait_ge(v_ready, i * 6 + 6)

                    def scores(u):
                        n, t, g = units[u]
                        if u:
                            eng.wait_ge(below_ready, i * U + u)
                        lo = 64 * t
                        K = 128 + 64 * t
                        for par in range(2):
                            for j in range(2):
                                h = 4 * g + 2 * j + par
                                rows = slice(64 * par, 64 * par + 64)
                                eng.matmul(pS[:, par, j, 0:K], qkT[n][rows, 0, h // 2, t * P:(t + 1) * P],
                                           qkT[n][rows, 1, h // 2, lo:lo + K], start=(j == 0), stop=True,
                                           skip_group_check=(j != 0))
                        m = band[:, 0:128] if t == 0 else band[:, 128:320]
                        for par in range(2):
                            for j in range(2):
                                ins = eng.matmul(pS[:, par, j, 0:K], ident16[:, :], m, start=False, stop=True,
                                                 skip_group_check=True)
                        ins.then_inc(scores_in_psum, 1)

                    def weigh(u):
                        n, t, g = units[u]
                        eng.wait_ge(prob_ready, i * U + (u + 1))
                        blocks = [(0, 128, 0)] if t == 0 else [(64, 192, 2), (0, 64, 1)]
                        base = 6 * (u // 4) + (0, 1, 2, 4)[u % 4]
                        if base + len(blocks) > 2:
                            eng.wait_ge(probT_ready, i * 12 + (base + len(blocks) - 2))
                        for b, (lo, hi, _) in enumerate(blocks):
                            c = base + b
                            for r in range(4):
                                ins = eng.transpose(pT[c % 2][0:hi - lo, r * P:(r + 1) * P],
                                                    prob[u % 2][:, r, lo:hi], core.ident[:, :])
                            ins.then_inc(probT_in_psum, 1)
                        if g == 0 and u >= 2:
                            eng.wait_ge(o_ready, i * 4 + (u // 2))
                        for b, (lo, hi, kb) in enumerate(blocks):
                            eng.wait_ge(probT_ready, i * 12 + (base + b + 1))
                            for r in range(4):
                                h = 4 * g + 2 * (r % 2) + r // 2
                                hh = 2 * (r % 2) + r // 2
                                ins = eng.matmul(pO[:, g, hh * (D + 1):(hh + 1) * (D + 1)],
                                                 probT[u % 2][0:hi - lo, b, r * P:(r + 1) * P],
                                                 v[n][0:hi - lo, kb, h, :], start=(b == 0 and r == 0), stop=True,
                                                 skip_group_check=not (b == 0 and r == 0))
                        if g == 1:
                            ins.then_inc(o_in_psum, 1)

                    def project_out(k):
                        eng.wait_ge(o_ready, i * 4 + (k + 1))
                        for c in range(4):
                            ins = eng.transpose(pQ[:, 0, c * P:(c + 1) * P], o[k % 2][:, c * P:(c + 1) * P], core.ident[:, :])
                        ins.then_inc(oT_in_psum, 1)
                        eng.wait_ge(oT_ready, i * 4 + (k + 1))
                        for c in range(4):
                            ins = eng.matmul(pQ[:, 1, k * P:(k + 1) * P], oT[k % 2][:, c, :], wo[:, c, :],
                                             start=(c == 0), stop=(c == 3))
                        if k == 3:
                            ins.then_inc(y_in_psum, 1)

                    scores(0)
                    for u in range(U):
                        if u + 1 < U:
                            scores(u + 1)
                        weigh(u)
                        if u % 2 == 0 and u >= 2:
                            project_out(u // 2 - 1)
                    project_out(3)

            @block.scalar
            def _(eng):
                eng.wait_ge(tables_ready, 1)
                with eng.Fori(0, S.turns) as i:
                    for n in range(2):
                        eng.wait_ge(S.xt_in_psum, S.nth(i, n))
                        eng.copy(S.xT[n][0:64, :], pT[n][0:64, 0:SEQ])
                        eng.copy(S.xT[n][64:128, 1:SEQ], pT[n][64:128, 0:SEQ - 1]).then_inc(S.xT_ready, 1)

                    def squares(k):
                        eng.wait_ge(qk_in_psum, i * 4 + (k + 1))
                        eng.activation(sq[k % 2][:, :, :], pQ[:, :, :], ACT.Square).then_inc(sq_ready, 1)

                    def values(n):
                        for j, rows in enumerate((128, 64, 128)):
                            c = 3 * n + j
                            eng.wait_ge(v_in_psum, i * 6 + (c + 1))
                            eng.copy(v[n][0:rows, j, :, 0:D], pO[0:rows, c % 2, :].rearrange("p (h d) -> p h d", h=H))\
                               .then_inc(v_ready, 1)

                    def turned(k):
                        n, t = tiles[k]
                        for a in range(2):
                            for half in range(2):
                                c = 4 * k + 2 * a + half
                                eng.wait_ge(qkT_in_psum, i * 16 + (c + 1))
                                eng.copy(qkT[n][:, a, 2 * half:2 * half + 2, t * P:(t + 1) * P],
                                         pT[c % 2][:, 0:2 * P].rearrange("p (j s) -> p j s", j=2)).then_inc(qkT_ready, 1)

                    squares(0)
                    values(0)
                    squares(1)
                    turned(0)
                    squares(2)
                    values(1)
                    turned(1)
                    squares(3)
                    turned(2)
                    turned(3)

                    def out_turned(k):
                        eng.wait_ge(oT_in_psum, i * 4 + (k + 1))
                        eng.copy(oT[k % 2][:, :, :], pQ[:, 0, :].rearrange("p (c s) -> p c s", c=4)).then_inc(oT_ready, 1)

                    for u, (n, t, g) in enumerate(units):
                        K = 128 + 64 * t
                        eng.wait_ge(below_ready, i * U + (u + 1))
                        eng.activation(prob[u % 2][:, :, 0:K], prob[u % 2][:, :, 0:K], ACT.Exp, scale=8.0)\
                           .then_inc(prob_ready, 1)
                        base = 6 * (u // 4) + (0, 1, 2, 4)[u % 4]
                        for b, rows in enumerate((128,) if t == 0 else (128, 64)):
                            eng.wait_ge(probT_in_psum, i * 12 + (base + b + 1))
                            eng.copy(probT[u % 2][0:rows, b, :], pT[(base + b) % 2][0:rows, :]).then_inc(probT_ready, 1)
                        if u % 2 == 0 and u >= 2:
                            out_turned(u // 2 - 1)
                    out_turned(3)
        S.clear_semaphores()


GLU = 3


def glu_stage(nc, core, W, depth):
    last = depth == 1
    T = 4
    N = T * P
    with ExitStack() as ctx:
        S = Stage(nc, ctx, f"l2g{depth}", 1, core, tiles=T, src=core.Y)
        w1 = S.sb("w1", [P, 2 * GLU * P])
        w2 = S.sb("w2", [P, GLU, P])
        b1 = S.sb("b1", [P, 2 * GLU])
        b2 = S.sb("b2", [P, P])
        ln_g = S.sb("ln_g", [P, 1])
        ln_b = S.sb("ln_b", [P, 1])
        before = S.sb("before", [P, P])
        before_tile = S.sb("before_tile", [P, P])
        gated = [S.sb(f"gated{k}", [P, GLU, N]) for k in range(2)]
        gelu = [S.sb(f"gelu{k}", [P, N]) for k in range(2)]
        pR = S.ps("pR", [P, N])
        pX = S.ps("pX", [P, N])
        pA = [S.ps(f"pA{k}", [P, N]) for k in range(2)]
        pG = [S.ps(f"pG{k}", [P, N]) for k in range(2)]
        pY = S.ps("pY", [P, N])
        rows3 = pR[:, :].rearrange("p (t c) -> p t c", t=T)
        (weights_in, weights_ready, b1_in_psum, rows_in_psum, hidden_in_psum, gelu_ready, gated_ready,
         y_in_psum) = (S.sem(s) for s in ("weights_in", "weights_ready", "b1_in_psum", "rows_in_psum",
                                          "hidden_in_psum", "gelu_ready", "gated_ready", "y_in_psum"))
        with nc.Block() as block:
            @block.sync
            def _(eng):
                eng.dma_start(w1[:, :], W["L2_ffn_w1"][depth]).then_inc(weights_in, 16)
                eng.dma_start(w2[:, :, :], W["L2_ffn_w2"][depth].rearrange("(k p) n -> p k n", p=P)).then_inc(weights_in, 16)
                eng.dma_start(b1[:, :], W["L2_ffn_b1"][depth]).then_inc(weights_in, 16)
                eng.dma_start(b2[:, :], W["L2_ffn_b2"][depth].partition_broadcast(P)).then_inc(weights_in, 16)
                eng.dma_start(ln_g[:, :], W["L2_ffn_ln_g"][depth]).then_inc(weights_in, 16)
                eng.dma_start(ln_b[:, :], W["L2_ffn_ln_b"][depth]).then_inc(weights_in, 16)
                eng.dma_start(before[:, :], W["row_before"]).then_inc(weights_in, 16)
                eng.dma_start(before_tile[:, :], W["row_before_tile"]).then_inc(weights_in, 16)
                eng.wait_ge(weights_in, 128)

            @block.vector
            def _(eng):
                chain = Chain(eng, S.v_chain)
                eng.wait_ge(weights_in, 128)
                eng.wait_ge(b1_in_psum, 1)
                eng.tensor_tensor(b1[:, :], b1[:, :], pY[:, 0:2 * GLU], ALU.add)
                eng.tensor_scalar(w1[:, :], w1[:, :], ln_g[:, 0:1], None, ALU.mult).then_inc(weights_ready, 1)
                eng.wait_ge(weights_ready, 1)

                def front(i):
                    eng.wait_ge(rows_in_psum, i + 1)
                    for t in range(T):
                        ins = eng.bn_stats(S.stats[:, 0, t, :], rows3[:, t, :])
                    chain.link(ins)
                    for t in range(T):
                        ins = eng.bn_aggr(S.mv[:, 0, t, :], S.stats[:, 0, t, :])
                    ins.then_inc(S.mv_ready, 1)
                    eng.wait_ge(S.rstd_ready, i + 1)
                    for t in range(T):
                        ins = eng.tensor_scalar(S.xn[0][:, t, :], rows3[:, t, :], S.mv[:, 0, t, 0:1],
                                                S.rstd[:, 0, t:t + 1], ALU.subtract, ALU.mult)
                    ins.then_inc(S.xn_ready, 1)

                def turn(i, between):
                    for c in range(GLU):
                        eng.wait_ge(gelu_ready, i * GLU + (c + 1))
                        eng.scalar_tensor_tensor(out=gated[0][:, c, :], in0=pA[c % 2][:, :], scalar=b1[:, c:c + 1],
                                                 in1=gelu[c % 2][:, :], op0=ALU.add, op1=ALU.mult).then_inc(gated_ready, 1)
                    between()
                    r = S.r[0]
                    eng.wait_ge(y_in_psum, i + 1)
                    chain.link(eng.tensor_tensor(r[:, :, :], pY[:, :].rearrange("p (t c) -> p t c", t=T),
                                                 b2[:, :].unsqueeze(1).to_broadcast([P, T, P]), ALU.add))
                    for t in range(T):
                        out = r[:, t, :] if last else S.of(core.Y, i, 0, t)
                        ins = eng.tensor_tensor(out, r[:, t, :], S.rows(i, 0, t), ALU.add)
                    chain.link(ins)
                    if last:
                        S.back_norm_stats(eng, chain, 0, r)
                        S.back_residual(eng, chain, i, 0, r)
                    chain.restart()

                front(0)
                chain.restart()
                with eng.Fori(0, S.turns - 1) as i:
                    turn(i, lambda: front(i + 1))
                turn(S.turns - 1, lambda: None)

            @block.gpsimd
            def _(eng):
                chain = Chain(eng, S.p_chain)

                def turn(i, between):
                    between()
                    if last:
                        S.back_rstd_step(eng, chain, i, 0)
                    chain.restart()

                S.front_rstd(eng, chain, 0, 0)
                chain.restart()
                with eng.Fori(0, S.turns - 1) as i:
                    turn(i, lambda: S.front_rstd(eng, chain, i + 1, 0))
                turn(S.turns - 1, lambda: None)

            @block.tensor
            def _(eng):
                eng.wait_ge(weights_in, 128)
                for c in range(2 * GLU):
                    ins = eng.matmul(pY[:, c:c + 1], w1[:, c * P:(c + 1) * P], ln_b[:, :], start=True, stop=True)
                ins.then_inc(b1_in_psum, 1)
                eng.wait_ge(weights_ready, 1)

                def shift(i):
                    for t in range(T):
                        x = S.rows(i, 0, t)
                        eng.matmul(rows3[:, t, 0:64], core.ident[:, :], x[:, 0:64], start=(t == 0), stop=True,
                                   skip_group_check=(t != 0))
                        ins = eng.matmul(rows3[:, t, 64:P], before[:, :], x[:, 64:P], start=False, stop=True,
                                         skip_group_check=True)
                        if t % TILES:
                            ins = eng.matmul(rows3[:, t, 64:P], before_tile[:, :], S.rows(i, 0, t - 1)[:, 64:P],
                                             start=False, stop=True, skip_group_check=True)
                    ins.then_inc(rows_in_psum, 1)

                def turn(i, between):
                    S.front_transpose(eng, i, 0, pX)
                    eng.wait_ge(S.xT_ready, i + 1)
                    for c in range(GLU):
                        if c >= 2:
                            eng.wait_ge(gated_ready, i * GLU + (c - 1))
                        eng.matmul(pG[c % 2][:, :], w1[:, (GLU + c) * P:(GLU + c + 1) * P], S.xT[0][:, :], start=True, stop=True)
                        eng.matmul(pA[c % 2][:, :], w1[:, c * P:(c + 1) * P], S.xT[0][:, :], start=True, stop=True)\
                           .then_inc(hidden_in_psum, 1)
                    between()
                    eng.wait_ge(gated_ready, i * GLU + GLU)
                    for t in range(T):
                        for c in range(GLU):
                            ins = eng.matmul(pY[:, t * P:(t + 1) * P], gated[0][:, c, t * P:(t + 1) * P], w2[:, c, :],
                                             start=(c == 0), stop=(c == GLU - 1))
                    ins.then_inc(y_in_psum, 1)

                shift(0)
                with eng.Fori(0, S.turns - 1) as i:
                    turn(i, lambda: shift(i + 1))
                turn(S.turns - 1, lambda: None)

            @block.scalar
            def _(eng):
                eng.wait_ge(weights_ready, 1)
                with eng.Fori(0, S.turns) as i:
                    S.front_copy(eng, i, 0, pX[:, :])
                    for c in range(GLU):
                        eng.wait_ge(hidden_in_psum, i * GLU + (c + 1))
                        eng.activation(gelu[c % 2][:, :], pG[c % 2][:, :], ACT.Gelu, bias=b1[:, GLU + c:GLU + c + 1])\
                           .then_inc(gelu_ready, 1)
        S.clear_semaphores()


def local_stage(nc, core, W):
    with ExitStack() as ctx:
        inner_rows(nc, ctx, core, "l2f_rows")
        for depth in range(2):
            local_attn_stage(nc, core, W, depth)
            glu_stage(nc, core, W, depth)


def dense_ffn_stage(nc, core, W):
    FC = 4
    with ExitStack() as ctx:
        S = Stage(nc, ctx, "l3f", 2, core)
        w1 = S.sb("w1", [P, FC * P])
        b1 = S.sb("b1", [P, FC])
        w2 = S.sb("w2", [P, FC, P])
        b2 = S.sb("b2", [P, P])
        hT = [S.sb(f"hT{k}", [P, FC, SEQ]) for k in range(2)]
        pT = [S.ps(f"pT{k}", [P, 512]) for k in range(2)]
        pH = [S.ps(f"pH{k}", [P, FC * SEQ]) for k in range(2)]
        weights_in, h_in_psum, h_ready, y_in_psum = (S.sem(n) for n in ("weights_in", "h_in_psum", "h_ready", "y_in_psum"))
        with nc.Block() as block:
            @block.sync
            def _(eng):
                eng.dma_start(w1[:, :], W["L3_ffn_w1"]).then_inc(weights_in, 16)
                eng.dma_start(b1[:, :], W["L3_ffn_b1"]).then_inc(weights_in, 16)
                eng.dma_start(w2[:, :, :], W["L3_ffn_w2"].rearrange("(k p) n -> p k n", p=P)).then_inc(weights_in, 16)
                eng.dma_start(b2[:, :], W["L3_ffn_b2"].partition_broadcast(P)).then_inc(weights_in, 16)
                eng.wait_ge(weights_in, 64)

            @block.vector
            def _(eng):
                chain = Chain(eng, S.v_chain)
                eng.wait_ge(weights_in, 64)
                with eng.Fori(0, S.turns) as i:
                    for n in range(2):
                        S.front_stats(eng, chain, i, n)
                    for n in range(2):
                        S.front_apply(eng, i, n)
                    for n in range(2):
                        eng.wait_ge(y_in_psum, S.nth(i, n))
                        for t in range(TILES):
                            ins = eng.tensor_tensor(S.r[n][:, t, :], pT[n][:, 256 + t * P:256 + (t + 1) * P], b2[:, :], ALU.add)
                        chain.link(ins)
                        S.back_norm_stats(eng, chain, n, S.r[n])
                    for n in range(2):
                        S.back_residual(eng, chain, i, n, S.r[n])
                    chain.restart()

            @block.gpsimd
            def _(eng):
                chain = Chain(eng, S.p_chain)
                with eng.Fori(0, S.turns) as i:
                    for n in range(2):
                        S.front_rstd(eng, chain, i, n)
                    for n in range(2):
                        S.back_rstd_step(eng, chain, i, n)
                    chain.restart()

            @block.tensor
            def _(eng):
                eng.wait_ge(weights_in, 64)
                with eng.Fori(0, S.turns) as i:
                    for n in range(2):
                        S.front_transpose(eng, i, n, pT[n][:, 0:256])
                    for n in range(2):
                        eng.wait_ge(S.xT_ready, S.nth(i, n))
                        for c in range(FC):
                            ins = eng.matmul(pH[n][:, c * SEQ:(c + 1) * SEQ], w1[:, c * P:(c + 1) * P], S.xT[n][:, :],
                                             start=True, stop=True)
                        ins.then_inc(h_in_psum, 1)
                    for n in range(2):
                        eng.wait_ge(h_ready, S.nth(i, n))
                        for t in range(TILES):
                            for c in range(FC):
                                ins = eng.matmul(pT[n][:, 256 + t * P:256 + (t + 1) * P], hT[n][:, c, t * P:(t + 1) * P],
                                                 w2[:, c, :], start=(c == 0), stop=(c == FC - 1))
                        ins.then_inc(y_in_psum, 1)

            @block.scalar
            def _(eng):
                eng.wait_ge(weights_in, 64)
                with eng.Fori(0, S.turns) as i:
                    for n in range(2):
                        S.front_copy(eng, i, n, pT[n][:, 0:256])
                    for n in range(2):
                        eng.wait_ge(h_in_psum, S.nth(i, n))
                        for c in range(FC):
                            ins = eng.activation(hT[n][:, c, :], pH[n][:, c * SEQ:(c + 1) * SEQ], ACT.Gelu,
                                                 bias=b1[:, c:c + 1])
                        ins.then_inc(h_ready, 1)
        S.clear_semaphores()


STAGES = {"l0a": mamba_stage, "l0f": routed_block_stage, "l1a": bond_attn_stage, "l1f": expert_ffn_stage,
          "l2a": linear_attn_stage, "l2f": local_stage, "l3a": alibi_attn_stage, "l3f": dense_ffn_stage}
ORDER = ["l0a", "l0f", "l1a", "l1f", "l2a", "l2f", "l3a", "l3f"]


def program(nc, x, W, out, n_seq, stages):
    with ExitStack() as ctx:
        core = Core(nc, ctx, n_seq)
        load_stage(nc, core, x)
        for s in stages:
            STAGES[s](nc, core, W)
        store_stage(nc, core, out)


def layout(inputs):
    import numpy as np
    a = {k: np.asarray(v) for k, v in inputs.items()}
    w = {}
    for n in ("w1", "w2", "b2"):
        w[f"L3_ffn_{n}"] = a[f"L3_ffn_{n}"]
    two = lambda m: m.reshape(2, 128, -1).transpose(1, 0, 2)
    w["L0_attn_in_proj"] = a["L0_attn_in_proj_w"].T
    w["L0_attn_conv_w"] = a["L0_attn_conv_w"].transpose(1, 2, 0).reshape(2, 128, 4, 256).transpose(1, 0, 2, 3)
    w["L0_attn_dt_w"] = two(a["L0_attn_dt_w"].T)
    bc = np.concatenate([a["L0_attn_B_w"], a["L0_attn_C_w"]]).T
    w["L0_attn_bc_w"] = two(np.concatenate([bc, np.zeros_like(bc), bc, bc], axis=1))
    w["L0_attn_out_w"] = two(a["L0_attn_out_w"].T)
    for n in ("conv_b", "dt_b", "D"):
        w[f"L0_attn_{n}"] = a[f"L0_attn_{n}"].reshape(2, 128).T
    w["L0_attn_A_log"] = two(a["L0_attn_A_log"])
    pick = np.zeros((128, 32, 128), np.float32)
    for part in (0, 64, 96):
        for n in range(32):
            pick[part + n, n, :] = 1.0
    w["bc_pick"] = pick.astype(mybir.dt.np(BF16))
    w["L3_ffn_b1"] = a["L3_ffn_b1"].reshape(4, 128).T
    w["L2_attn_Wqkv"] = np.concatenate([a[f"L2_attn_W{n}"].T for n in "qkv"], axis=1)
    w["L2_attn_Wo"] = a["L2_attn_Wo"].T
    w["L2_attn_norm_const"] = np.repeat(a["L2_attn_norm_const"].reshape(16), 8)
    head = np.arange(128) // 8
    w["same_head"] = (head[:, None] == head[None, :]).astype(np.float32)
    for n in ("router_W", "router_b", "W1", "b2"):
        w[f"L1_ffn_{n}"] = a[f"L1_ffn_{n}"]
    w["L1_ffn_W2"] = a["L1_ffn_W2"].reshape(-1, 128)
    w["L1_ffn_b1"] = a["L1_ffn_b1"].reshape(32, 128).T
    w["L1_ffn_ln_g"] = a["L1_ffn_ln_g"].T
    w["L1_ffn_ln_b"] = a["L1_ffn_ln_b"].T
    w["expert_index"] = np.arange(8, dtype=np.float32)
    w["expert_zero"] = np.zeros(8, np.float32)
    for n in ("router_w", "w1", "w2"):
        w[f"L0_ffn_{n}"] = a[f"L0_ffn_{n}"]
    w["L0_ffn_ln2_w"] = np.repeat(a["L0_ffn_ln2_w"][:, None], 8, axis=1)

    def spread(m):
        o = np.zeros((128, 4, 4, 32), np.float32)
        o[:, :, :, 0:8] = m.reshape(128, 4, 4, 8)
        return o.reshape(128, 4, 128)

    c_attn = a["L0_ffn_c_attn_w"]
    w["L0_ffn_wq"], w["L0_ffn_wk"], w["L0_ffn_wv"] = spread(c_attn[:, 0:128]), spread(c_attn[:, 128:256]), c_attn[:, 256:]
    w["L0_ffn_wo"] = a["L0_ffn_c_proj_w"]
    w["L0_ffn_ln1_w"] = a["L0_ffn_ln1_w"][:, None]
    kqv = a["L3_attn_W_kqv"].T
    w["L3_attn_wk"], w["L3_attn_wq"], w["L3_attn_wv"] = spread(kqv[:, 0:128]), spread(kqv[:, 128:256]), kqv[:, 256:]
    slopes = np.array([1.0 / (2.0 ** 8) ** ((h + 1) / 16.0) for h in range(16)]) * 128.0 ** 0.5
    at = np.arange(256)
    bq, bk = np.zeros((4, 32, 4, 256)), np.zeros((4, 32, 4, 256))
    for h in range(16):
        bq[h % 4, 8, h // 4], bk[h % 4, 8, h // 4] = 1.0, slopes[h] * at
        bq[h % 4, 9, h // 4], bk[h % 4, 9, h // 4] = -slopes[h] * at, 1.0
    w["alibi_q"], w["alibi_k"] = (b.reshape(128, 4, 256).astype(np.float32) for b in (bq, bk))
    row = np.arange(128)
    bf16 = mybir.dt.np(BF16)
    w["L2_ffn_wqkv"] = a["L2_ffn_wqkv"]
    w["L2_ffn_wo"] = a["L2_ffn_wo"]
    qs = np.stack([a["L2_ffn_q_scale"], a["L2_ffn_k_scale"]], axis=1)
    w["L2_ffn_qk_scale"] = qs
    w["L2_ffn_qk_scale_rot"] = np.roll(qs, 32, axis=-1)
    half = np.arange(0, 64, 2)
    angle = at[:, None] / 10000.0 ** (half / 64.0)[None, :]
    power = (at - 128) / 32.0
    xscale = ((half + 25.6) / 89.6)[None, :] ** power[:, None]
    both = lambda m: np.concatenate([m, m], axis=1)
    sign = np.where(np.arange(64) < 32, -1.0, 1.0)[None, :]
    cos = np.stack([both(np.cos(angle) * xscale), both(np.cos(angle) / xscale)], axis=1)
    sin = np.stack([both(np.sin(angle) * xscale) * sign, both(np.sin(angle) / xscale) * sign], axis=1)
    w["xpos_cos"], w["xpos_sin"] = (m.reshape(2, 128, 2, 64).transpose(1, 0, 2, 3).astype(np.float32) for m in (cos, sin))
    gap0 = row[:, None] - row[None, :]
    gap1 = row[:, None] + 64 - np.arange(192)[None, :]
    band = np.concatenate([gap0, gap1], axis=1)
    w["band_mask"] = np.where((band < 0) | (band > 64), -1e30, 0.0).astype(bf16)
    pad = lambda m, axis: np.concatenate([m, np.zeros(m.shape[:axis] + (43,) + m.shape[axis + 1:], np.float32)], axis=axis)
    w1 = a["L2_ffn_w1"]
    w["L2_ffn_w1"] = np.concatenate([pad(w1[:, :, :341], 2), pad(w1[:, :, 341:], 2)], axis=2)
    b1 = a["L2_ffn_b1"]
    w["L2_ffn_b1"] = np.concatenate([pad(b1[:, :341], 1), pad(b1[:, 341:], 1)], axis=1).reshape(2, 6, 128).transpose(0, 2, 1)
    w["L2_ffn_w2"] = pad(a["L2_ffn_w2"], 1)
    w["L2_ffn_b2"] = a["L2_ffn_b2"]
    w["L2_ffn_ln_g"] = a["L2_ffn_ln_g"][:, :, None]
    w["L2_ffn_ln_b"] = a["L2_ffn_ln_b"][:, :, None]
    w["row_before"] = np.eye(128, k=1, dtype=np.float32)
    corner = np.zeros((128, 128), np.float32)
    corner[127, 0] = 1.0
    w["row_before_tile"] = corner
    w["causal_mask"] = np.where(row[None, :] > row[:, None], -1e30, 0.0).astype(bf16)
    w["ident16"] = np.eye(128).astype(bf16)
    for n in ("w_disp", "w_val", "w_cproj", "b_val", "b_cproj", "b_bond_out"):
        w[f"L1_attn_{n}"] = a[f"L1_attn_{n}"]

    def per_head(m):
        o = np.zeros((8, 16, 8, 16), np.float32)
        for h in range(8):
            o[h, :, h, :] = m
        return o.reshape(128, 128)

    def out_columns(v):
        o = np.zeros((8, 16, 16, 8, 16), np.float32)
        for h in range(8):
            for k in range(16):
                o[h, :, k, h, k] = v[:, 0]
        return o.reshape(128, 16, 128)

    small = [a[f"L1_attn_w_{n}"] for n in ("state", "strain", "state_i", "state_j", "damage", "strain")]
    w["L1_attn_w_small"] = np.stack([per_head(m) for m in small], axis=1)
    w["L1_attn_w_bond"] = out_columns(a["L1_attn_w_bond_out"])
    w["L1_attn_w_damage_out"] = out_columns(a["L1_attn_w_damage_out"])
    heads8 = lambda v: np.tile(v, 8)
    w["L1_attn_biases"] = np.stack([a["L1_attn_b_disp"][:128], a["L1_attn_b_disp"][128:], heads8(a["L1_attn_b_state"]),
                                    heads8(a["L1_attn_b_strain"]), heads8(a["L1_attn_b_damage"]),
                                    np.repeat(a["L1_attn_b_damage_out"], 128)], axis=1)
    w["L1_attn_w_pos"] = np.tile(a["L1_attn_w_pos"], (1, 8))
    w["L1_attn_rel_emb"] = a["L1_attn_rel_pos_emb"].T
    key = at[:, None] - 31 + np.arange(32)[None, :]
    w["L1_attn_mask"] = np.where(key < 0, -1e30, 0.0).reshape(2, 128, 32).transpose(1, 0, 2).astype(np.float32)
    gap = at[None, :] - at[:, None]
    mean = ((gap >= 0) & (gap < 32)) / np.minimum(at + 1, 32)[None, :]
    w["L1_attn_mean_w"] = mean.reshape(2, 128, 256).transpose(1, 0, 2).astype(np.float32)
    return a["L0_attn_x"].reshape(-1, 128), {k: np.ascontiguousarray(v) for k, v in w.items()}


def kernel(**inputs):
    import numpy as np
    import concourse.bacc as bacc
    from concourse.bass_utils import run_bass_kernel_spmd

    x, w = layout(inputs)
    nc = bacc.Bacc("TRN2", target_bir_lowering=False, num_devices=1)
    arrays = {"x": np.ascontiguousarray(x), **w}
    aps = {n: nc.dram_tensor(n, a.shape, mybir.dt.from_np(a.dtype), kind="ExternalInput").ap() for n, a in arrays.items()}
    out = nc.dram_tensor("out", x.shape, F32, kind="ExternalOutput").ap()
    program(nc, aps["x"], aps, out, 32, ORDER)
    r = run_bass_kernel_spmd(nc, [arrays], core_ids=[0])
    return r.results[0]["out"].reshape(32, SEQ, P)
```

```python
from contextlib import ExitStack

import concourse.bass as bass
from concourse import mybir

F32 = mybir.dt.float32
BF16 = mybir.dt.bfloat16
ALU = mybir.AluOpType
ACT = mybir.ActivationFunctionType
AX = mybir.AxisListType

P = 128
SEQ = 256
TILES = SEQ // P
EPS = 1e-5


class Chain:

    def __init__(self, eng, sem):
        self.eng, self.sem, self.n = eng, sem, 0

    def link(self, ins):
        self.n += 1
        ins.then_inc(self.sem, 1)
        self.eng.wait_ge(self.sem, self.n)

    def restart(self):
        if self.n:
            self.eng.sem_clear(self.sem)
        self.n = 0


class Stage:

    def __init__(self, nc, ctx, name, lanes, core, tiles=2, src=None):
        self.nc, self.ctx, self.name, self.lanes, self.core = nc, ctx, name, lanes, core
        self.tiles = tiles
        self.sems = []
        self.turns = core.n_seq * TILES // (lanes * tiles)
        self.src = core.X if src is None else src
        self.mv_ready = self.sem("mv_ready")
        self.rstd_ready = self.sem("rstd_ready")
        self.xn_ready = self.sem("xn_ready")
        self.xt_in_psum = self.sem("xt_in_psum")
        self.xT_ready = self.sem("xT_ready")
        self.back_mv_ready = self.sem("back_mv_ready")
        self.back_rstd_ready = self.sem("back_rstd_ready")
        self.v_chain = self.sem("v_chain")
        self.a_chain = self.sem("a_chain")
        self.p_chain = self.sem("p_chain")
        self.stats = self.sb("stats", [P, lanes, tiles, 6])
        self.mv = self.sb("mv", [P, lanes, tiles, 2])
        self.rstd = self.sb("rstd", [P, lanes, tiles])
        self.back_stats = self.sb("back_stats", [P, lanes, tiles, 6])
        self.back_mv = self.sb("back_mv", [P, lanes, tiles, 2])
        self.back_rstd = self.sb("back_rstd", [P, lanes, tiles])
        self.xn = [self.sb(f"xn{k}", [P, tiles, P]) for k in range(lanes)]
        self.xT = [self.sb(f"xT{k}", [P, tiles * P]) for k in range(lanes)]
        self.r = [self.sb(f"r{k}", [P, tiles, P]) for k in range(lanes)]

    def sem(self, name):
        self.sems.append(self.ctx.enter_context(self.nc.semaphore(f"{self.name}_{name}")))
        return self.sems[-1]

    def clear_semaphores(self):
        with self.nc.Block() as block:
            @block.vector
            def _(eng):
                for sem in self.sems[0::3]:
                    eng.sem_clear(sem)

            @block.scalar
            def _(eng):
                for sem in self.sems[1::3]:
                    eng.sem_clear(sem)

            @block.gpsimd
            def _(eng):
                for sem in self.sems[2::3]:
                    eng.sem_clear(sem)

    def sb(self, name, shape, dt=F32):
        return self.ctx.enter_context(self.nc.sbuf_tensor(f"{self.name}_{name}", shape, dt))

    def ps(self, name, shape, dt=F32):
        return self.ctx.enter_context(self.nc.psum_tensor(f"{self.name}_{name}", shape, dt))

    def nth(self, i, lane, per=1, k=0):
        return i * (self.lanes * per) + (lane * per + k + 1)

    def rows(self, i, lane, tile):
        return self.of(self.src, i, lane, tile)

    def of(self, rows, i, lane, tile):
        return rows[:, i * (self.lanes * self.tiles) + (lane * self.tiles + tile), :]

    def front_stats(self, eng, chain, i, lane):
        for t in range(self.tiles):
            ins = eng.bn_stats(self.stats[:, lane, t, :], self.rows(i, lane, t))
        chain.link(ins)
        for t in range(self.tiles):
            ins = eng.bn_aggr(self.mv[:, lane, t, :], self.stats[:, lane, t, :])
        ins.then_inc(self.mv_ready, 1)

    def front_apply(self, eng, i, lane):
        eng.wait_ge(self.rstd_ready, self.nth(i, lane))
        for t in range(self.tiles):
            ins = eng.tensor_scalar(self.xn[lane][:, t, :], self.rows(i, lane, t), self.mv[:, lane, t, 0:1],
                                    self.rstd[:, lane, t:t + 1], ALU.subtract, ALU.mult)
        ins.then_inc(self.xn_ready, 1)

    def back_norm_stats(self, eng, chain, lane, src):
        for t in range(self.tiles):
            ins = eng.bn_stats(self.back_stats[:, lane, t, :], src[:, t, :])
        chain.link(ins)
        for t in range(self.tiles):
            ins = eng.bn_aggr(self.back_mv[:, lane, t, :], self.back_stats[:, lane, t, :])
        ins.then_inc(self.back_mv_ready, 1)

    def back_residual(self, eng, chain, i, lane, src):
        eng.wait_ge(self.back_rstd_ready, self.nth(i, lane))
        for t in range(self.tiles):
            ins = eng.tensor_scalar(self.r[lane][:, t, :], src[:, t, :],
                                    self.back_mv[:, lane, t, 0:1], self.back_rstd[:, lane, t:t + 1],
                                    ALU.subtract, ALU.mult)
        chain.link(ins)
        for t in range(self.tiles):
            x = self.of(self.core.X, i, lane, t)
            ins = eng.tensor_tensor(x, x, self.r[lane][:, t, :], ALU.add)
        chain.link(ins)

    def power(self, eng, chain, out, var, eps):
        n = out.shape[1]
        chain.link(eng.tensor_tensor(out, var, eps[:, 0:n], ALU.add))
        return eng.tensor_tensor(out, out, self.core.minus_half[:, 0:n], ALU.pow)

    def front_rstd(self, eng, chain, i, lane):
        eng.wait_ge(self.mv_ready, self.nth(i, lane))
        self.power(eng, chain, self.rstd[:, lane, :], self.mv[:, lane, :, 1], self.core.eps).then_inc(self.rstd_ready, 1)

    def back_rstd_step(self, eng, chain, i, lane):
        eng.wait_ge(self.back_mv_ready, self.nth(i, lane))
        self.power(eng, chain, self.back_rstd[:, lane, :], self.back_mv[:, lane, :, 1], self.core.eps)\
            .then_inc(self.back_rstd_ready, 1)

    def transpose_rows(self, eng, i, lane, out, src, ready, done):
        eng.wait_ge(ready, self.nth(i, lane))
        for t in range(self.tiles):
            ins = eng.transpose(out[:, t * P:(t + 1) * P], src[:, t, :], self.core.ident[:, :])
        ins.then_inc(done, 1)

    def front_transpose(self, eng, i, lane, out):
        self.transpose_rows(eng, i, lane, out, self.xn[lane], self.xn_ready, self.xt_in_psum)

    def front_copy(self, eng, i, lane, src):
        eng.wait_ge(self.xt_in_psum, self.nth(i, lane))
        eng.copy(self.xT[lane][:, :], src).then_inc(self.xT_ready, 1)


class Core:

    def __init__(self, nc, ctx, n_seq):
        self.n_seq = n_seq
        self.X = ctx.enter_context(nc.sbuf_tensor("rows", [P, n_seq * TILES, P], F32))
        self.ident = ctx.enter_context(nc.sbuf_tensor("ident", [P, P], F32))
        self.eps = ctx.enter_context(nc.sbuf_tensor("eps", [P, 8], F32))
        self.e = ctx.enter_context(nc.sbuf_tensor("e", [P, 64], F32))
        self.minus_half = ctx.enter_context(nc.sbuf_tensor("minus_half", [P, 64], F32))


def inner_rows(nc, ctx, core, name):
    core.Y = ctx.enter_context(nc.sbuf_tensor(name, [P, core.n_seq * TILES, P], F32))


def load_stage(nc, core, x):
    with ExitStack() as ctx:
        x_loaded = ctx.enter_context(nc.semaphore("x_loaded"))
        zeroed = ctx.enter_context(nc.semaphore("zeroed"))
        with nc.Block() as block:
            @block.sync
            def _(eng):
                eng.dma_start(core.X[:, :, :], x.rearrange("(n p) c -> p n c", p=P)).then_inc(x_loaded, 16)
                eng.wait_ge(x_loaded, 16)

            @block.gpsimd
            def _(eng):
                eng.memset(core.minus_half[:, :], -0.5).then_inc(zeroed, 1)
                eng.memset(core.eps[:, :], EPS).then_inc(zeroed, 1)
                eng.memset(core.e[:, :], 2.718281828459045).then_inc(zeroed, 1)
                eng.memset(core.ident[:, :], 0.0).then_inc(zeroed, 1)
                eng.wait_ge(zeroed, 4)
                eng.affine_select(out=core.ident[:, :], in_=core.ident[:, :], compare_op=ALU.not_equal, fill=1.0,
                                  base=0, pattern=[[-1, P]], channel_multiplier=1).then_inc(zeroed, 1)
                eng.wait_ge(zeroed, 5)

        with nc.Block() as block:
            @block.gpsimd
            def _(eng):
                eng.sem_clear(x_loaded)
                eng.sem_clear(zeroed)


def store_stage(nc, core, out):
    with ExitStack() as ctx:
        stored = ctx.enter_context(nc.semaphore("stored"))
        with nc.Block() as block:
            @block.sync
            def _(eng):
                eng.dma_start(out.rearrange("(n p) c -> p n c", p=P), core.X[:, :, :]).then_inc(stored, 16)
                eng.wait_ge(stored, 16)


def mamba_stage(nc, core, W):
    D_IN, STATES, TAPS = 256, 16, 4
    HALVES = D_IN // P
    GROUP = 4
    U = HALVES * STATES // GROUP
    LANES = 2
    with ExitStack() as ctx:
        S = Stage(nc, ctx, "l0a", LANES, core)
        w_in = S.sb("w_in", [P, 2 * D_IN])
        w_conv = S.sb("w_conv", [P, HALVES, TAPS, D_IN])
        w_dt = S.sb("w_dt", [P, HALVES, D_IN])
        w_bc = S.sb("w_bc", [P, HALVES, P])
        w_out = S.sb("w_out", [P, HALVES, P])
        pick = S.sb("pick", [P, 2 * STATES, P], BF16)
        conv_b = S.sb("conv_b", [P, HALVES])
        dt_b = S.sb("dt_b", [P, HALVES])
        skip = S.sb("skip", [P, HALVES])
        a_neg = S.sb("a_neg", [P, HALVES, STATES])
        tiny = S.sb("tiny", [P, 1])
        xc = [S.sb(f"xc{n}", [P, HALVES, TAPS - 1 + SEQ]) for n in range(LANES)]
        z_tanh = [S.sb(f"z_tanh{n}", [P, HALVES, SEQ]) for n in range(LANES)]
        z_gate = [S.sb(f"z_gate{n}", [P, HALVES, SEQ]) for n in range(LANES)]
        u_in = [S.sb(f"u{n}", [P, HALVES, SEQ]) for n in range(LANES)]
        dt = [S.sb(f"dt{n}", [P, HALVES, SEQ]) for n in range(LANES)]
        dtu = [S.sb(f"dtu{n}", [P, HALVES, SEQ]) for n in range(LANES)]
        bc = [S.sb(f"bc{n}", [P, SEQ], BF16) for n in range(LANES)]
        bc_rest = S.sb("bc_rest", [P, SEQ])
        y = [S.sb(f"y{n}", [P, HALVES, SEQ]) for n in range(LANES)]
        dta = [S.sb(f"dta{k}", [P, GROUP, SEQ]) for k in range(2)]
        decay = [S.sb(f"decay{k}", [P, GROUP, SEQ]) for k in range(2)]
        drive = [S.sb(f"drive{k}", [P, GROUP, SEQ]) for k in range(2)]
        state = [S.sb(f"state{k}", [P, GROUP, SEQ]) for k in range(2)]
        prod = [S.sb(f"prod{k}", [P, GROUP, SEQ]) for k in range(2)]
        pB = S.ps("pB", [P, GROUP, SEQ])
        pC = S.ps("pC", [P, GROUP, SEQ])
        pY = S.ps("pY", [P, HALVES, SEQ])
        p1 = S.ps("p1", [P, HALVES, SEQ])
        p2 = S.ps("p2", [P, HALVES, SEQ])
        pO = S.ps("pO", [P, 2, SEQ])
        out_rows = pO[:, 1, :].rearrange("p (t c) -> p t c", t=TILES)
        (weights_in, a_ready, const_ready, xc_in_psum, xc_ready, z_in_psum, z_tanh_ready, z_gate_ready,
         u_in_psum, u_ready, dt_in_psum, dt_tanh_ready, bc_in_psum, lane_ready, dta_ready, decay_ready,
         b_in_psum, drive_ready, drive_done, c_in_psum, prod_ready, y_in_psum, y_ready, out_in_psum) = (
             S.sem(s) for s in (
                 "weights_in", "a_ready", "const_ready", "xc_in_psum", "xc_ready", "z_in_psum", "z_tanh_ready",
                 "z_gate_ready", "u_in_psum", "u_ready", "dt_in_psum", "dt_tanh_ready", "bc_in_psum", "lane_ready",
                 "dta_ready", "decay_ready", "b_in_psum", "drive_ready", "drive_done", "c_in_psum", "prod_ready",
                 "y_in_psum", "y_ready", "out_in_psum"))
        N_LOADS = 10

        def unit(w):
            return w // U % LANES, w % U // (U // HALVES), w % (U // HALVES) * GROUP

        def at(i, w):
            return i * (LANES * U) + (w + 1)

        def turns(eng, turn):
            with eng.Fori(0, S.turns - 1) as i:
                turn(i, False)
            turn(S.turns - 1, True)

        with nc.Block() as block:
            @block.sync
            def _(eng):
                for dst, name in ((w_in, "in_proj"), (w_conv, "conv_w"), (w_dt, "dt_w"), (w_bc, "bc_w"), (w_out, "out_w"),
                                  (pick, "pick"), (conv_b, "conv_b"), (dt_b, "dt_b"), (skip, "D"), (a_neg, "A_log")):
                    src = W["bc_pick" if name == "pick" else f"L0_attn_{name}"]
                    eng.dma_start(dst[:], src).then_inc(weights_in, 16)
                eng.wait_ge(weights_in, 16 * N_LOADS)

            @block.vector
            def _(eng):
                chain = Chain(eng, S.v_chain)
                for n in range(LANES):
                    eng.memset(xc[n][:, :, 0:TAPS - 1], 0.0)
                for k in range(2):
                    eng.memset(dta[k][:, :, 0:1], -1e30)
                eng.memset(tiny[:, :], 1e-6)
                eng.wait_ge(a_ready, 1)
                eng.tensor_scalar(dt_b[:, :], dt_b[:, :], 0.5, None, ALU.mult)
                eng.tensor_scalar(a_neg[:, :, :], a_neg[:, :, :], -1.0, None, ALU.mult).then_inc(const_ready, 1)
                eng.wait_ge(const_ready, 1)

                def prepare(i, n, step):
                    if step == 0:
                        S.front_stats(eng, chain, i, n)
                    elif step == 1:
                        S.front_apply(eng, i, n)
                    elif step == 4:
                        eng.wait_ge(z_tanh_ready, S.nth(i, n))
                        eng.scalar_tensor_tensor(out=z_gate[n][:, :, :], in0=z_tanh[n][:, :, :], scalar=1.0,
                                                 in1=p2[:, :, :], op0=ALU.add, op1=ALU.mult).then_inc(z_gate_ready, 1)
                    elif step == 6:
                        eng.wait_ge(dt_tanh_ready, S.nth(i, n))
                        chain.link(eng.tensor_scalar(dt[n][:, :, :], dt[n][:, :, :], 0.5, 0.5, ALU.mult, ALU.add))
                        chain.link(eng.tensor_scalar(dt[n][:, :, :], dt[n][:, :, :], 1e-4, 1.0, ALU.max, ALU.min))
                        eng.tensor_tensor(dtu[n][:, :, :], dt[n][:, :, :], u_in[n][:, :, :], ALU.mult)
                        eng.wait_ge(bc_in_psum, S.nth(i, n))
                        chain.link(eng.tensor_copy(bc[n][:, :], pO[:, 0, :]))
                        chain.link(eng.tensor_tensor(bc_rest[64:128, :], pO[64:128, 0, :], bc[n][64:128, :], ALU.subtract))
                        chain.link(eng.tensor_copy(bc[n][64:128, :], bc_rest[64:128, :]))
                        chain.link(eng.tensor_tensor(bc_rest[96:128, :], bc_rest[96:128, :], bc[n][96:128, :], ALU.subtract))
                        chain.link(eng.tensor_copy(bc[n][96:128, :], bc_rest[96:128, :]))
                        eng.sem_inc(lane_ready, 1)

                def start_unit(i, w):
                    n, half, first = unit(w)
                    k = w % 2
                    for g in range(GROUP):
                        ins = eng.tensor_scalar(dta[k][:, g, 1:SEQ], dt[n][:, half, 1:SEQ],
                                                a_neg[:, half, first + g:first + g + 1], -5.0, ALU.mult, ALU.max)
                    ins.then_inc(dta_ready, 1)
                    eng.wait_ge(b_in_psum, at(i, w))
                    eng.tensor_tensor(drive[k][:, :, :], pB[:, :, :],
                                      dtu[n][:, half, :].unsqueeze(1).to_broadcast([P, GROUP, SEQ]), ALU.mult)\
                       .then_inc(drive_ready, 1)

                def finish_lane(i, n):
                    eng.wait_ge(y_in_psum, S.nth(i, n))
                    for h in range(HALVES):
                        ins = eng.scalar_tensor_tensor(out=y[n][:, h, :], in0=u_in[n][:, h, :], scalar=skip[:, h:h + 1],
                                                       in1=pY[:, h, :], op0=ALU.mult, op1=ALU.add)
                    chain.link(ins)
                    eng.scalar_tensor_tensor(out=y[n][:, :, :], in0=y[n][:, :, :], scalar=0.5, in1=z_gate[n][:, :, :],
                                             op0=ALU.mult, op1=ALU.mult).then_inc(y_ready, 1)

                def back_stats(i, n):
                    eng.wait_ge(out_in_psum, S.nth(i, n))
                    S.back_norm_stats(eng, chain, n, out_rows)

                def turn(i, last):
                    for w in range(LANES * U):
                        n, half, first = unit(w)
                        k = w % 2
                        if w + 1 < LANES * U:
                            start_unit(i, w + 1)
                        elif not last:
                            start_unit(i + 1, 0)
                        eng.wait_ge(decay_ready, at(i, w))
                        eng.wait_ge(drive_done, at(i, w))
                        chain.link(eng.tensor_tensor_scan(
                            out=state[k][:, :, :].rearrange("p g s -> p (g s)"),
                            data0=decay[k][:, :, :].rearrange("p g s -> p (g s)"),
                            data1=drive[k][:, :, :].rearrange("p g s -> p (g s)"), initial=0.0, op0=ALU.mult, op1=ALU.add))
                        eng.wait_ge(c_in_psum, at(i, w))
                        eng.tensor_tensor(prod[k][:, :, :], state[k][:, :, :], pC[:, :, :], ALU.mult).then_inc(prod_ready, 1)
                        if w < U:
                            prepare(i, 1, w)
                        elif not last:
                            prepare(i + 1, 0, w - U)
                        if w % U == U - 1:
                            finish_lane(i, n)
                        if w == U + 1:
                            back_stats(i, 0)
                        if w == U + 2:
                            S.back_residual(eng, chain, i, 0, out_rows)
                    back_stats(i, 1)
                    S.back_residual(eng, chain, i, 1, out_rows)
                    chain.restart()

                for step in range(U):
                    prepare(0, 0, step)
                start_unit(0, 0)
                chain.restart()
                turns(eng, turn)

            @block.gpsimd
            def _(eng):
                chain = Chain(eng, S.p_chain)

                def turn(i, last):
                    S.front_rstd(eng, chain, i, 1)
                    if not last:
                        S.front_rstd(eng, chain, i + 1, 0)
                    S.back_rstd_step(eng, chain, i, 0)
                    S.back_rstd_step(eng, chain, i, 1)
                    chain.restart()

                S.front_rstd(eng, chain, 0, 0)
                chain.restart()
                turns(eng, turn)

            @block.tensor
            def _(eng):
                eng.wait_ge(weights_in, 16 * N_LOADS)

                def prepare(i, n, step):
                    if step == 1:
                        S.front_transpose(eng, i, n, p1[:, 0, :])
                    elif step == 2:
                        eng.wait_ge(S.xT_ready, S.nth(i, n))
                        for h in range(HALVES):
                            ins = eng.matmul(p1[:, h, :], w_in[:, h * P:(h + 1) * P], S.xT[n][:, :], start=True, stop=True)
                        ins.then_inc(xc_in_psum, 1)
                        for h in range(HALVES):
                            ins = eng.matmul(p2[:, h, :], w_in[:, D_IN + h * P:D_IN + (h + 1) * P], S.xT[n][:, :],
                                             start=True, stop=True)
                        ins.then_inc(z_in_psum, 1)
                    elif step in (3, 4):
                        if step == 3:
                            eng.wait_ge(xc_ready, S.nth(i, n))
                        h = step - 3
                        for j in range(HALVES * TAPS):
                            c, tap = j // TAPS, j % TAPS
                            ins = eng.matmul(p1[:, h, :], w_conv[:, c, tap, h * P:(h + 1) * P], xc[n][:, c, tap:tap + SEQ],
                                             start=(j == 0), stop=(j == HALVES * TAPS - 1))
                        if h == 1:
                            ins.then_inc(u_in_psum, 1)
                    elif step == 5:
                        eng.wait_ge(u_ready, S.nth(i, n))
                        eng.wait_ge(z_gate_ready, S.nth(i, n))
                        for h in range(HALVES):
                            for c in range(HALVES):
                                ins = eng.matmul(p2[:, h, :], w_dt[:, c, h * P:(h + 1) * P], u_in[n][:, c, :],
                                                 start=(c == 0), stop=(c == HALVES - 1))
                        ins.then_inc(dt_in_psum, 1)
                        for c in range(HALVES):
                            ins = eng.matmul(pO[:, 0, :], w_bc[:, c, :], u_in[n][:, c, :], start=(c == 0), stop=(c == HALVES - 1))
                        ins.then_inc(bc_in_psum, 1)

                def spread_b(i, w):
                    n, half, first = unit(w)
                    if w % U == 0:
                        eng.wait_ge(lane_ready, S.nth(i, n))
                    for g in range(GROUP):
                        ins = eng.matmul(pB[:, g, :], pick[:, first + g, :], bc[n][:, :], start=True, stop=True)
                    ins.then_inc(b_in_psum, 1)

                def spread_c(i, w):
                    n, half, first = unit(w)
                    for g in range(GROUP):
                        ins = eng.matmul(pC[:, g, :], pick[:, STATES + first + g, :], bc[n][:, :], start=True, stop=True)
                    ins.then_inc(c_in_psum, 1)

                def sum_states(i, w):
                    n, half, first = unit(w)
                    eng.wait_ge(prod_ready, at(i, w))
                    for g in range(GROUP):
                        s = first + g
                        ins = eng.matmul(pY[:, half, :], core.ident[:, :], prod[w % 2][:, g, :], start=(s == 0),
                                         stop=(s == STATES - 1))
                    if w % U == U - 1:
                        ins.then_inc(y_in_psum, 1)

                def project_out(i, n):
                    eng.wait_ge(y_ready, S.nth(i, n))
                    for t in range(TILES):
                        for h in range(HALVES):
                            ins = eng.matmul(out_rows[:, t, :], y[n][:, h, t * P:(t + 1) * P], w_out[:, h, :],
                                             start=(h == 0), stop=(h == HALVES - 1))
                    ins.then_inc(out_in_psum, 1)

                def turn(i, last):
                    for w in range(LANES * U):
                        if w:
                            eng.wait_ge(prod_ready, at(i, w - 1))
                        spread_c(i, w)
                        if w + 1 < LANES * U:
                            eng.wait_ge(drive_ready, at(i, w))
                            spread_b(i, w + 1)
                        elif not last:
                            eng.wait_ge(drive_ready, at(i, w))
                            spread_b(i + 1, 0)
                        if w:
                            sum_states(i, w - 1)
                        if w < U:
                            prepare(i, 1, w)
                        elif not last:
                            prepare(i + 1, 0, w - U)
                        if w == U:
                            project_out(i, 0)
                    sum_states(i, LANES * U - 1)
                    project_out(i, 1)

                for step in range(U):
                    prepare(0, 0, step)
                spread_b(0, 0)
                turns(eng, turn)

            @block.scalar
            def _(eng):
                eng.wait_ge(weights_in, 16 * N_LOADS)
                eng.activation(a_neg[:, :, :], a_neg[:, :, :], ACT.Exp).then_inc(a_ready, 1)
                eng.wait_ge(const_ready, 1)

                def prepare(i, n, step):
                    if step == 1:
                        S.front_copy(eng, i, n, p1[:, 0, :])
                    elif step == 2:
                        eng.wait_ge(xc_in_psum, S.nth(i, n))
                        eng.copy(xc[n][:, :, TAPS - 1:], p1[:, :, :]).then_inc(xc_ready, 1)
                        eng.wait_ge(z_in_psum, S.nth(i, n))
                        eng.activation(z_tanh[n][:, :, :], p2[:, :, :], ACT.Tanh, scale=0.5).then_inc(z_tanh_ready, 1)
                    elif step == 4:
                        eng.wait_ge(u_in_psum, S.nth(i, n))
                        for h in range(HALVES):
                            ins = eng.activation(u_in[n][:, h, :], p1[:, h, :], ACT.Identity, bias=conv_b[:, h:h + 1])
                        ins.then_inc(u_ready, 1)
                    elif step == 5:
                        eng.wait_ge(dt_in_psum, S.nth(i, n))
                        for h in range(HALVES):
                            ins = eng.activation(dt[n][:, h, :], p2[:, h, :], ACT.Tanh, bias=dt_b[:, h:h + 1], scale=0.5)
                        ins.then_inc(dt_tanh_ready, 1)

                def start_unit(i, w):
                    k = w % 2
                    eng.wait_ge(dta_ready, at(i, w))
                    eng.activation(decay[k][:, :, :], dta[k][:, :, :], ACT.Exp).then_inc(decay_ready, 1)
                    eng.wait_ge(drive_ready, at(i, w))
                    eng.activation(drive[k][:, :, :], drive[k][:, :, :], ACT.Identity, bias=tiny[:, 0:1]).then_inc(drive_done, 1)

                def turn(i, last):
                    for w in range(LANES * U):
                        if w + 1 < LANES * U:
                            start_unit(i, w + 1)
                        elif not last:
                            start_unit(i + 1, 0)
                        if w < U:
                            prepare(i, 1, w)
                        elif not last:
                            prepare(i + 1, 0, w - U)

                for step in range(U):
                    prepare(0, 0, step)
                start_unit(0, 0)
                turns(eng, turn)
        S.clear_semaphores()


EXPERTS = 8


def moe_stage(nc, core, name, FC, src, setup, load, has_bias):
    T = 4
    N = T * P
    E = EXPERTS
    with ExitStack() as ctx:
        S = Stage(nc, ctx, name, 1, core, tiles=T, src=src)
        w1 = S.sb("w1", [P, E, FC * P])
        w2 = S.sb("w2", [P, E * FC, P])
        router = S.sb("router", [P, E])
        router_b = S.sb("router_b", [P, E])
        channel = S.sb("channel", [P, E])
        scale = S.sb("scale", [P, E])
        shift = S.sb("shift", [P, E])
        b1 = S.sb("b1", [P, E * FC])
        b2 = S.sb("b2", [E, P])
        hT = [S.sb(f"hT{k}", [P, FC, N]) for k in range(2)]
        logits = S.sb("logits", [P, T, E])
        top = S.sb("top", [P, T, 8])
        top_at = S.sb("top_at", [P, T, 8], mybir.dt.uint32)
        below_top = S.sb("below_top", [P, T, E])
        expd = S.sb("expd", [P, T, E])
        first = S.sb("first", [P, T, E])
        chosen = S.sb("chosen", [P, T, E])
        gate_sum = S.sb("gate_sum", [P, T])
        gates = S.sb("gates", [P, T, E])
        gT = S.sb("gT", [E, N])
        acc = S.r[0]
        pX = S.ps("pX", [P, N])
        pL = S.ps("pL", [P, N])
        pH = [S.ps(f"pH{k}", [P, N]) for k in range(4)]
        pY = [S.ps(f"pY{k}", [P, N]) for k in range(2)]
        logits3 = pL[:, 0:T * E].rearrange("p (t e) -> p t e", t=T)
        (weights_in, scaled, b1_in_psum, weights_ready, logits_in_psum, below_ready, expd_ready, gates_ready,
         gT_in_psum, gT_ready, b2_in_psum, acc_started, h_in_psum, h_ready, y_in_psum, y_used) = (S.sem(n) for n in (
             "weights_in", "scaled", "b1_in_psum", "weights_ready", "logits_in_psum", "below_ready", "expd_ready",
             "gates_ready", "gT_in_psum", "gT_ready", "b2_in_psum", "acc_started", "h_in_psum", "h_ready",
             "y_in_psum", "y_used"))

        def to_tiles(ap):
            return ap.unsqueeze(2).to_broadcast([P, T, E])

        with nc.Block() as block:
            @block.sync
            def _(eng):
                n = load(eng, weights_in, dict(w1=w1, w2=w2, router=router, router_b=router_b, scale=scale,
                                               shift=shift, b1=b1, b2=b2, channel=channel))
                eng.wait_ge(weights_in, 16 * n)

            n_loads = len(setup)

            @block.vector
            def _(eng):
                chain = Chain(eng, S.v_chain)
                eng.wait_ge(weights_in, 16 * n_loads)
                if has_bias:
                    eng.wait_ge(b1_in_psum, 1)
                    eng.tensor_tensor(b1[:, :], b1[:, :], pL[:, 0:E * FC], ALU.add)
                else:
                    eng.tensor_scalar(router[:, :], router[:, :], scale[:, 0:1], None, ALU.mult)
                for e in range(E):
                    ins = eng.tensor_scalar(w1[:, e, :], w1[:, e, :], scale[:, e:e + 1], None, ALU.mult)
                ins.then_inc(weights_ready, 1)

                def front(i):
                    S.front_stats(eng, chain, i, 0)
                    S.front_apply(eng, i, 0)

                def route(i):
                    eng.wait_ge(logits_in_psum, i + 1)
                    chain.link(eng.tensor_tensor(logits[:, :, :], logits3, router_b[:, :].unsqueeze(1)
                                                 .to_broadcast([P, T, E]), ALU.add))
                    for t in range(T):
                        ins = eng.max(top[:, t, :], logits[:, t, :])
                    chain.link(ins)
                    eng.tensor_tensor(below_top[:, :, :], logits[:, :, :], to_tiles(top[:, :, 0]),
                                      ALU.subtract).then_inc(below_ready, 1)
                    for t in range(T):
                        ins = eng.max_index(top_at[:, t, :], top[:, t, :], logits[:, t, :])
                    chain.link(ins)
                    eng.tensor_tensor(first[:, :, :], channel[:, :].unsqueeze(1).to_broadcast([P, T, E]),
                                      to_tiles(top_at[:, :, 0]), ALU.is_equal)
                    chain.link(eng.tensor_tensor(chosen[:, :, :], channel[:, :].unsqueeze(1).to_broadcast([P, T, E]),
                                                 to_tiles(top_at[:, :, 1]), ALU.is_equal))
                    chain.link(eng.tensor_tensor(chosen[:, :, :], chosen[:, :, :], first[:, :, :], ALU.add))
                    eng.wait_ge(expd_ready, i + 1)
                    chain.link(eng.tensor_tensor(expd[:, :, :], expd[:, :, :], chosen[:, :, :], ALU.mult))
                    chain.link(eng.tensor_reduce(gate_sum[:, :], expd[:, :, :], AX.X, ALU.add))
                    chain.link(eng.reciprocal(gate_sum[:, :], gate_sum[:, :]))
                    eng.tensor_tensor(gates[:, :, :], expd[:, :, :], to_tiles(gate_sum[:, :]), ALU.mult)\
                       .then_inc(gates_ready, 1)
                    eng.wait_ge(gates_ready, i + 1)

                def experts(i, after_first):
                    if has_bias:
                        eng.wait_ge(b2_in_psum, i + 1)
                        chain.link(eng.tensor_tensor(acc[:, :, :], S.xn[0][:, :, :],
                                                     pX[:, :].rearrange("p (t c) -> p t c", t=T), ALU.add))
                    else:
                        for t in range(T):
                            ins = eng.tensor_copy(acc[:, t, :], S.rows(i, 0, t))
                        chain.link(ins)
                    for e in range(E):
                        eng.wait_ge(y_in_psum, i * E + (e + 1))
                        for t in range(T):
                            ins = eng.scalar_tensor_tensor(out=acc[:, t, :], in0=pY[e % 2][:, t * P:(t + 1) * P],
                                                           scalar=gates[:, t, e:e + 1], in1=acc[:, t, :],
                                                           op0=ALU.mult, op1=ALU.add)
                        ins.then_inc(y_used, 1)
                        eng.wait_ge(y_used, i * E + (e + 3))
                        if e == 0:
                            after_first()

                def turn(i, after_first):
                    route(i)
                    experts(i, after_first)
                    S.back_norm_stats(eng, chain, 0, acc)
                    S.back_residual(eng, chain, i, 0, acc)
                    chain.restart()

                eng.sem_inc(y_used, 2)
                front(0)
                chain.restart()
                with eng.Fori(0, S.turns - 1) as i:
                    turn(i, lambda: front(i + 1))
                turn(S.turns - 1, lambda: None)

            @block.gpsimd
            def _(eng):
                chain = Chain(eng, S.p_chain)

                def front(i):
                    S.front_rstd(eng, chain, i, 0)

                def turn(i, between):
                    eng.wait_ge(below_ready, i + 1)
                    eng.tensor_tensor(expd[:, :, :], core.e[:, 0:T * E].rearrange("p (t e) -> p t e", t=T),
                                      below_top[:, :, :], ALU.pow).then_inc(expd_ready, 1)
                    between()
                    S.back_rstd_step(eng, chain, i, 0)
                    chain.restart()

                front(0)
                chain.restart()
                with eng.Fori(0, S.turns - 1) as i:
                    turn(i, lambda: front(i + 1))
                turn(S.turns - 1, lambda: None)

            @block.tensor
            def _(eng):
                eng.wait_ge(weights_in, 16 * n_loads)
                if has_bias:
                    for e in range(E):
                        for c in range(FC):
                            ins = eng.matmul(pL[:, e * FC + c:e * FC + c + 1], w1[:, e, c * P:(c + 1) * P],
                                             shift[:, e:e + 1], start=True, stop=True)
                    ins.then_inc(b1_in_psum, 1)
                eng.wait_ge(weights_ready, 1)

                def hidden(i, e):
                    for c in range(FC):
                        k = e * FC + c
                        if k >= 4:
                            eng.wait_ge(h_ready, i * (E * FC) + (k + 1 - 4))
                        eng.matmul(pH[k % 4][:, :], w1[:, e, c * P:(c + 1) * P], S.xT[0][:, :],
                                   start=True, stop=True).then_inc(h_in_psum, 1)

                def back_to_rows(i, e):
                    eng.wait_ge(h_ready, i * (E * FC) + (e + 1) * FC)
                    eng.wait_ge(y_used, i * E + (e + 1))
                    for t in range(T):
                        for c in range(FC):
                            ins = eng.matmul(pY[e % 2][:, t * P:(t + 1) * P], hT[e % 2][:, c, t * P:(t + 1) * P],
                                             w2[:, e * FC + c, :], start=(c == 0), stop=(c == FC - 1))
                    ins.then_inc(y_in_psum, 1)

                def turn(i):
                    S.front_transpose(eng, i, 0, pX)
                    eng.wait_ge(S.xT_ready, i + 1)
                    for t in range(T):
                        ins = eng.matmul(pL[:, t * E:(t + 1) * E], S.xT[0][:, t * P:(t + 1) * P], router[:, :],
                                         start=True, stop=True)
                    ins.then_inc(logits_in_psum, 1)
                    hidden(i, 0)
                    hidden(i, 1)
                    for e in range(E):
                        back_to_rows(i, e)
                        if e + 2 < E:
                            hidden(i, e + 2)
                        if has_bias and e == 0:
                            eng.wait_ge(gates_ready, i + 1)
                            for t in range(T):
                                ins = eng.transpose(pL[0:E, t * P:(t + 1) * P], gates[:, t, :], core.ident[:, :])
                            ins.then_inc(gT_in_psum, 1)
                        if has_bias and e == 1:
                            eng.wait_ge(gT_ready, i + 1)
                            for t in range(T):
                                ins = eng.matmul(pX[:, t * P:(t + 1) * P], gT[:, t * P:(t + 1) * P], b2[:, :],
                                                 start=True, stop=True)
                            ins.then_inc(b2_in_psum, 1)

                with eng.Fori(0, S.turns) as i:
                    turn(i)

            @block.scalar
            def _(eng):
                eng.wait_ge(weights_in, 16 * n_loads)
                eng.wait_ge(weights_ready, 1)
                with eng.Fori(0, S.turns) as i:
                    S.front_copy(eng, i, 0, pX[:, :])
                    for e in range(E):
                        for c in range(FC):
                            k = e * FC + c
                            eng.wait_ge(h_in_psum, i * (E * FC) + (k + 1))
                            if c == 0 and e >= 2:
                                eng.wait_ge(y_in_psum, i * E + (e - 1))
                            eng.activation(hT[e % 2][:, c, :], pH[k % 4][:, :], ACT.Gelu,
                                           bias=b1[:, k:k + 1] if has_bias else 0.0).then_inc(h_ready, 1)
                            if has_bias and e == 2 and c == FC - 1:
                                eng.wait_ge(gT_in_psum, i + 1)
                                eng.copy(gT[:, :], pL[0:E, :]).then_inc(gT_ready, 1)
        S.clear_semaphores()


def expert_ffn_stage(nc, core, W):
    names = ["router", "router_b", "scale", "shift", "b1", "b2", "channel", "w1", "w2"]

    def load(eng, done, sb):
        eng.dma_start(sb["router"][:, :], W["L1_ffn_router_W"]).then_inc(done, 16)
        eng.dma_start(sb["router_b"][:, :], W["L1_ffn_router_b"].partition_broadcast(P)).then_inc(done, 16)
        eng.dma_start(sb["scale"][:, :], W["L1_ffn_ln_g"]).then_inc(done, 16)
        eng.dma_start(sb["shift"][:, :], W["L1_ffn_ln_b"]).then_inc(done, 16)
        eng.dma_start(sb["b1"][:, :], W["L1_ffn_b1"]).then_inc(done, 16)
        eng.dma_start(sb["b2"][:, :], W["L1_ffn_b2"]).then_inc(done, 16)
        eng.dma_start(sb["channel"][:, :], W["expert_index"].partition_broadcast(P)).then_inc(done, 16)
        eng.dma_start(sb["w1"][:, :, :], W["L1_ffn_W1"].rearrange("e p f -> p e f")).then_inc(done, 16)
        eng.dma_start(sb["w2"][:, :, :], W["L1_ffn_W2"].rearrange("(k p) n -> p k n", p=P)).then_inc(done, 16)
        return len(names)

    moe_stage(nc, core, "l1f", 4, core.X, names, load, True)


def routed_ffn_stage(nc, core, W):
    names = ["router", "router_b", "scale", "channel", "w1", "w2"]

    def load(eng, done, sb):
        eng.dma_start(sb["router"][:, :], W["L0_ffn_router_w"]).then_inc(done, 16)
        eng.dma_start(sb["router_b"][:, :], W["expert_zero"].partition_broadcast(P)).then_inc(done, 16)
        eng.dma_start(sb["scale"][:, :], W["L0_ffn_ln2_w"]).then_inc(done, 16)
        eng.dma_start(sb["channel"][:, :], W["expert_index"].partition_broadcast(P)).then_inc(done, 16)
        eng.dma_start(sb["w1"][:, :, :], W["L0_ffn_w1"].rearrange("p (e f) -> p e f", e=EXPERTS)).then_inc(done, 16)
        eng.dma_start(sb["w2"][:, :, :], W["L0_ffn_w2"].rearrange("(k p) n -> p k n", p=P)).then_inc(done, 16)
        return len(names)

    moe_stage(nc, core, "l0f", 2, core.Y, names, load, False)


HEADS = 16
HEAD = P // HEADS
GROUPS = HEADS // 4
KEYS = 3 * P


def causal_attn_stage(nc, core, W, name, scale, load, n_loads, alibi, inner):
    with ExitStack() as ctx:
        S = Stage(nc, ctx, name, 2, core)
        wq = S.sb("wq", [P, GROUPS, P])
        wk = S.sb("wk", [P, GROUPS, P])
        wv = S.sb("wv", [P, P])
        wo = S.sb("wo", [P, P])
        ln_w = S.sb("ln_w", [P, 1])
        mask = S.sb("mask", [P, P], BF16)
        ident16 = S.sb("ident16", [P, P], BF16)
        k_bias = S.sb("k_bias", [P, GROUPS, SEQ]) if alibi else None
        qT = [S.sb(f"qT{n}", [P, GROUPS, 4, SEQ]) for n in range(2)]
        kT = [S.sb(f"kT{n}", [P, GROUPS, SEQ]) for n in range(2)]
        v = [S.sb(f"v{n}", [P, TILES, HEADS, 32]) for n in range(2)]
        prob = [S.sb(f"prob{n}", [P, 4, KEYS]) for n in range(2)]
        probT = [S.sb(f"probT{n}", [P, 3, 4 * P]) for n in range(2)]
        highest = [S.sb(f"highest{n}", [P, 2, 4]) for n in range(2)]
        oU = [S.sb(f"oU{n}", [P, SEQ]) for n in range(2)]
        rden = [S.sb(f"rden{n}", [P, TILES, 4]) for n in range(2)]
        oT = [S.sb(f"oT{n}", [P, SEQ]) for n in range(2)]
        pS = S.ps("pS", [P, 4, 512])
        pT = [S.ps(f"pT{n}", [P, 512]) for n in range(2)]
        pO = [S.ps(f"pO{n}", [P, 512]) for n in range(2)]
        by_channel = [pO[0][:, k * SEQ:(k + 1) * SEQ] for k in range(2)]
        by_row = [pO[1][:, k * SEQ:(k + 1) * SEQ].rearrange("p (t r d) -> p t r d", t=TILES, r=4) for k in range(2)]
        units = [(g, n) for g in range(GROUPS) for n in range(2)]
        U = len(units)
        (weights_in, zeroed, q_rows_in, weights_ready, inner_xn, proj_in_psum, q_copied, q_copied_too, kv_copied,
         scores_in_psum, below_ready, prob_ready, probT_in_psum, probT_ready, unit_in_psum, unit_copied, unit_by_row,
         unit_read, o_ready, oT_in_psum, oT_ready, y_in_psum) = (S.sem(s) for s in (
            "weights_in", "zeroed", "q_rows_in", "weights_ready", "inner_xn", "proj_in_psum", "q_copied",
            "q_copied_too", "kv_copied", "scores_in_psum", "below_ready", "prob_ready", "probT_in_psum",
            "probT_ready", "unit_in_psum", "unit_copied", "unit_by_row", "unit_read", "o_ready", "oT_in_psum",
            "oT_ready", "y_in_psum"))

        def copy_q(eng, copy, i, n, heads, done):
            for b in range(2):
                eng.wait_ge(proj_in_psum, S.nth(i, n, 5, b))
                for r in heads:
                    rows = slice(32 * r, 32 * r + HEAD)
                    ins = copy(qT[n][rows, 2 * b:2 * b + 2, r, :], pT[b][rows, :].rearrange("p (g s) -> p g s", g=2))
                ins.then_inc(done, 1)

        with nc.Block() as block:
            @block.sync
            def _(eng):
                load(eng, weights_in, dict(wq=wq, wk=wk, wv=wv, wo=wo, ln_w=ln_w, mask=mask, ident16=ident16,
                                           k_bias=k_bias))
                eng.wait_ge(weights_in, 16 * n_loads)
                if alibi:
                    eng.wait_ge(zeroed, 2)
                    for n in range(2):
                        for r in range(4):
                            bias_rows = slice(32 * r + HEAD, 32 * r + HEAD + 2)
                            eng.dma_start(qT[n][bias_rows, :, r, :], W["alibi_q"][bias_rows, :, :]).then_inc(q_rows_in, 16)
                    eng.wait_ge(q_rows_in, 16 * 8)

            @block.vector
            def _(eng):
                chain = Chain(eng, S.v_chain)
                for n in range(2):
                    eng.memset(v[n][:, :, :, HEAD:HEAD + 1], 1.0)
                    eng.memset(v[n][:, :, :, HEAD + 1:32], 0.0)
                eng.wait_ge(weights_in, 16 * n_loads)
                if inner:
                    eng.tensor_scalar(wv[:, :], wv[:, :], ln_w[:, 0:1], None, ALU.mult)
                    eng.tensor_scalar(wk[:, :, :], wk[:, :, :], ln_w[:, 0:1], None, ALU.mult)
                eng.tensor_scalar(wq[:, :, :], wq[:, :, :], ln_w[:, 0:1] if inner else 1.0, None, ALU.mult)\
                   .then_inc(weights_ready, 1)

                def front(i, n, step):
                    if step == 0:
                        S.front_stats(eng, chain, i, n)
                    elif step == 1:
                        S.front_apply(eng, i, n)
                        if inner:
                            eng.wait_ge(S.xn_ready, S.nth(i, n))
                            S.back_norm_stats(eng, chain, n, S.xn[n])
                            for t in range(TILES):
                                eng.tensor_copy(S.of(core.Y, i, n, t), S.xn[n][:, t, :])
                    elif inner:
                        eng.wait_ge(S.back_rstd_ready, S.nth(i, n))
                        for t in range(TILES):
                            ins = eng.tensor_scalar(S.xn[n][:, t, :], S.xn[n][:, t, :], S.back_mv[:, n, t, 0:1],
                                                    S.back_rstd[:, n, t:t + 1], ALU.subtract, ALU.mult)
                        ins.then_inc(inner_xn, 1)

                def turn(i, more):
                    for n in range(2):
                        copy_q(eng, eng.tensor_copy, i, n, (2, 3), q_copied_too)
                        for b in range(2, 4):
                            eng.wait_ge(proj_in_psum, S.nth(i, n, 5, b))
                            dst = kT[n][:, 2 * (b % 2):2 * (b % 2) + 2, :]
                            src = pT[b % 2][:, :].rearrange("p (g s) -> p g s", g=2)
                            if alibi:
                                bias = k_bias[:, 2 * (b % 2):2 * (b % 2) + 2, :]
                                eng.tensor_tensor(dst, src, bias, ALU.add).then_inc(kv_copied, 1)
                            else:
                                eng.tensor_copy(dst, src).then_inc(kv_copied, 1)
                        eng.wait_ge(proj_in_psum, S.nth(i, n, 5, 4))
                        eng.tensor_copy(v[n][:, :, :, 0:HEAD],
                                        pT[0][:, 0:SEQ].rearrange("p (t h d) -> p t h d", t=TILES, h=HEADS))\
                           .then_inc(kv_copied, 1)

                    def outputs(u):
                        g, n = units[u]
                        eng.wait_ge(unit_by_row, i * U + (u + 1))
                        chain.link(eng.reciprocal(rden[u % 2][:, :, :], by_row[u % 2][:, :, :, HEAD]))
                        dst = S.r[n][:, :, 4 * HEAD * g:4 * HEAD * (g + 1)].rearrange("p t (r d) -> p t r d", r=4)
                        chain.link(eng.tensor_tensor(dst, by_row[u % 2][:, :, :, 0:HEAD],
                                                     rden[u % 2][:, :, :].unsqueeze(3).to_broadcast([P, TILES, 4, HEAD]),
                                                     ALU.mult))
                        eng.sem_inc(unit_read, 1)
                        if g == GROUPS - 1:
                            eng.sem_inc(o_ready, 1)

                    for u, (g, n) in enumerate(units):
                        for pair in range(2):
                            two = slice(2 * pair, 2 * pair + 2)
                            top = highest[u % 2]
                            eng.wait_ge(scores_in_psum, i * (2 * U) + (2 * u + pair + 1))
                            eng.tensor_reduce(top[:, 0, two], pS[:, two, 0:P], AX.X, ALU.max)
                            chain.link(eng.tensor_reduce(top[:, 1, two], pS[:, two, P:KEYS], AX.X, ALU.max))
                            for a, (lo, hi) in enumerate(((0, P), (P, KEYS))):
                                ins = eng.tensor_tensor(prob[u % 2][:, two, lo:hi], pS[:, two, lo:hi],
                                                        top[:, a, two].unsqueeze(2).to_broadcast([P, 2, hi - lo]),
                                                        ALU.subtract)
                            ins.then_inc(below_ready, 1)
                        if u >= 3:
                            outputs(u - 3)
                        if more and u >= U - 4 and u < U - 1:
                            for k in range(2):
                                front(i + 1, k, u - (U - 4))
                    for u in range(U - 3, U):
                        outputs(u)
                    for n in range(2):
                        if inner:
                            eng.wait_ge(y_in_psum, S.nth(i, n))
                            for t in range(TILES):
                                y = S.of(core.Y, i, n, t)
                                eng.tensor_tensor(y, y, pO[n][:, t * P:(t + 1) * P], ALU.add)
                        else:
                            S.back_norm_stats(eng, chain, n, S.r[n])
                    if not inner:
                        for n in range(2):
                            S.back_residual(eng, chain, i, n, S.r[n])
                    chain.restart()

                for step in range(3):
                    for n in range(2):
                        front(0, n, step)
                chain.restart()
                with eng.Fori(0, S.turns - 1) as i:
                    turn(i, True)
                turn(S.turns - 1, False)

            @block.gpsimd
            def _(eng):
                chain = Chain(eng, S.p_chain)
                for n in range(2):
                    eng.memset(qT[n][:, :, :, :], 0.0).then_inc(zeroed, 1)

                def front(i):
                    for n in range(2):
                        S.front_rstd(eng, chain, i, n)
                    if inner:
                        for n in range(2):
                            S.back_rstd_step(eng, chain, i, n)

                def turn(i, more):
                    if more:
                        front(i + 1)
                    if not inner:
                        for n in range(2):
                            S.back_rstd_step(eng, chain, i, n)
                    chain.restart()

                front(0)
                chain.restart()
                with eng.Fori(0, S.turns - 1) as i:
                    turn(i, True)
                turn(S.turns - 1, False)

            @block.tensor
            def _(eng):
                eng.wait_ge(weights_in, 16 * n_loads)
                eng.wait_ge(weights_ready, 1)
                if alibi:
                    eng.wait_ge(q_rows_in, 16 * 8)

                def scores(i, u):
                    g, n = units[u]
                    eng.wait_ge(q_copied, S.nth(i, n, 2, 1))
                    eng.wait_ge(q_copied_too, S.nth(i, n, 2, 1))
                    eng.wait_ge(kv_copied, S.nth(i, n, 3, 2))
                    for pair in range(2):
                        if u > 0:
                            eng.wait_ge(below_ready, i * (2 * U) + (2 * u - 1 + pair))
                        for r in (2 * pair, 2 * pair + 1):
                            q = qT[n][:, g, r, :]
                            k = kT[n][:, g, :]
                            eng.matmul(pS[:, r, 0:P], q[:, 0:P], k[:, 0:P], start=True, stop=True)
                            eng.matmul(pS[:, r, P:KEYS], q[:, P:SEQ], k, start=False, stop=True, skip_group_check=True)
                        for r in (2 * pair, 2 * pair + 1):
                            eng.matmul(pS[:, r, 0:P], ident16[:, :], mask[:, :], start=False, stop=True,
                                       skip_group_check=True)
                            ins = eng.matmul(pS[:, r, 2 * P:3 * P], ident16[:, :], mask[:, :], start=False, stop=True,
                                             skip_group_check=True)
                        ins.then_inc(scores_in_psum, 1)

                def back_to_rows(i, u):
                    eng.wait_ge(unit_copied, i * U + (u + 1))
                    if u:
                        eng.wait_ge(unit_read, i * U + u)
                    for t in range(TILES):
                        ins = eng.transpose(pO[1][:, (u % 2) * SEQ + t * P:(u % 2) * SEQ + (t + 1) * P],
                                            oU[u % 2][:, t * P:(t + 1) * P], core.ident[:, :])
                    ins.then_inc(unit_by_row, 1)

                def weigh(i, u):
                    g, n = units[u]
                    eng.wait_ge(probT_ready, i * (3 * U) + (3 * u + 3))
                    for r in range(4):
                        out = by_channel[u % 2][32 * r:32 * r + 32, :]
                        heads = slice(r * P, (r + 1) * P)
                        eng.matmul(out.rearrange("p (t s) -> p t s", t=TILES), v[n][:, 0, 4 * g + r, :],
                                   probT[u % 2][:, 0:2, heads], start=True, stop=True)
                        ins = eng.matmul(out[:, P:SEQ], v[n][:, 1, 4 * g + r, :], probT[u % 2][:, 2, heads],
                                         start=False, stop=True, skip_group_check=True)
                    ins.then_inc(unit_in_psum, 1)

                def transposes(i, u):
                    eng.wait_ge(prob_ready, i * U + (u + 1))
                    for c in range(3):
                        k = 3 * u + c
                        if c == 2 and u >= 2:
                            back_to_rows(i, u - 2)
                        if c == 2 and u >= 1:
                            weigh(i, u - 1)
                        if k >= 2:
                            eng.wait_ge(probT_ready, i * (3 * U) + (k - 1))
                        for r in range(4):
                            ins = eng.transpose(pT[k % 2][:, r * P:(r + 1) * P],
                                                prob[u % 2][:, r, c * P:(c + 1) * P], core.ident[:, :])
                        ins.then_inc(probT_in_psum, 1)

                def front(i, before=None):
                    for n in range(2):
                        if before is not None:
                            eng.wait_ge(probT_ready, before * (3 * U) + (3 * U - 1 + n))
                        S.transpose_rows(eng, i, n, pT[n], S.xn[n], inner_xn if inner else S.xn_ready, S.xt_in_psum)

                def turn(i, more):
                    for n in range(2):
                        eng.wait_ge(S.xT_ready, S.nth(i, 1))
                        for b in range(5):
                            if b == 0 and n:
                                eng.wait_ge(kv_copied, S.nth(i, n - 1, 3, 2))
                            elif b in (2, 3):
                                eng.wait_ge(q_copied, S.nth(i, n, 2, b - 2))
                                eng.wait_ge(q_copied_too, S.nth(i, n, 2, b - 2))
                            elif b == 4:
                                eng.wait_ge(kv_copied, S.nth(i, n, 3, 0))
                            if b < 4:
                                for h in range(2):
                                    ins = eng.matmul(pT[b % 2][:, h * SEQ:(h + 1) * SEQ],
                                                     (wq if b < 2 else wk)[:, 2 * (b % 2) + h, :], S.xT[n][:, :],
                                                     start=True, stop=True)
                            else:
                                for t in range(TILES):
                                    ins = eng.matmul(pT[0][:, t * P:(t + 1) * P], S.xT[n][:, t * P:(t + 1) * P],
                                                     wv[:, :], start=True, stop=True)
                            ins.then_inc(proj_in_psum, 1)
                    scores(i, 0)
                    for u in range(U):
                        if u + 1 < U:
                            scores(i, u + 1)
                        transposes(i, u)
                    if more:
                        front(i + 1, i)
                    back_to_rows(i, U - 2)
                    weigh(i, U - 1)
                    back_to_rows(i, U - 1)
                    if inner:
                        for n in range(2):
                            S.transpose_rows(eng, i, n, pO[n], S.r[n], o_ready, oT_in_psum)
                        for n in range(2):
                            eng.wait_ge(oT_ready, S.nth(i, n))
                            for t in range(TILES):
                                ins = eng.matmul(pO[n][:, t * P:(t + 1) * P], oT[n][:, t * P:(t + 1) * P], wo[:, :],
                                                 start=True, stop=True)
                            ins.then_inc(y_in_psum, 1)

                front(0)
                with eng.Fori(0, S.turns - 1) as i:
                    turn(i, True)
                turn(S.turns - 1, False)

            @block.scalar
            def _(eng):
                eng.wait_ge(zeroed, 2)

                def front(i):
                    for n in range(2):
                        S.front_copy(eng, i, n, pT[n][:, 0:SEQ])

                def turn(i, more):
                    for n in range(2):
                        copy_q(eng, eng.copy, i, n, (0, 1), q_copied)

                    def copy_unit(u):
                        eng.wait_ge(unit_in_psum, i * U + (u + 1))
                        eng.copy(oU[u % 2][:, :], by_channel[u % 2]).then_inc(unit_copied, 1)

                    for u in range(U):
                        eng.wait_ge(below_ready, i * (2 * U) + (2 * u + 2))
                        eng.activation(prob[u % 2][:, :, :], prob[u % 2][:, :, :], ACT.Exp, scale=scale)\
                           .then_inc(prob_ready, 1)
                        for c in range(3):
                            k = 3 * u + c
                            if c == 2 and u:
                                copy_unit(u - 1)
                            eng.wait_ge(probT_in_psum, i * (3 * U) + (k + 1))
                            eng.copy(probT[u % 2][:, c, :], pT[k % 2][:, :]).then_inc(probT_ready, 1)
                    if more:
                        front(i + 1)
                    copy_unit(U - 1)
                    if inner:
                        for n in range(2):
                            eng.wait_ge(oT_in_psum, S.nth(i, n))
                            eng.copy(oT[n][:, :], pO[n][:, 0:SEQ]).then_inc(oT_ready, 1)

                front(0)
                with eng.Fori(0, S.turns - 1) as i:
                    turn(i, True)
                turn(S.turns - 1, False)
        S.clear_semaphores()


def alibi_attn_stage(nc, core, W):
    def load(eng, done, sb):
        for n in ("wq", "wk", "wv"):
            dst = sb[n][:, :] if n == "wv" else sb[n][:, :, :]
            eng.dma_start(dst, W[f"L3_attn_{n}"]).then_inc(done, 16)
        eng.dma_start(sb["k_bias"][:, :, :], W["alibi_k"]).then_inc(done, 16)
        eng.dma_start(sb["mask"][:, :], W["causal_mask"]).then_inc(done, 16)
        eng.dma_start(sb["ident16"][:, :], W["ident16"]).then_inc(done, 16)

    causal_attn_stage(nc, core, W, "l3a", float(P) ** -0.5, load, 6, True, False)


def routed_block_stage(nc, core, W):
    def load(eng, done, sb):
        for n in ("wq", "wk", "wv", "wo"):
            dst = sb[n][:, :] if n in ("wv", "wo") else sb[n][:, :, :]
            eng.dma_start(dst, W[f"L0_ffn_{n}"]).then_inc(done, 16)
        eng.dma_start(sb["ln_w"][:, :], W["L0_ffn_ln1_w"]).then_inc(done, 16)
        eng.dma_start(sb["mask"][:, :], W["causal_mask"]).then_inc(done, 16)
        eng.dma_start(sb["ident16"][:, :], W["ident16"]).then_inc(done, 16)

    with ExitStack() as ctx:
        inner_rows(nc, ctx, core, "l0f_rows")
        causal_attn_stage(nc, core, W, "l0t", float(HEAD) ** -0.5, load, 7, False, True)
        routed_ffn_stage(nc, core, W)


def bond_attn_stage(nc, core, W):
    H, BD, K = 16, 16, 32
    HALVES = 2
    T = 4
    N = T * P
    SEQS = 2
    PAD = K - 1
    BATCH = 4
    RUN = 16
    BATCHES = HALVES * K // BATCH
    RUNS = HALVES * K // RUN
    RING = 2
    HG = 8
    scratch = nc.dram_tensor("val_rows", [SEQS, PAD + SEQ, P], F32).ap()
    with ExitStack() as ctx:
        S = Stage(nc, ctx, "l1a", 1, core, tiles=T)
        w_disp = S.sb("w_disp", [P, 2 * P])
        w_val = S.sb("w_val", [P, P])
        w_cproj = S.sb("w_cproj", [P, P])
        w_small = S.sb("w_small", [P, 6, P])
        w_bond = S.sb("w_bond", [P, RUN, P])
        w_damage_out = S.sb("w_damage_out", [P, RUN, P])
        biases = S.sb("biases", [P, 6])
        w_pos = S.sb("w_pos", [BD, P])
        rel_emb = S.sb("rel_emb", [BD, K])
        pos = S.sb("pos", [P, K])
        b_val = S.sb("b_val", [P, P])
        b_cproj = S.sb("b_cproj", [P, P])
        b_bond = S.sb("b_bond", [P, 1])
        mask = S.sb("mask", [P, TILES, K])
        mean_w = S.sb("mean_w", [P, TILES, SEQ])
        zeros = S.sb("zeros", [PAD, P])
        diff = S.sb("diff", [P, N])
        disp = S.sb("disp", [P, N])
        disp_diff = S.sb("disp_diff", [P, N])
        state = S.sb("state", [P, N])
        a_bond = S.sb("a_bond", [P, HALVES, SEQS, PAD + SEQ])
        b_bond_in = S.sb("b_bond_in", [P, HALVES, SEQS, SEQ])
        a_dmg = S.sb("a_dmg", [P, HALVES, SEQS, PAD + SEQ])
        b_dmg = S.sb("b_dmg", [P, HALVES, SEQS, SEQ])
        bond = [S.sb(f"bond{k}", [P, BATCH, SEQS, SEQ]) for k in range(RING)]
        dmg = [S.sb(f"dmg{k}", [P, BATCH, SEQS, SEQ]) for k in range(RING)]
        logit = S.sb("logit", [P, RUNS, N])
        damage = S.sb("damage", [P, RUNS, N])
        weight = S.sb("weight", [P, T, H, K])
        highest = S.sb("highest", [P, T * H])
        total = S.sb("total", [P, T * H])
        val = S.sb("val", [P, T, P])
        window = S.sb("window", [P, K, P])
        prod = S.sb("prod", [P, HG, P // H, K])
        o = S.r[0]
        oT = S.sb("oT", [P, N])
        p1 = S.ps("p1", [P, N])
        p2 = S.ps("p2", [P, N])
        p3 = S.ps("p3", [P, N])
        p4 = S.ps("p4", [P, N])
        pBond = [S.ps(f"pBond{k}", [P, N]) for k in range(2)]
        pDmg = [S.ps(f"pDmg{k}", [P, N]) for k in range(2)]
        (weights_in, pad_ready, setup_psum, setup_ready, pad_stored, mean_in_psum, diff_ready, lin_in_psum, lin_ready,
         val_in_psum, val_ready, val_stored, window_in, window_used, bond_in, dmg_in, bond_act, dmg_act, bond_used,
         dmg_used, run_in_psum, run_copied, tanh_ready, logits_ready, logits_in_psum, below_ready, exp_ready,
         o_ready, oT_in_psum, oT_ready, y_in_psum) = (S.sem(s) for s in (
             "weights_in", "pad_ready", "setup_psum", "setup_ready", "pad_stored", "mean_in_psum", "diff_ready",
             "lin_in_psum", "lin_ready", "val_in_psum", "val_ready", "val_stored", "window_in", "window_used",
             "bond_in", "dmg_in", "bond_act", "dmg_act", "bond_used", "dmg_used", "run_in_psum", "run_copied",
             "tanh_ready", "logits_ready", "logits_in_psum", "below_ready", "exp_ready", "o_ready", "oT_in_psum",
             "oT_ready", "y_in_psum"))
        LIN = 7
        N_LOADS = 14

        TANH_AT, LOGITS_AT = 1, 1
        SOFTMAX_AT, EXP_AT, TOTALS_AT = 2, 3, 4
        SUMS_FROM, SUMS_TO = 5, 14
        LIN_1_AT = (3, 4, 5)
        ROWS_AT, DIFF_AT = 6, 8
        LIN_0_AT = (9, 10, 11)
        PIECES = 2 * T * H // HG

        def pieces(b):
            n = SUMS_TO + 1 - SUMS_FROM
            inside = SUMS_FROM <= b <= SUMS_TO
            return range((b - SUMS_FROM) * PIECES // n, (b + 1 - SUMS_FROM) * PIECES // n) if inside else ()

        def batch(b):
            return b // (K // BATCH), b % (K // BATCH) * BATCH

        def two(ap):
            return ap.rearrange("p (n s) -> p n s", n=SEQS)

        with nc.Block() as block:
            @block.sync
            def _(eng):
                loads = [(w_disp, "w_disp"), (w_val, "w_val"), (w_cproj, "w_cproj"), (w_small, "w_small"),
                         (w_bond, "w_bond"), (w_damage_out, "w_damage_out"), (biases, "biases"), (w_pos, "w_pos"),
                         (rel_emb, "rel_emb"), (mask, "mask"), (mean_w, "mean_w")]
                for dst, name in loads:
                    eng.dma_start(dst[:], W[f"L1_attn_{name}"]).then_inc(weights_in, 16)
                for dst, name in ((b_val, "b_val"), (b_cproj, "b_cproj"), (b_bond, "b_bond_out")):
                    eng.dma_start(dst[:, :], W[f"L1_attn_{name}"].partition_broadcast(P)).then_inc(weights_in, 16)
                eng.wait_ge(weights_in, 16 * N_LOADS)
                eng.wait_ge(pad_ready, 1)
                for n in range(SEQS):
                    eng.dma_start(scratch[n, 0:PAD, :], zeros[:, :]).then_inc(pad_stored, 16)
                eng.wait_ge(pad_stored, 16 * SEQS)

                def store_values(i, windows):
                    eng.wait_ge(val_ready, i + 1)
                    if windows is not None:
                        eng.wait_ge(window_in, windows * (16 * T) + 16 * T)
                    for n in range(SEQS):
                        eng.dma_start(scratch[n, PAD:, :].rearrange("(t p) c -> p t c", p=P),
                                      val[:, n * TILES:(n + 1) * TILES, :]).then_inc(val_stored, 16)

                def load_windows(i):
                    eng.wait_ge(val_stored, i * (16 * SEQS) + 16 * SEQS)
                    for t in range(T):
                        eng.wait_ge(window_used, i * T + (t + 1))
                        rows = scratch[t // TILES]
                        src = bass.AP(tensor=rows.tensor, offset=rows.offset + t % TILES * P * P, ap=[[P, P], [1, K * P]])
                        eng.dma_start(window[:, :, :].rearrange("p k c -> p (k c)"), src).then_inc(window_in, 16)

                store_values(0, None)
                with eng.Fori(0, S.turns - 1) as i:
                    load_windows(i)
                    store_values(i + 1, i)
                load_windows(S.turns - 1)

            @block.vector
            def _(eng):
                chain = Chain(eng, S.v_chain)
                eng.memset(zeros[:, :], 0.0).then_inc(pad_ready, 1)
                eng.memset(a_bond[:, :, :, 0:PAD], 0.0)
                eng.memset(a_dmg[:, :, :, 0:PAD], 0.0)
                eng.wait_ge(weights_in, 16 * N_LOADS)
                eng.wait_ge(setup_psum, 1)
                eng.tensor_copy(pos[:, :], p1[:, 0:K])
                chain.link(eng.tensor_scalar(b_bond[:, :], b_bond[:, :], -5.0, None, ALU.add))
                eng.tensor_scalar(mask[:, :, :], mask[:, :, :], b_bond[:, 0:1], None, ALU.add)
                eng.tensor_scalar(biases[:, 5:6], biases[:, 5:6], 0.5, None, ALU.mult)
                eng.tensor_scalar(w_small[:, 5, :], w_small[:, 5, :], -1.0, None, ALU.mult).then_inc(setup_ready, 1)
                eng.wait_ge(setup_ready, 1)
                eng.sem_inc(window_used, 1)
                chain.restart()

                rows3 = weight[:, :, :, :].rearrange("p t h k -> p (t h) k")
                o3 = o[:, :, :].rearrange("p t (h e) -> p (t h) e", h=H)

                def logits(i):
                    eng.wait_ge(tanh_ready, i + 1)
                    eng.scalar_tensor_tensor(out=logit[:, :, :], in0=damage[:, :, :], scalar=-5.0, in1=logit[:, :, :],
                                             op0=ALU.mult, op1=ALU.add).then_inc(logits_ready, 1)
                    for t in range(T):
                        eng.wait_ge(logits_in_psum, i * T + (t + 1))
                        src = (p1, p2, p3, p4)[t][:, :].rearrange("p (a b h k) -> p a b h k", a=HALVES, b=2, h=8)
                        dst = weight[:, t, :, :].rearrange("p (a h) (b k) -> p a b h k", a=HALVES, b=2)
                        for a in range(HALVES):
                            m = mask[:, t % TILES, :].rearrange("p (b k) -> p b k", b=2).unsqueeze(2)\
                                .to_broadcast([P, 2, 8, RUN])
                            ins = eng.tensor_tensor(dst[:, a], src[:, a], m, ALU.add)
                    chain.link(ins)

                def below_highest(i):
                    chain.link(eng.tensor_reduce(highest[:, :], rows3, AX.X, ALU.max))
                    eng.tensor_tensor(rows3, rows3, highest[:, :].unsqueeze(2).to_broadcast([P, T * H, K]), ALU.subtract)\
                       .then_inc(below_ready, 1)

                def totals(i):
                    eng.wait_ge(exp_ready, i + 1)
                    chain.link(eng.tensor_reduce(total[:, :], rows3, AX.X, ALU.add))
                    chain.link(eng.reciprocal(total[:, :], total[:, :]))

                def sum_piece(i, piece):
                    t, g, second = piece // 4, piece % 4 // 2, piece % 2
                    if not second:
                        if g == 0:
                            eng.wait_ge(window_in, i * (16 * T) + 16 * (t + 1))
                        v = window[:, :, g * HG * 8:(g + 1) * HG * 8].rearrange("p k (h e) -> p h e k", h=HG)
                        wgt = weight[:, t, g * HG:(g + 1) * HG, :]
                        mul = eng.tensor_tensor(prod[:, :, :, :], v, wgt.unsqueeze(2).to_broadcast([P, HG, 8, K]), ALU.mult)
                        if g == H // HG - 1:
                            mul.then_inc(window_used, 1)
                            eng.wait_ge(window_used, i * T + (t + 2))
                        else:
                            chain.link(mul)
                    else:
                        chain.link(eng.tensor_reduce(o[:, t, g * HG * 8:(g + 1) * HG * 8].rearrange("p (h e) -> p h e", h=HG),
                                                     prod[:, :, :, :], AX.X, ALU.add))

                def scale_sums(i):
                    eng.tensor_tensor(o3, o3, total[:, :].unsqueeze(2).to_broadcast([P, T * H, P // H]), ALU.mult)\
                       .then_inc(o_ready, 1)

                def residual(i):
                    eng.wait_ge(y_in_psum, i + 1)
                    chain.link(eng.tensor_tensor(o[:, :, :], p3[:, :].rearrange("p (t c) -> p t c", t=T),
                                                 b_cproj[:, :].unsqueeze(1).to_broadcast([P, T, P]), ALU.add))
                    S.back_norm_stats(eng, chain, 0, o)
                    S.back_residual(eng, chain, i, 0, o)

                def rows(i):
                    S.front_stats(eng, chain, i, 0)
                    S.front_apply(eng, i, 0)

                def difference(i):
                    eng.wait_ge(mean_in_psum, i + 1)
                    eng.wait_ge(S.xT_ready, i + 1)
                    eng.tensor_tensor(diff[:, :], p2[:, :], S.xT[0][:, :], ALU.subtract).then_inc(diff_ready, 1)

                def values(i, before):
                    eng.wait_ge(val_in_psum, i + 1)
                    if before is not None:
                        eng.wait_ge(val_stored, before * (16 * SEQS) + 16 * SEQS)
                    eng.tensor_tensor(val[:, :, :], p2[:, :].rearrange("p (t c) -> p t c", t=T),
                                      b_val[:, :].unsqueeze(1).to_broadcast([P, T, P]), ALU.add).then_inc(val_ready, 1)

                def turn(i, last, more):
                    for b in range(BATCHES):
                        half, k0 = batch(b)
                        eng.wait_ge(lin_ready, i * (HALVES * LIN) + (half * LIN + LIN))
                        eng.wait_ge(bond_used, i * BATCHES + (b + 1))
                        for j in range(BATCH):
                            k = k0 + j
                            ins = eng.scalar_tensor_tensor(out=bond[b % RING][:, j, :, :],
                                                           in0=a_bond[:, half, :, k:k + SEQ], scalar=pos[:, k:k + 1],
                                                           in1=b_bond_in[:, half, :, :], op0=ALU.add, op1=ALU.add)
                        ins.then_inc(bond_in, 1)
                        if last is not None:
                            if b == SOFTMAX_AT:
                                logits(last)
                                below_highest(last)
                            if b == TOTALS_AT:
                                totals(last)
                            for piece in pieces(b):
                                sum_piece(last, piece)
                            if b == SUMS_TO:
                                scale_sums(last)
                        if more and b == ROWS_AT:
                            rows(i + 1)
                        if more and b == DIFF_AT:
                            difference(i + 1)
                    if more:
                        values(i + 1, i)
                    if last is not None:
                        residual(last)
                    chain.restart()

                rows(0)
                difference(0)
                values(0, None)
                chain.restart()
                turn(0, None, True)
                with eng.Fori(1, S.turns - 1) as i:
                    turn(i, i - 1, True)
                end = S.turns - 1
                turn(end, end - 1, False)
                logits(end)
                below_highest(end)
                totals(end)
                for piece in range(PIECES):
                    sum_piece(end, piece)
                scale_sums(end)
                residual(end)

            @block.gpsimd
            def _(eng):
                chain = Chain(eng, S.p_chain)
                eng.wait_ge(setup_ready, 1)

                def turn(i, last, more):
                    for b in range(BATCHES):
                        half, k0 = batch(b)
                        eng.wait_ge(lin_ready, i * (HALVES * LIN) + (half * LIN + LIN))
                        eng.wait_ge(dmg_used, i * BATCHES + (b + 1))
                        for j in range(BATCH):
                            k = k0 + j
                            ins = eng.tensor_tensor(dmg[b % RING][:, j, :, :], a_dmg[:, half, :, k:k + SEQ],
                                                    b_dmg[:, half, :, :], ALU.add)
                        ins.then_inc(dmg_in, 1)
                        if more and b == ROWS_AT:
                            S.front_rstd(eng, chain, i + 1, 0)
                    if last is not None:
                        S.back_rstd_step(eng, chain, last, 0)
                    chain.restart()

                S.front_rstd(eng, chain, 0, 0)
                chain.restart()
                turn(0, None, True)
                with eng.Fori(1, S.turns - 1) as i:
                    turn(i, i - 1, True)
                turn(S.turns - 1, S.turns - 2, False)
                S.back_rstd_step(eng, chain, S.turns - 1, 0)

            @block.tensor
            def _(eng):
                eng.wait_ge(weights_in, 16 * N_LOADS)
                eng.matmul(p1[:, 0:K], w_pos[:, :], rel_emb[:, :], start=True, stop=True).then_inc(setup_psum, 1)
                eng.wait_ge(setup_ready, 1)
                eng.sem_inc(bond_used, RING)
                eng.sem_inc(dmg_used, RING)
                STATE, STRAIN, STATE_I, STATE_J, DAMAGE, MINUS_STRAIN = range(6)

                def project_out(i):
                    S.transpose_rows(eng, i, 0, p1, o, o_ready, oT_in_psum)
                    eng.wait_ge(oT_ready, i + 1)
                    for t in range(T):
                        ins = eng.matmul(p3[:, t * P:(t + 1) * P], oT[:, t * P:(t + 1) * P], w_cproj[:, :],
                                         start=True, stop=True)
                    ins.then_inc(y_in_psum, 1)

                def rows(i, before):
                    if before is not None:
                        eng.wait_ge(lin_ready, before * (HALVES * LIN) + HALVES * LIN)
                    S.front_transpose(eng, i, 0, p1)
                    for n in range(SEQS):
                        for t in range(TILES):
                            ins = eng.matmul(p2[:, n * SEQ:(n + 1) * SEQ], S.xn[0][:, n * TILES + t, :], mean_w[:, t, :],
                                             start=(t == 0), stop=(t == TILES - 1))
                    ins.then_inc(mean_in_psum, 1)

                def values(i):
                    eng.wait_ge(diff_ready, i + 1)
                    for t in range(T):
                        ins = eng.matmul(p2[:, t * P:(t + 1) * P], S.xT[0][:, t * P:(t + 1) * P], w_val[:, :],
                                         start=True, stop=True)
                    ins.then_inc(val_in_psum, 1)

                def logits(i):
                    eng.wait_ge(logits_ready, i + 1)
                    eng.wait_ge(lin_ready, i * (HALVES * LIN) + HALVES * LIN)
                    for t in range(T):
                        for r in range(RUNS):
                            ins = eng.transpose((p1, p2, p3, p4)[t][:, r * P:(r + 1) * P], logit[:, r, t * P:(t + 1) * P],
                                                core.ident[:, :])
                        ins.then_inc(logits_in_psum, 1)

                def linear(i, half, step):
                    base = half * LIN
                    before = i * (HALVES * LIN)
                    if step == 0:
                        if half == 0:
                            eng.wait_ge(diff_ready, i + 1)
                        else:
                            eng.wait_ge(lin_ready, before + base)
                        cols = slice(half * P, (half + 1) * P)
                        eng.matmul(p1[:, :], w_disp[:, cols], S.xT[0][:, :], start=True, stop=True).then_inc(lin_in_psum, 1)
                        eng.matmul(p3[:, :], w_disp[:, cols], diff[:, :], start=True, stop=True).then_inc(lin_in_psum, 1)
                    elif step == 1:
                        eng.wait_ge(lin_ready, before + (base + 2))
                        eng.matmul(p4[:, :], w_small[:, STATE, :], disp_diff[:, :], start=True, stop=True).then_inc(lin_in_psum, 1)
                        eng.matmul(p1[:, :], w_small[:, DAMAGE, :], disp[:, :], start=True, stop=True).then_inc(lin_in_psum, 1)
                    else:
                        eng.wait_ge(lin_ready, before + (base + 3))
                        eng.matmul(p3[:, :], w_small[:, STRAIN, :], disp[:, :], start=True, stop=False)
                        eng.matmul(p3[:, :], w_small[:, STATE_J, :], state[:, :], start=False, stop=True).then_inc(lin_in_psum, 1)
                        eng.matmul(p4[:, :], w_small[:, STATE_I, :], state[:, :], start=True, stop=False)
                        eng.matmul(p4[:, :], w_small[:, MINUS_STRAIN, :], disp[:, :], start=False, stop=True).then_inc(lin_in_psum, 1)

                def turn(i, last, more):
                    for b in range(BATCHES):
                        half, k0 = batch(b)
                        run = b * BATCH // RUN
                        if b * BATCH % RUN == 0 and run >= 2:
                            eng.wait_ge(run_copied, i * RUNS + (run - 1))
                        for act, used, w, bank, buf in ((bond_act, bond_used, w_bond, pBond, bond),
                                                        (dmg_act, dmg_used, w_damage_out, pDmg, dmg)):
                            eng.wait_ge(act, i * BATCHES + (b + 1))
                            for j in range(BATCH):
                                k = (k0 + j) % RUN
                                ins = eng.matmul(two(bank[run % 2][:, :]), w[:, k, :], buf[b % RING][:, j, :, :],
                                                 start=(k == 0), stop=(k == RUN - 1))
                            ins.then_inc(used, 1)
                        if (b + 1) * BATCH % RUN == 0:
                            eng.wait_ge(dmg_used, i * BATCHES + (b + 1 + RING))
                            eng.sem_inc(run_in_psum, 1)
                        if last is not None and b == LOGITS_AT:
                            logits(last)
                        if b in LIN_1_AT:
                            if last is not None and b == LIN_1_AT[0]:
                                eng.wait_ge(below_ready, last + 1)
                            linear(i, 1, LIN_1_AT.index(b))
                        if more and b == ROWS_AT:
                            rows(i + 1, i)
                        if more and b in LIN_0_AT:
                            linear(i + 1, 0, LIN_0_AT.index(b))
                        if b == SUMS_TO:
                            eng.wait_ge(lin_ready, i * (HALVES * LIN) + (HALVES + (1 if more else 0)) * LIN)
                            if more:
                                values(i + 1)
                            if last is not None:
                                project_out(last)

                rows(0, None)
                for step in range(3):
                    linear(0, 0, step)
                values(0)
                turn(0, None, True)
                with eng.Fori(1, S.turns - 1) as i:
                    turn(i, i - 1, True)
                turn(S.turns - 1, S.turns - 2, False)
                logits(S.turns - 1)
                project_out(S.turns - 1)

            @block.scalar
            def _(eng):
                eng.wait_ge(weights_in, 16 * N_LOADS)
                eng.wait_ge(setup_ready, 1)

                def exps(i):
                    eng.wait_ge(below_ready, i + 1)
                    eng.activation(weight[:, :, :, :], weight[:, :, :, :], ACT.Exp).then_inc(exp_ready, 1)

                def turn_sums(i):
                    eng.wait_ge(oT_in_psum, i + 1)
                    eng.copy(oT[:, :], p1[:, :]).then_inc(oT_ready, 1)

                def linear(i, half, step):
                    def copies(k, outs):
                        eng.wait_ge(lin_in_psum, i * (HALVES * (LIN - 1)) + (half * (LIN - 1) + k))
                        for out, src, bias, sign in outs:
                            eng.activation(out, src, ACT.Identity, bias=bias, scale=sign).then_inc(lin_ready, 1)

                    if step == 0:
                        copies(1, [(disp[:, :], p1[:, :], biases[:, half:half + 1], 1.0)])
                        copies(2, [(disp_diff[:, :], p3[:, :], 0.0, 1.0)])
                    elif step == 1:
                        copies(3, [(state[:, :], p4[:, :], biases[:, 2:3], 1.0)])
                        copies(4, [(a_dmg[:, half, :, PAD:], two(p1[:, :]), 0.0, 1.0),
                                   (b_dmg[:, half, :, :], two(p1[:, :]), biases[:, 4:5], -1.0)])
                    else:
                        copies(5, [(a_bond[:, half, :, PAD:], two(p3[:, :]), 0.0, 1.0)])
                        copies(6, [(b_bond_in[:, half, :, :], two(p4[:, :]), biases[:, 3:4], 1.0)])

                def copy_run(i, run):
                    eng.wait_ge(run_in_psum, i * RUNS + (run + 1))
                    eng.copy(logit[:, run, :], pBond[run % 2][:, :])
                    eng.copy(damage[:, run, :], pDmg[run % 2][:, :]).then_inc(run_copied, 1)

                def tanhs(i):
                    copy_run(i, RUNS - 1)
                    eng.wait_ge(run_copied, i * RUNS + RUNS)
                    eng.activation(damage[:, :, :], damage[:, :, :], ACT.Tanh, bias=biases[:, 5:6], scale=0.5)\
                       .then_inc(tanh_ready, 1)

                def turn(i, last, more):
                    for b in range(BATCHES):
                        for came, act, buf in ((bond_in, bond_act, bond), (dmg_in, dmg_act, dmg)):
                            eng.wait_ge(came, i * BATCHES + (b + 1))
                            eng.activation(buf[b % RING][:], buf[b % RING][:], ACT.Gelu).then_inc(act, 1)
                        if b and b * BATCH % RUN == 0:
                            copy_run(i, b * BATCH // RUN - 1)
                        if last is not None and b == TANH_AT:
                            tanhs(last)
                        if b - 1 in LIN_1_AT:
                            linear(i, 1, LIN_1_AT.index(b - 1))
                        if more and b - 1 == ROWS_AT:
                            S.front_copy(eng, i + 1, 0, p1[:, :])
                        if more and b - 1 in LIN_0_AT:
                            linear(i + 1, 0, LIN_0_AT.index(b - 1))
                        if last is not None and b == EXP_AT:
                            exps(last)
                    if last is not None:
                        turn_sums(last)

                S.front_copy(eng, 0, 0, p1[:, :])
                for step in range(3):
                    linear(0, 0, step)
                turn(0, None, True)
                with eng.Fori(1, S.turns - 1) as i:
                    turn(i, i - 1, True)
                turn(S.turns - 1, S.turns - 2, False)
                tanhs(S.turns - 1)
                exps(S.turns - 1)
                turn_sums(S.turns - 1)
        S.clear_semaphores()


def linear_attn_stage(nc, core, W):
    HD = 8
    HEADS = P // HD
    LOG_C = 5.545177444479562
    with ExitStack() as ctx:
        S = Stage(nc, ctx, "l2a", 2, core)
        wqkv = S.sb("wqkv", [P, 3 * P])
        wo = S.sb("wo", [P, P])
        norm_const = S.sb("norm_const", [P, P])
        v_factor = S.sb("v_factor", [P, P])
        same_head = S.sb("same_head", [P, P])
        sq = [S.sb(f"sq{k}", [P, TILES, 2 * P]) for k in range(2)]
        n2 = [S.sb(f"n2{k}", [P, TILES * 2 * HEADS]) for k in range(2)]
        qk = [S.sb(f"qk{k}", [P, TILES, 2 * P]) for k in range(2)]
        v = [S.sb(f"v{k}", [P, TILES, P]) for k in range(2)]
        qT = [S.sb(f"qT{k}", [P, SEQ]) for k in range(2)]
        kv = [S.sb(f"kv{k}", [P, P]) for k in range(2)]
        oT = [S.sb(f"oT{k}", [P, SEQ]) for k in range(2)]
        pT = [S.ps(f"pT{k}", [P, 512]) for k in range(2)]
        pQ = [S.ps(f"pQ{k}", [P, TILES, 512]) for k in range(2)]
        pM = [S.ps(f"pM{k}", [P, 512]) for k in range(2)]
        y = [pT[k][:, 256:512].rearrange("p (t c) -> p t c", t=TILES) for k in range(2)]
        (weights_in, qkv_in_psum, sq_ready, n2_ready, norm_ready, qkv_ready, kv_in_psum, kv_ready, qT_ready,
         oT_in_psum, oT_ready, y_in_psum, factor, mask_ready) = (S.sem(n) for n in (
            "weights_in", "qkv_in_psum", "sq_ready", "n2_ready", "norm_ready", "qkv_ready", "kv_in_psum",
            "kv_ready", "qT_ready", "oT_in_psum", "oT_ready", "y_in_psum", "factor", "mask_ready"))
        with nc.Block() as block:
            @block.sync
            def _(eng):
                eng.dma_start(wqkv[:, :], W["L2_attn_Wqkv"]).then_inc(weights_in, 16)
                eng.dma_start(wo[:, :], W["L2_attn_Wo"]).then_inc(weights_in, 16)
                eng.dma_start(norm_const[:, :], W["L2_attn_norm_const"].partition_broadcast(P)).then_inc(weights_in, 16)
                eng.dma_start(same_head[:, :], W["same_head"]).then_inc(weights_in, 16)
                eng.wait_ge(weights_in, 64)

            @block.vector
            def _(eng):
                chain = Chain(eng, S.v_chain)
                eng.wait_ge(factor, 1)
                eng.tensor_scalar(v_factor[:, :], v_factor[:, :], 1.0, -0.5 * LOG_C, ALU.add, ALU.mult).then_inc(mask_ready, 1)
                eng.wait_ge(factor, 2)
                with eng.Fori(0, S.turns) as i:
                    for n in range(2):
                        S.front_stats(eng, chain, i, n)
                    for n in range(2):
                        S.front_apply(eng, i, n)
                    for n in range(2):
                        eng.wait_ge(sq_ready, S.nth(i, n))
                        chain.link(eng.tensor_reduce(n2[n][:, :].rearrange("p (t h) -> p t h", t=TILES),
                                                     sq[n][:, :, :].rearrange("p t (h d) -> p t h d", d=HD), AX.X, ALU.add))
                        eng.tensor_scalar(n2[n][:, :], n2[n][:, :], 1e-24, None, ALU.max).then_inc(n2_ready, 1)
                    for n in range(2):
                        for t in range(TILES):
                            ins = eng.tensor_tensor(v[n][:, t, :], pQ[n][:, t, 2 * P:3 * P], v_factor[:, :], ALU.mult)
                        eng.wait_ge(norm_ready, S.nth(i, n))
                        chain.link(eng.reciprocal(n2[n][:, :], n2[n][:, :]))
                        eng.tensor_tensor(qk[n][:, :, :].rearrange("p t (h d) -> p t h d", d=HD),
                                          pQ[n][:, :, 0:2 * P].rearrange("p t (h d) -> p t h d", d=HD),
                                          n2[n][:, :].rearrange("p (t h) -> p t h", t=TILES).unsqueeze(3)
                                          .to_broadcast([P, TILES, 2 * HEADS, HD]), ALU.mult).then_inc(qkv_ready, 1)
                    for n in range(2):
                        eng.wait_ge(kv_in_psum, S.nth(i, n))
                        eng.tensor_tensor(kv[n][:, :], pM[n][:, 0:P], same_head[:, :], ALU.mult).then_inc(kv_ready, 1)
                    for n in range(2):
                        eng.wait_ge(y_in_psum, S.nth(i, n))
                        S.back_norm_stats(eng, chain, n, y[n])
                    for n in range(2):
                        S.back_residual(eng, chain, i, n, y[n])
                    chain.restart()

            @block.gpsimd
            def _(eng):
                chain = Chain(eng, S.p_chain)
                with eng.Fori(0, S.turns) as i:
                    for n in range(2):
                        S.front_rstd(eng, chain, i, n)
                    for n in range(2):
                        S.back_rstd_step(eng, chain, i, n)
                    chain.restart()

            @block.tensor
            def _(eng):
                eng.wait_ge(weights_in, 64)
                with eng.Fori(0, S.turns) as i:
                    for n in range(2):
                        S.front_transpose(eng, i, n, pT[n][:, 0:256])
                    for n in range(2):
                        eng.wait_ge(S.xT_ready, S.nth(i, n))
                        for t in range(TILES):
                            ins = eng.matmul(pQ[n][:, t, 0:3 * P], S.xT[n][:, t * P:(t + 1) * P], wqkv[:, :],
                                             start=True, stop=True)
                        ins.then_inc(qkv_in_psum, 1)
                    for n in range(2):
                        eng.wait_ge(qkv_ready, S.nth(i, n))
                        for t in range(TILES):
                            eng.transpose(pT[n][:, t * P:(t + 1) * P], qk[n][:, t, 0:P], core.ident[:, :])
                        for t in range(TILES):
                            ins = eng.matmul(pM[n][:, 0:P], qk[n][:, t, P:2 * P], v[n][:, t, :],
                                             start=(t == 0), stop=(t == TILES - 1))
                        ins.then_inc(kv_in_psum, 1)
                    for n in range(2):
                        eng.wait_ge(kv_ready, S.nth(i, n))
                        eng.wait_ge(qT_ready, S.nth(i, n))
                        eng.matmul(pM[n][:, P:P + SEQ], kv[n][:, :], qT[n][:, :], start=True, stop=True)\
                           .then_inc(oT_in_psum, 1)
                    for n in range(2):
                        eng.wait_ge(oT_ready, S.nth(i, n))
                        for t in range(TILES):
                            ins = eng.matmul(y[n][:, t, :], oT[n][:, t * P:(t + 1) * P], wo[:, :], start=True, stop=True)
                        ins.then_inc(y_in_psum, 1)

            @block.scalar
            def _(eng):
                eng.wait_ge(weights_in, 64)
                eng.activation(v_factor[:, :], norm_const[:, :], ACT.Tanh, scale=0.5).then_inc(factor, 1)
                eng.wait_ge(mask_ready, 1)
                eng.activation(v_factor[:, :], v_factor[:, :], ACT.Exp).then_inc(factor, 1)
                with eng.Fori(0, S.turns) as i:
                    for n in range(2):
                        S.front_copy(eng, i, n, pT[n][:, 0:256])
                    for n in range(2):
                        eng.wait_ge(qkv_in_psum, S.nth(i, n))
                        eng.activation(sq[n][:, :, :], pQ[n][:, :, 0:2 * P], ACT.Square).then_inc(sq_ready, 1)
                    for n in range(2):
                        eng.wait_ge(n2_ready, S.nth(i, n))
                        eng.activation(n2[n][:, :], n2[n][:, :], ACT.Sqrt).then_inc(norm_ready, 1)
                    for n in range(2):
                        eng.wait_ge(kv_in_psum, S.nth(i, n))
                        eng.copy(qT[n][:, :], pT[n][:, 0:SEQ]).then_inc(qT_ready, 1)
                    for n in range(2):
                        eng.wait_ge(oT_in_psum, S.nth(i, n))
                        eng.copy(oT[n][:, :], pM[n][:, P:P + SEQ]).then_inc(oT_ready, 1)
        S.clear_semaphores()


L2_HEADS = 8
L2_HEAD = 64
L2_INNER = L2_HEADS * L2_HEAD
WINDOW = 64


def local_attn_stage(nc, core, W, depth):
    first = depth == 0
    H, D, HALF = L2_HEADS, L2_HEAD, L2_HEAD // 2
    with ExitStack() as ctx:
        S = Stage(nc, ctx, f"l2t{depth}", 2, core, src=None if first else core.Y)
        wqkv = S.sb("wqkv", [P, 3 * L2_INNER])
        wo = S.sb("wo", [P, 4, P])
        cos_f = S.sb("cos_f", [P, TILES, 2, D])
        sin_f = S.sb("sin_f", [P, TILES, 2, D])
        qk_scale = S.sb("qk_scale", [P, 2, D])
        qk_scale_rot = S.sb("qk_scale_rot", [P, 2, D])
        band = S.sb("band", [P, 128 + 192], BF16)
        ident16 = S.sb("ident16", [P, P], BF16)
        raw = [S.sb(f"raw{t}", [P, 2, L2_INNER]) for t in range(TILES)]
        sq = [S.sb(f"sq{t}", [P, 2, L2_INNER]) for t in range(TILES)]
        n2 = [S.sb(f"n2{t}", [P, 2 * H]) for t in range(TILES)]
        inv = [S.sb(f"inv{t}", [P, 2 * H]) for t in range(TILES)]
        direct = [S.sb(f"direct{t}", [P, 2, L2_INNER]) for t in range(TILES)]
        rotated = [S.sb(f"rotated{t}", [P, 2, L2_INNER]) for t in range(TILES)]
        kT = [S.sb(f"kT{n}", [P, 4, SEQ]) for n in range(2)]
        qT = [S.sb(f"qT{n}", [P, 2, 4, SEQ]) for n in range(2)]
        v = [S.sb(f"v{n}", [P, 3, H, D + 1]) for n in range(2)]
        prob = [S.sb(f"prob{k}", [P, 4, 192]) for k in range(2)]
        highest = [S.sb(f"highest{k}", [P, 4]) for k in range(2)]
        probT = [S.sb(f"probT{k}", [P, 2, 4 * P]) for k in range(2)]
        rden = [S.sb(f"rden{k}", [P, H]) for k in range(2)]
        o = [S.sb(f"o{k}", [P, L2_INNER]) for k in range(2)]
        oT = [S.sb(f"oT{k}", [P, 4, P]) for k in range(2)]
        y = [S.sb(f"y{k}", [P, P]) for k in range(2)]
        pQ = S.ps("pQ", [P, 2, 512])
        pT = [S.ps(f"pT{k}", [P, 512]) for k in range(2)]
        pS = S.ps("pS", [P, 2, 2, 256])
        pO = S.ps("pO", [P, 2, 512])
        units = [(n, t, g) for n in range(2) for t in range(TILES) for g in range(2)]
        U = len(units)
        HALF_U = U // 2
        FILLS = 7
        (weights_in, zeroed, tables_ready, fill_in_psum, fill_copied, n2_ready, inv_ready, parts_ready, sum_ready, qk_ready,
         passed_in_psum, passed_copied, scores_in_psum, below_ready, prob_ready, o_in_psum, o_ready,
         y_added) = (S.sem(s) for s in (
             "weights_in", "zeroed", "tables_ready", "fill_in_psum", "fill_copied", "n2_ready", "inv_ready", "parts_ready",
             "sum_ready", "qk_ready", "passed_in_psum", "passed_copied", "scores_in_psum", "below_ready", "prob_ready",
             "o_in_psum", "o_ready", "y_added"))

        def blocks(t):
            return [(0, 128, 0)] if t == 0 else [(64, 192, 2), (0, 64, 1)]

        LEFT = [("y", 2), ("o", 3), ("y", 3)]

        def steps(u, more, left):
            out = []
            if u < U:
                out += [("prob", u, b) for b in range(len(blocks(units[u][1])))]
                lane = 1 - u // HALF_U
                if u % HALF_U == 0:
                    out += [("qk", 1 - lane, 1, a) for a in range(2)]
                if u % HALF_U == 2 and (lane == 1 or more):
                    out += [("qk", lane, 0, a) for a in range(2)]
                if u % HALF_U == 2 and more:
                    out += [("rows", 1 - lane)]
                if u % 2 == 1 and u >= 3:
                    out += [("o", (u - 3) // 2)]
                if u % 2 == 0 and u >= 4:
                    out += [("y", (u - 4) // 2)]
                if left and u < len(LEFT):
                    out += [("left",) + LEFT[u]]
            return out

        BEFORE = [("rows", 0), ("qk", 0, 0, 0), ("qk", 0, 0, 1), ("rows", 1)]

        def order(more, left):
            return [x for u in range(U) for x in steps(u, more, left)]

        FIRST, PASSED = len(order(True, False)), len(order(True, True))
        assert PASSED % 2 == 0
        AFTER_LAST = PASSED - order(True, True).index(("prob", U - 1, 0))

        def passed(i, more, what):
            if i is None:
                at = len(BEFORE) + FIRST + (S.turns - 2) * PASSED + len(order(False, True)) + LEFT.index(what[1:])
                return at, (len(BEFORE) + FIRST + len(order(False, True)) + LEFT.index(what[1:])) % 2
            left = not isinstance(i, int) or i > 0
            at = len(BEFORE) + order(more, left).index(what)
            if not left:
                return at, at % 2
            return (i - 1) * PASSED + (FIRST + at), (FIRST + at) % 2

        def fill(i, lane, f):
            return i * (2 * FILLS) + (lane * FILLS + f), (lane * FILLS + f) % 2

        def fills_of(t):
            return ([(0, 0), (1, 1)], [(2, 0, 0, 128), (3, 1, 64, 128)]) if t == 0 else ([(4, 0), (5, 1)], [(6, 2, 128, 256)])

        def tile_no(i, lane, t):
            return i * 4 + (2 * lane + t + 1)

        def beside(i, u):
            return (i, 1) if u < HALF_U else (i + 1, 0)

        with nc.Block() as block:
            @block.sync
            def _(eng):
                eng.dma_start(wqkv[:, :], W["L2_ffn_wqkv"][depth]).then_inc(weights_in, 16)
                eng.dma_start(wo[:, :, :], W["L2_ffn_wo"][depth].rearrange("(k p) n -> p k n", p=P)).then_inc(weights_in, 16)
                eng.dma_start(cos_f[:, :, :, :], W["xpos_cos"]).then_inc(weights_in, 16)
                eng.dma_start(sin_f[:, :, :, :], W["xpos_sin"]).then_inc(weights_in, 16)
                eng.dma_start(qk_scale[:, :, :], W["L2_ffn_qk_scale"][depth].partition_broadcast(P)).then_inc(weights_in, 16)
                eng.dma_start(qk_scale_rot[:, :, :], W["L2_ffn_qk_scale_rot"][depth].partition_broadcast(P))\
                   .then_inc(weights_in, 16)
                eng.dma_start(band[:, :], W["band_mask"]).then_inc(weights_in, 16)
                eng.dma_start(ident16[:, :], W["ident16"]).then_inc(weights_in, 16)
                eng.wait_ge(weights_in, 128)

            @block.vector
            def _(eng):
                chain = Chain(eng, S.v_chain)
                for n in range(2):
                    eng.memset(v[n][:, :, :, D:D + 1], 1.0)
                    eng.memset(S.xT[n][64:128, 0:1], 0.0)
                eng.wait_ge(weights_in, 128)
                for t in range(TILES):
                    eng.tensor_tensor(cos_f[:, t, :, :], cos_f[:, t, :, :], qk_scale[:, :, :], ALU.mult)
                    ins = eng.tensor_tensor(sin_f[:, t, :, :], sin_f[:, t, :, :], qk_scale_rot[:, :, :], ALU.mult)
                ins.then_inc(tables_ready, 1)
                eng.wait_ge(tables_ready, 1)

                def front_first(i, lane):
                    if first:
                        S.front_stats(eng, chain, i, lane)

                def front_second(i, lane):
                    if first:
                        S.front_apply(eng, i, lane)
                        eng.wait_ge(S.xn_ready, S.nth(i, lane))
                        for t in range(TILES):
                            eng.tensor_copy(S.of(core.Y, i, lane, t), S.xn[lane][:, t, :])
                    else:
                        for t in range(TILES):
                            ins = eng.tensor_copy(S.xn[lane][:, t, :], S.rows(i, lane, t))
                        ins.then_inc(S.xn_ready, 1)

                def parts(i, lane, t):
                    qk, _ = fills_of(t)
                    eng.wait_ge(fill_copied, fill(i, lane, qk[1][0])[0] + 1)
                    chain.link(eng.tensor_reduce(n2[t][:, :], sq[t][:, :, :].rearrange("p a (h d) -> p (a h) d", h=H),
                                                 AX.X, ALU.add))
                    eng.tensor_scalar(n2[t][:, :], n2[t][:, :], 1e-24, None, ALU.max).then_inc(n2_ready, 1)
                    for a in range(2):
                        q4 = raw[t][:, a, :].rearrange("p (h s d) -> p h s d", h=H, s=2)
                        r4 = rotated[t][:, a, :].rearrange("p (h s d) -> p h s d", h=H, s=2)
                        for s in range(2):
                            eng.tensor_tensor(r4[:, :, s, :], q4[:, :, 1 - s, :],
                                              sin_f[:, t, a, s * HALF:(s + 1) * HALF].unsqueeze(1).to_broadcast([P, H, HALF]),
                                              ALU.mult)
                        ins = eng.tensor_tensor(direct[t][:, a, :].rearrange("p (h d) -> p h d", h=H),
                                                raw[t][:, a, :].rearrange("p (h d) -> p h d", h=H),
                                                cos_f[:, t, a, :].unsqueeze(1).to_broadcast([P, H, D]), ALU.mult)
                    ins.then_inc(parts_ready, 1)

                def normed(i, lane, t):
                    eng.wait_ge(sum_ready, tile_no(i, lane, t))
                    eng.wait_ge(inv_ready, tile_no(i, lane, t))
                    heads = direct[t][:, :, :].rearrange("p a (h d) -> p (a h) d", h=H)
                    eng.tensor_tensor(heads, heads, inv[t][:, :].unsqueeze(2).to_broadcast([P, 2 * H, D]), ALU.mult)\
                       .then_inc(qk_ready, 1)

                def finish(i, more, last):
                    def outputs(k):
                        eng.wait_ge(o_in_psum, last * 4 + (k + 1))
                        o4 = pO[:, :, 0:4 * (D + 1)].rearrange("p b (h d) -> p b h d", h=4)
                        chain.link(eng.reciprocal(rden[k % 2][:, :].rearrange("p (b h) -> p b h", b=2), o4[:, :, :, D]))
                        eng.tensor_tensor(o[k % 2][:, :].rearrange("p (b h d) -> p b h d", b=2, h=4), o4[:, :, :, 0:D],
                                          rden[k % 2][:, :].rearrange("p (b h) -> p b h", b=2).unsqueeze(3)
                                          .to_broadcast([P, 2, 4, D]), ALU.mult).then_inc(o_ready, 1)

                    def add_y(k, left):
                        eng.wait_ge(passed_copied, passed(i, more, (("left",) if left else ()) + ("y", k))[0] + 1)
                        rows = S.of(core.Y, last, k // TILES, k % TILES)
                        eng.tensor_tensor(rows, rows, y[k % 2][:, :], ALU.add).then_inc(y_added, 1)

                    return outputs, add_y

                def turn(i, more, last):
                    outputs, add_y = finish(i, more, i)
                    for u, (n, t, g) in enumerate(units):
                        K = 128 + 64 * t
                        for par in range(2):
                            eng.wait_ge(scores_in_psum, i * (2 * U) + (2 * u + par + 1))
                            two = slice(2 * par, 2 * par + 2)
                            chain.link(eng.tensor_reduce(highest[u % 2][:, two], pS[:, par, :, 0:K], AX.X, ALU.max))
                            eng.tensor_tensor(prob[u % 2][:, two, 0:K], pS[:, par, :, 0:K],
                                              highest[u % 2][:, two].unsqueeze(2).to_broadcast([P, 2, K]),
                                              ALU.subtract).then_inc(below_ready, 1)
                        ahead, lane = beside(i, u)
                        if u % HALF_U == 0 and more:
                            front_first(i + 1, 1 - lane)
                        if u % HALF_U == 1 and more:
                            front_second(i + 1, 1 - lane)
                        if u % HALF_U == 0:
                            normed(i, 1 - lane, 1)
                        elif u % HALF_U == 2 and (lane == 1 or more):
                            normed(ahead, lane, 0)
                        elif lane == 1 or more:
                            parts(ahead, lane, u % HALF_U // 2)
                        if u % 2 == 0 and u >= 2:
                            outputs(u // 2 - 1)
                        if u % 2 == 1 and u >= 5:
                            add_y((u - 5) // 2, False)
                        if last is not None:
                            outputs_left, add_y_left = finish(i, more, last)
                            if u == 0:
                                outputs_left(3)
                            if u in (1, 3):
                                add_y_left(2 if u == 1 else 3, True)
                    chain.restart()

                front_first(0, 0)
                front_first(0, 1)
                front_second(0, 0)
                front_second(0, 1)
                for t in range(TILES):
                    parts(0, 0, t)
                normed(0, 0, 0)
                chain.restart()
                turn(0, True, None)
                with eng.Fori(1, S.turns - 1) as i:
                    turn(i, True, i - 1)
                turn(S.turns - 1, False, S.turns - 2)
                outputs, add_y = finish(None, False, S.turns - 1)
                outputs(3)
                add_y(2, True)
                add_y(3, True)

            @block.gpsimd
            def _(eng):
                chain = Chain(eng, S.p_chain)
                for n in range(2):
                    eng.memset(qT[n][:, :, :, :], 0.0).then_inc(zeroed, 1)
                eng.wait_ge(zeroed, 2)

                def front(i, lane):
                    if first:
                        S.front_rstd(eng, chain, i, lane)

                def tile(i, lane, t):
                    eng.wait_ge(n2_ready, tile_no(i, lane, t))
                    eng.tensor_tensor(inv[t][:, :], n2[t][:, :], core.minus_half[:, 0:2 * H], ALU.pow).then_inc(inv_ready, 1)
                    eng.wait_ge(parts_ready, tile_no(i, lane, t))
                    eng.tensor_tensor(direct[t][:, :, :], direct[t][:, :, :], rotated[t][:, :, :], ALU.add)\
                       .then_inc(sum_ready, 1)

                def turn(i, more, last):
                    for half in range(2):
                        ahead, lane = beside(i, half * HALF_U)
                        if more:
                            front(i + 1, 1 - lane)
                        if lane == 1 or more:
                            for t in range(TILES):
                                tile(ahead, lane, t)
                    chain.restart()

                front(0, 0)
                front(0, 1)
                for t in range(TILES):
                    tile(0, 0, t)
                chain.restart()
                turn(0, True, None)
                with eng.Fori(1, S.turns - 1) as i:
                    turn(i, True, i - 1)
                turn(S.turns - 1, False, S.turns - 2)

            @block.tensor
            def _(eng):
                eng.wait_ge(weights_in, 128)

                def scores(i, u, qk_passed=None):
                    n, t, g = units[u]
                    if qk_passed is not None:
                        eng.wait_ge(passed_copied, qk_passed + 1)
                    lo = 64 * t
                    K = 128 + 64 * t
                    for par in range(2):
                        before = 2 * u - 1 + par
                        if u or not isinstance(i, int) or i:
                            eng.wait_ge(below_ready, i * (2 * U) + before)
                        for j in range(2):
                            h = 4 * g + 2 * j + par
                            eng.matmul(pS[:, par, j, 0:K], qT[n][:, par, h // 2, t * P:(t + 1) * P],
                                       kT[n][:, h // 2, lo:lo + K], start=(j == 0), stop=True,
                                       skip_group_check=(j != 0))
                        m = band[:, 0:128] if t == 0 else band[:, 128:320]
                        for j in range(2):
                            ins = eng.matmul(pS[:, par, j, 0:K], ident16[:, :], m, start=False, stop=True,
                                             skip_group_check=True)
                        ins.then_inc(scores_in_psum, 1)

                def bank(at, which):
                    if not isinstance(at, int) or at >= 2:
                        eng.wait_ge(passed_copied, at - 1)
                    return pT[which]

                def project(i, lane, t):
                    qk, vals = fills_of(t)
                    if t == 0:
                        eng.wait_ge(S.xT_ready, S.nth(i, lane))
                    for f, a in qk:
                        at, which = fill(i, lane, f)
                        if not isinstance(at, int) or at >= 2:
                            eng.wait_ge(fill_copied, at - 1)
                        eng.matmul(pQ[:, which, :], S.xT[lane][:, t * P:(t + 1) * P],
                                   wqkv[:, a * L2_INNER:(a + 1) * L2_INNER], start=True, stop=True).then_inc(fill_in_psum, 1)
                    for f, _, lo, hi in vals:
                        at, which = fill(i, lane, f)
                        eng.wait_ge(fill_copied, at - 1)
                        eng.matmul(pQ[0:hi - lo, which, :], S.xT[lane][:, lo:hi], wqkv[:, 2 * L2_INNER:3 * L2_INNER],
                                   start=True, stop=True).then_inc(fill_in_psum, 1)

                def turn_qk(i, lane, t, places):
                    eng.wait_ge(qk_ready, tile_no(i, lane, t))
                    for a in range(2):
                        out = bank(*places[a])
                        for ch in range(4):
                            ins = eng.transpose(out[:, ch * P:(ch + 1) * P], direct[t][:, a, ch * P:(ch + 1) * P],
                                                core.ident[:, :])
                        ins.then_inc(passed_in_psum, 1)

                def rows(i, lane, place):
                    eng.wait_ge(S.xn_ready, S.nth(i, lane))
                    out = bank(*place)
                    for t in range(TILES):
                        ins = eng.transpose(out[:, t * P:(t + 1) * P], S.xn[lane][:, t, :], core.ident[:, :])
                    ins.then_inc(passed_in_psum, 1)

                def weigh(i, u, first_prob):
                    n, t, g = units[u]
                    if g == 0:
                        eng.wait_ge(fill_copied, fill(i, n, FILLS - 1 if t else 3)[0] + 1)
                        if u or not isinstance(i, int) or i:
                            eng.wait_ge(o_ready, i * 4 + u // 2)
                    for b, (lo, hi, kb) in enumerate(blocks(t)):
                        eng.wait_ge(passed_copied, first_prob + (b + 1))
                        for r in range(4):
                            hh = 2 * (r % 2) + r // 2
                            ins = eng.matmul(pO[:, g, hh * (D + 1):(hh + 1) * (D + 1)],
                                             probT[u % 2][0:hi - lo, b, r * P:(r + 1) * P],
                                             v[n][0:hi - lo, kb, 4 * g + hh, :], start=(b == 0 and r == 0), stop=True,
                                             skip_group_check=not (b == 0 and r == 0))
                    if g == 1:
                        ins.then_inc(o_in_psum, 1)

                def pass_on(i, more, of, what):
                    left = what[0] == "left"
                    kind, k = what[-2:]
                    if kind == "o":
                        eng.wait_ge(o_ready, of * 4 + (k + 1))
                        out = bank(*passed(i, more, what))
                        for c in range(4):
                            ins = eng.transpose(out[:, c * P:(c + 1) * P], o[k % 2][:, c * P:(c + 1) * P],
                                                core.ident[:, :])
                    else:
                        at, which = passed(i, more, what)
                        eng.wait_ge(passed_copied, at)
                        out = pT[which]
                        for c in range(4):
                            ins = eng.matmul(out[:, 0:P], oT[k % 2][:, c, :], wo[:, c, :], start=(c == 0), stop=(c == 3))
                    ins.then_inc(passed_in_psum, 1)

                def turn(i, more, last):
                    def place(what):
                        return passed(i, more, what)

                    left = last is not None
                    for u, (n, t, g) in enumerate(units):
                        if u == U - 1:
                            if more:
                                scores(i + 1, 0, place(("qk", 0, 0, 1))[0])
                        elif u + 1 == 2:
                            scores(i, u + 1, place(("qk", 0, 1, 1))[0])
                        elif u + 1 == 4:
                            scores(i, u + 1, place(("qk", 1, 0, 1))[0])
                        elif u + 1 == 6:
                            scores(i, u + 1, place(("qk", 1, 1, 1))[0])
                        else:
                            scores(i, u + 1)
                        eng.wait_ge(prob_ready, i * U + (u + 1))
                        for what in steps(u, more, left):
                            if what[0] == "prob":
                                lo, hi, _ = blocks(t)[what[2]]
                                at, which = place(what)
                                out = pT[which]
                                if what[2] == 0:
                                    eng.wait_ge(passed_copied, at - 1 + (len(blocks(t)) - 1))
                                for r in range(4):
                                    ins = eng.transpose(out[0:hi - lo, r * P:(r + 1) * P], prob[u % 2][:, r, lo:hi],
                                                        core.ident[:, :])
                                ins.then_inc(passed_in_psum, 1)
                        if u:
                            weigh(i, u - 1, place(("prob", u - 1, 0))[0])
                        elif left:
                            weigh(last, U - 1, place(("prob", 0, 0))[0] - AFTER_LAST)
                        ahead, lane = beside(i, u)
                        if u % HALF_U < 2 and (lane == 1 or more):
                            project(ahead, lane, u % HALF_U)
                        for what in steps(u, more, left):
                            if what[0] == "qk" and what[3] == 0:
                                of = i if what[1] == n or what[1] == 1 else i + 1
                                turn_qk(of, what[1], what[2], [place(what), place(what[:3] + (1,))])
                            elif what[0] == "rows":
                                rows(i + 1, what[1], place(what))
                            elif what[0] in ("o", "y"):
                                pass_on(i, more, i, what)
                            elif what[0] == "left":
                                pass_on(i, more, last, what)

                rows(0, 0, (0, 0))
                project(0, 0, 0)
                project(0, 0, 1)
                turn_qk(0, 0, 0, [(1, 1), (2, 0)])
                rows(0, 1, (3, 1))
                scores(0, 0, 2)
                turn(0, True, None)
                with eng.Fori(1, S.turns - 1) as i:
                    turn(i, True, i - 1)
                turn(S.turns - 1, False, S.turns - 2)
                end = S.turns - 1
                weigh(end, U - 1, passed(end, False, ("prob", U - 1, 0))[0])
                for what in LEFT:
                    pass_on(None, False, end, ("left",) + what)

            @block.scalar
            def _(eng):
                eng.wait_ge(tables_ready, 1)
                eng.wait_ge(zeroed, 2)

                def fills(i, lane, t):
                    qk, vals = fills_of(t)
                    for f, a in qk:
                        at, which = fill(i, lane, f)
                        eng.wait_ge(fill_in_psum, at + 1)
                        eng.copy(raw[t][:, a, :], pQ[:, which, :])
                        eng.activation(sq[t][:, a, :], pQ[:, which, :], ACT.Square).then_inc(fill_copied, 1)
                    for f, j, lo, hi in vals:
                        at, which = fill(i, lane, f)
                        eng.wait_ge(fill_in_psum, at + 1)
                        eng.copy(v[lane][0:hi - lo, j, :, 0:D], pQ[0:hi - lo, which, :].rearrange("p (h d) -> p h d", h=H))\
                           .then_inc(fill_copied, 1)

                def turned(lane, t, a, place):
                    at, which = place
                    eng.wait_ge(passed_in_psum, at + 1)
                    at_t = slice(t * P, (t + 1) * P)
                    src = pT[which][:, :].rearrange("p (j s) -> p j s", j=4)
                    if a == 0:
                        eng.copy(qT[lane][0:64, 0, :, at_t], src[0:64])
                        eng.copy(qT[lane][64:128, 1, :, at_t], src[64:128]).then_inc(passed_copied, 1)
                    else:
                        eng.copy(kT[lane][:, :, at_t], src).then_inc(passed_copied, 1)

                def rows(lane, place):
                    at, which = place
                    eng.wait_ge(passed_in_psum, at + 1)
                    eng.copy(S.xT[lane][0:64, :], pT[which][0:64, 0:SEQ])
                    eng.copy(S.xT[lane][64:128, 1:SEQ], pT[which][64:128, 0:SEQ - 1]).then_inc(passed_copied, 1)
                    eng.wait_ge(passed_copied, at + 1)
                    eng.sem_inc(S.xT_ready, 1)

                def copy_passed(i, more, what, of=None):
                    at, which = passed(i, more, what)
                    kind, k = what[-2:]
                    eng.wait_ge(passed_in_psum, at + 1)
                    if kind == "o":
                        ins = eng.copy(oT[k % 2][:, :, :], pT[which][:, :].rearrange("p (c s) -> p c s", c=4))
                    else:
                        if k >= 2:
                            eng.wait_ge(y_added, (S.turns - 1 if i is None else of) * 4 + (k - 1))
                        ins = eng.copy(y[k % 2][:, :], pT[which][:, 0:P])
                    ins.then_inc(passed_copied, 1)

                def turn(i, more, last):
                    for u, (n, t, g) in enumerate(units):
                        K = 128 + 64 * t
                        eng.wait_ge(below_ready, i * (2 * U) + (2 * u + 2))
                        eng.activation(prob[u % 2][:, :, 0:K], prob[u % 2][:, :, 0:K], ACT.Exp, scale=8.0)\
                           .then_inc(prob_ready, 1)
                        now = steps(u, more, last is not None)
                        for what in now:
                            if what[0] == "prob":
                                at, which = passed(i, more, what)
                                lo, hi, _ = blocks(t)[what[2]]
                                eng.wait_ge(passed_in_psum, at + 1)
                                eng.copy(probT[u % 2][0:hi - lo, what[2], :], pT[which][0:hi - lo, :])\
                                   .then_inc(passed_copied, 1)
                        ahead, lane = beside(i, u)
                        if u % HALF_U < 2 and (lane == 1 or more):
                            fills(ahead, lane, u % HALF_U)
                        for what in now:
                            if what[0] == "qk":
                                turned(what[1], what[2], what[3], passed(i, more, what))
                            elif what[0] == "rows":
                                rows(what[1], passed(i, more, what))
                            elif what[0] == "left":
                                copy_passed(i, more, what, last)
                            elif what[0] != "prob":
                                copy_passed(i, more, what, i)

                rows(0, (0, 0))
                fills(0, 0, 0)
                fills(0, 0, 1)
                for a in range(2):
                    turned(0, 0, a, (1 + a, 1 - a))
                rows(1, (3, 1))
                turn(0, True, None)
                with eng.Fori(1, S.turns - 1) as i:
                    turn(i, True, i - 1)
                turn(S.turns - 1, False, S.turns - 2)
                for what in LEFT:
                    copy_passed(None, False, ("left",) + what)
        S.clear_semaphores()


GLU = 3


def glu_stage(nc, core, W, depth):
    last = depth == 1
    T = 4
    N = T * P
    with ExitStack() as ctx:
        S = Stage(nc, ctx, f"l2g{depth}", 1, core, tiles=T, src=core.Y)
        w1 = S.sb("w1", [P, 2 * GLU * P])
        w2 = S.sb("w2", [P, GLU, P])
        b1 = S.sb("b1", [P, 2 * GLU])
        b2 = S.sb("b2", [P, P])
        ln_g = S.sb("ln_g", [P, 1])
        ln_b = S.sb("ln_b", [P, 1])
        before = S.sb("before", [P, P])
        before_tile = S.sb("before_tile", [P, P])
        gated = [S.sb(f"gated{k}", [P, GLU, N]) for k in range(2)]
        gelu = [S.sb(f"gelu{k}", [P, N]) for k in range(2)]
        pR = S.ps("pR", [P, N])
        pX = S.ps("pX", [P, N])
        pA = [S.ps(f"pA{k}", [P, N]) for k in range(2)]
        pG = [S.ps(f"pG{k}", [P, N]) for k in range(2)]
        pY = S.ps("pY", [P, N])
        rows3 = pR[:, :].rearrange("p (t c) -> p t c", t=T)
        (weights_in, weights_ready, b1_in_psum, rows_in_psum, hidden_in_psum, gelu_ready, gated_ready,
         y_in_psum) = (S.sem(s) for s in ("weights_in", "weights_ready", "b1_in_psum", "rows_in_psum",
                                          "hidden_in_psum", "gelu_ready", "gated_ready", "y_in_psum"))
        with nc.Block() as block:
            @block.sync
            def _(eng):
                eng.dma_start(w1[:, :], W["L2_ffn_w1"][depth]).then_inc(weights_in, 16)
                eng.dma_start(w2[:, :, :], W["L2_ffn_w2"][depth].rearrange("(k p) n -> p k n", p=P)).then_inc(weights_in, 16)
                eng.dma_start(b1[:, :], W["L2_ffn_b1"][depth]).then_inc(weights_in, 16)
                eng.dma_start(b2[:, :], W["L2_ffn_b2"][depth].partition_broadcast(P)).then_inc(weights_in, 16)
                eng.dma_start(ln_g[:, :], W["L2_ffn_ln_g"][depth]).then_inc(weights_in, 16)
                eng.dma_start(ln_b[:, :], W["L2_ffn_ln_b"][depth]).then_inc(weights_in, 16)
                eng.dma_start(before[:, :], W["row_before"]).then_inc(weights_in, 16)
                eng.dma_start(before_tile[:, :], W["row_before_tile"]).then_inc(weights_in, 16)
                eng.wait_ge(weights_in, 128)

            @block.vector
            def _(eng):
                chain = Chain(eng, S.v_chain)
                eng.wait_ge(weights_in, 128)
                eng.wait_ge(b1_in_psum, 1)
                eng.tensor_tensor(b1[:, :], b1[:, :], pY[:, 0:2 * GLU], ALU.add)
                eng.tensor_scalar(w1[:, :], w1[:, :], ln_g[:, 0:1], None, ALU.mult).then_inc(weights_ready, 1)
                eng.wait_ge(weights_ready, 1)

                def front(i):
                    eng.wait_ge(rows_in_psum, i + 1)
                    for t in range(T):
                        ins = eng.bn_stats(S.stats[:, 0, t, :], rows3[:, t, :])
                    chain.link(ins)
                    for t in range(T):
                        ins = eng.bn_aggr(S.mv[:, 0, t, :], S.stats[:, 0, t, :])
                    ins.then_inc(S.mv_ready, 1)
                    eng.wait_ge(S.rstd_ready, i + 1)
                    for t in range(T):
                        ins = eng.tensor_scalar(S.xn[0][:, t, :], rows3[:, t, :], S.mv[:, 0, t, 0:1],
                                                S.rstd[:, 0, t:t + 1], ALU.subtract, ALU.mult)
                    ins.then_inc(S.xn_ready, 1)

                def turn(i, between):
                    for c in range(GLU):
                        eng.wait_ge(gelu_ready, i * GLU + (c + 1))
                        eng.scalar_tensor_tensor(out=gated[0][:, c, :], in0=pA[c % 2][:, :], scalar=b1[:, c:c + 1],
                                                 in1=gelu[c % 2][:, :], op0=ALU.add, op1=ALU.mult).then_inc(gated_ready, 1)
                    between()
                    r = S.r[0]
                    eng.wait_ge(y_in_psum, i + 1)
                    chain.link(eng.tensor_tensor(r[:, :, :], pY[:, :].rearrange("p (t c) -> p t c", t=T),
                                                 b2[:, :].unsqueeze(1).to_broadcast([P, T, P]), ALU.add))
                    for t in range(T):
                        out = r[:, t, :] if last else S.of(core.Y, i, 0, t)
                        ins = eng.tensor_tensor(out, r[:, t, :], S.rows(i, 0, t), ALU.add)
                    chain.link(ins)
                    if last:
                        S.back_norm_stats(eng, chain, 0, r)
                        S.back_residual(eng, chain, i, 0, r)
                    chain.restart()

                front(0)
                chain.restart()
                with eng.Fori(0, S.turns - 1) as i:
                    turn(i, lambda: front(i + 1))
                turn(S.turns - 1, lambda: None)

            @block.gpsimd
            def _(eng):
                chain = Chain(eng, S.p_chain)

                def turn(i, between):
                    between()
                    if last:
                        S.back_rstd_step(eng, chain, i, 0)
                    chain.restart()

                S.front_rstd(eng, chain, 0, 0)
                chain.restart()
                with eng.Fori(0, S.turns - 1) as i:
                    turn(i, lambda: S.front_rstd(eng, chain, i + 1, 0))
                turn(S.turns - 1, lambda: None)

            @block.tensor
            def _(eng):
                eng.wait_ge(weights_in, 128)
                for c in range(2 * GLU):
                    ins = eng.matmul(pY[:, c:c + 1], w1[:, c * P:(c + 1) * P], ln_b[:, :], start=True, stop=True)
                ins.then_inc(b1_in_psum, 1)
                eng.wait_ge(weights_ready, 1)

                def shift(i):
                    for t in range(T):
                        x = S.rows(i, 0, t)
                        eng.matmul(rows3[:, t, 0:64], core.ident[:, :], x[:, 0:64], start=(t == 0), stop=True,
                                   skip_group_check=(t != 0))
                        ins = eng.matmul(rows3[:, t, 64:P], before[:, :], x[:, 64:P], start=False, stop=True,
                                         skip_group_check=True)
                        if t % TILES:
                            ins = eng.matmul(rows3[:, t, 64:P], before_tile[:, :], S.rows(i, 0, t - 1)[:, 64:P],
                                             start=False, stop=True, skip_group_check=True)
                    ins.then_inc(rows_in_psum, 1)

                def turn(i, between):
                    S.front_transpose(eng, i, 0, pX)
                    eng.wait_ge(S.xT_ready, i + 1)
                    for c in range(GLU):
                        if c >= 2:
                            eng.wait_ge(gated_ready, i * GLU + (c - 1))
                        eng.matmul(pG[c % 2][:, :], w1[:, (GLU + c) * P:(GLU + c + 1) * P], S.xT[0][:, :], start=True, stop=True)
                        eng.matmul(pA[c % 2][:, :], w1[:, c * P:(c + 1) * P], S.xT[0][:, :], start=True, stop=True)\
                           .then_inc(hidden_in_psum, 1)
                    between()
                    eng.wait_ge(gated_ready, i * GLU + GLU)
                    for t in range(T):
                        for c in range(GLU):
                            ins = eng.matmul(pY[:, t * P:(t + 1) * P], gated[0][:, c, t * P:(t + 1) * P], w2[:, c, :],
                                             start=(c == 0), stop=(c == GLU - 1))
                    ins.then_inc(y_in_psum, 1)

                shift(0)
                with eng.Fori(0, S.turns - 1) as i:
                    turn(i, lambda: shift(i + 1))
                turn(S.turns - 1, lambda: None)

            @block.scalar
            def _(eng):
                eng.wait_ge(weights_ready, 1)
                with eng.Fori(0, S.turns) as i:
                    S.front_copy(eng, i, 0, pX[:, :])
                    for c in range(GLU):
                        eng.wait_ge(hidden_in_psum, i * GLU + (c + 1))
                        eng.activation(gelu[c % 2][:, :], pG[c % 2][:, :], ACT.Gelu, bias=b1[:, GLU + c:GLU + c + 1])\
                           .then_inc(gelu_ready, 1)
        S.clear_semaphores()


def local_stage(nc, core, W):
    with ExitStack() as ctx:
        inner_rows(nc, ctx, core, "l2f_rows")
        for depth in range(2):
            local_attn_stage(nc, core, W, depth)
            glu_stage(nc, core, W, depth)


def dense_ffn_stage(nc, core, W):
    FC = 4
    with ExitStack() as ctx:
        S = Stage(nc, ctx, "l3f", 2, core)
        w1 = S.sb("w1", [P, FC * P])
        b1 = S.sb("b1", [P, FC])
        w2 = S.sb("w2", [P, FC, P])
        b2 = S.sb("b2", [P, P])
        hT = [S.sb(f"hT{k}", [P, FC, SEQ]) for k in range(2)]
        pT = [S.ps(f"pT{k}", [P, 512]) for k in range(2)]
        pH = [S.ps(f"pH{k}", [P, FC * SEQ]) for k in range(2)]
        weights_in, h_in_psum, h_ready, y_in_psum = (S.sem(n) for n in ("weights_in", "h_in_psum", "h_ready", "y_in_psum"))
        with nc.Block() as block:
            @block.sync
            def _(eng):
                eng.dma_start(w1[:, :], W["L3_ffn_w1"]).then_inc(weights_in, 16)
                eng.dma_start(b1[:, :], W["L3_ffn_b1"]).then_inc(weights_in, 16)
                eng.dma_start(w2[:, :, :], W["L3_ffn_w2"].rearrange("(k p) n -> p k n", p=P)).then_inc(weights_in, 16)
                eng.dma_start(b2[:, :], W["L3_ffn_b2"].partition_broadcast(P)).then_inc(weights_in, 16)
                eng.wait_ge(weights_in, 64)

            @block.vector
            def _(eng):
                chain = Chain(eng, S.v_chain)
                eng.wait_ge(weights_in, 64)
                with eng.Fori(0, S.turns) as i:
                    for n in range(2):
                        S.front_stats(eng, chain, i, n)
                    for n in range(2):
                        S.front_apply(eng, i, n)
                    for n in range(2):
                        eng.wait_ge(y_in_psum, S.nth(i, n))
                        for t in range(TILES):
                            ins = eng.tensor_tensor(S.r[n][:, t, :], pT[n][:, 256 + t * P:256 + (t + 1) * P], b2[:, :], ALU.add)
                        chain.link(ins)
                        S.back_norm_stats(eng, chain, n, S.r[n])
                    for n in range(2):
                        S.back_residual(eng, chain, i, n, S.r[n])
                    chain.restart()

            @block.gpsimd
            def _(eng):
                chain = Chain(eng, S.p_chain)
                with eng.Fori(0, S.turns) as i:
                    for n in range(2):
                        S.front_rstd(eng, chain, i, n)
                    for n in range(2):
                        S.back_rstd_step(eng, chain, i, n)
                    chain.restart()

            @block.tensor
            def _(eng):
                eng.wait_ge(weights_in, 64)
                with eng.Fori(0, S.turns) as i:
                    for n in range(2):
                        S.front_transpose(eng, i, n, pT[n][:, 0:256])
                    for n in range(2):
                        eng.wait_ge(S.xT_ready, S.nth(i, n))
                        for c in range(FC):
                            ins = eng.matmul(pH[n][:, c * SEQ:(c + 1) * SEQ], w1[:, c * P:(c + 1) * P], S.xT[n][:, :],
                                             start=True, stop=True)
                        ins.then_inc(h_in_psum, 1)
                    for n in range(2):
                        eng.wait_ge(h_ready, S.nth(i, n))
                        for t in range(TILES):
                            for c in range(FC):
                                ins = eng.matmul(pT[n][:, 256 + t * P:256 + (t + 1) * P], hT[n][:, c, t * P:(t + 1) * P],
                                                 w2[:, c, :], start=(c == 0), stop=(c == FC - 1))
                        ins.then_inc(y_in_psum, 1)

            @block.scalar
            def _(eng):
                eng.wait_ge(weights_in, 64)
                with eng.Fori(0, S.turns) as i:
                    for n in range(2):
                        S.front_copy(eng, i, n, pT[n][:, 0:256])
                    for n in range(2):
                        eng.wait_ge(h_in_psum, S.nth(i, n))
                        for c in range(FC):
                            ins = eng.activation(hT[n][:, c, :], pH[n][:, c * SEQ:(c + 1) * SEQ], ACT.Gelu,
                                                 bias=b1[:, c:c + 1])
                        ins.then_inc(h_ready, 1)
        S.clear_semaphores()


STAGES = {"l0a": mamba_stage, "l0f": routed_block_stage, "l1a": bond_attn_stage, "l1f": expert_ffn_stage,
          "l2a": linear_attn_stage, "l2f": local_stage, "l3a": alibi_attn_stage, "l3f": dense_ffn_stage}
ORDER = ["l0a", "l0f", "l1a", "l1f", "l2a", "l2f", "l3a", "l3f"]


def program(nc, x, W, out, n_seq, stages):
    with ExitStack() as ctx:
        core = Core(nc, ctx, n_seq)
        load_stage(nc, core, x)
        for s in stages:
            STAGES[s](nc, core, W)
        store_stage(nc, core, out)


def layout(inputs):
    import numpy as np
    a = {k: np.asarray(v) for k, v in inputs.items()}
    w = {}
    for n in ("w1", "w2", "b2"):
        w[f"L3_ffn_{n}"] = a[f"L3_ffn_{n}"]
    two = lambda m: m.reshape(2, 128, -1).transpose(1, 0, 2)
    w["L0_attn_in_proj"] = a["L0_attn_in_proj_w"].T
    w["L0_attn_conv_w"] = a["L0_attn_conv_w"].transpose(1, 2, 0).reshape(2, 128, 4, 256).transpose(1, 0, 2, 3)
    w["L0_attn_dt_w"] = two(a["L0_attn_dt_w"].T)
    bc = np.concatenate([a["L0_attn_B_w"], a["L0_attn_C_w"]]).T
    w["L0_attn_bc_w"] = two(np.concatenate([bc, np.zeros_like(bc), bc, bc], axis=1))
    w["L0_attn_out_w"] = two(a["L0_attn_out_w"].T)
    for n in ("conv_b", "dt_b", "D"):
        w[f"L0_attn_{n}"] = a[f"L0_attn_{n}"].reshape(2, 128).T
    w["L0_attn_A_log"] = two(a["L0_attn_A_log"])
    pick = np.zeros((128, 32, 128), np.float32)
    for part in (0, 64, 96):
        for n in range(32):
            pick[part + n, n, :] = 1.0
    w["bc_pick"] = pick.astype(mybir.dt.np(BF16))
    w["L3_ffn_b1"] = a["L3_ffn_b1"].reshape(4, 128).T
    w["L2_attn_Wqkv"] = np.concatenate([a[f"L2_attn_W{n}"].T for n in "qkv"], axis=1)
    w["L2_attn_Wo"] = a["L2_attn_Wo"].T
    w["L2_attn_norm_const"] = np.repeat(a["L2_attn_norm_const"].reshape(16), 8)
    head = np.arange(128) // 8
    w["same_head"] = (head[:, None] == head[None, :]).astype(np.float32)
    for n in ("router_W", "router_b", "W1", "b2"):
        w[f"L1_ffn_{n}"] = a[f"L1_ffn_{n}"]
    w["L1_ffn_W2"] = a["L1_ffn_W2"].reshape(-1, 128)
    w["L1_ffn_b1"] = a["L1_ffn_b1"].reshape(32, 128).T
    w["L1_ffn_ln_g"] = a["L1_ffn_ln_g"].T
    w["L1_ffn_ln_b"] = a["L1_ffn_ln_b"].T
    w["expert_index"] = np.arange(8, dtype=np.float32)
    w["expert_zero"] = np.zeros(8, np.float32)
    for n in ("router_w", "w1", "w2"):
        w[f"L0_ffn_{n}"] = a[f"L0_ffn_{n}"]
    w["L0_ffn_ln2_w"] = np.repeat(a["L0_ffn_ln2_w"][:, None], 8, axis=1)

    def spread(m):
        o = np.zeros((128, 4, 4, 32), np.float32)
        o[:, :, :, 0:8] = m.reshape(128, 4, 4, 8)
        return o.reshape(128, 4, 128)

    c_attn = a["L0_ffn_c_attn_w"]
    w["L0_ffn_wq"], w["L0_ffn_wk"], w["L0_ffn_wv"] = spread(c_attn[:, 0:128]), spread(c_attn[:, 128:256]), c_attn[:, 256:]
    w["L0_ffn_wo"] = a["L0_ffn_c_proj_w"]
    w["L0_ffn_ln1_w"] = a["L0_ffn_ln1_w"][:, None]
    kqv = a["L3_attn_W_kqv"].T
    w["L3_attn_wk"], w["L3_attn_wq"], w["L3_attn_wv"] = spread(kqv[:, 0:128]), spread(kqv[:, 128:256]), kqv[:, 256:]
    slopes = np.array([1.0 / (2.0 ** 8) ** ((h + 1) / 16.0) for h in range(16)]) * 128.0 ** 0.5
    at = np.arange(256)
    bq, bk = np.zeros((4, 32, 4, 256)), np.zeros((4, 32, 4, 256))
    for h in range(16):
        bq[h % 4, 8, h // 4], bk[h % 4, 8, h // 4] = 1.0, slopes[h] * at
        bq[h % 4, 9, h // 4], bk[h % 4, 9, h // 4] = -slopes[h] * at, 1.0
    w["alibi_q"], w["alibi_k"] = (b.reshape(128, 4, 256).astype(np.float32) for b in (bq, bk))
    row = np.arange(128)
    bf16 = mybir.dt.np(BF16)
    w["L2_ffn_wqkv"] = a["L2_ffn_wqkv"]
    w["L2_ffn_wo"] = a["L2_ffn_wo"]
    qs = np.stack([a["L2_ffn_q_scale"], a["L2_ffn_k_scale"]], axis=1)
    w["L2_ffn_qk_scale"] = qs
    w["L2_ffn_qk_scale_rot"] = np.roll(qs, 32, axis=-1)
    half = np.arange(0, 64, 2)
    angle = at[:, None] / 10000.0 ** (half / 64.0)[None, :]
    power = (at - 128) / 32.0
    xscale = ((half + 25.6) / 89.6)[None, :] ** power[:, None]
    both = lambda m: np.concatenate([m, m], axis=1)
    sign = np.where(np.arange(64) < 32, -1.0, 1.0)[None, :]
    cos = np.stack([both(np.cos(angle) * xscale), both(np.cos(angle) / xscale)], axis=1)
    sin = np.stack([both(np.sin(angle) * xscale) * sign, both(np.sin(angle) / xscale) * sign], axis=1)
    w["xpos_cos"], w["xpos_sin"] = (m.reshape(2, 128, 2, 64).transpose(1, 0, 2, 3).astype(np.float32) for m in (cos, sin))
    gap0 = row[:, None] - row[None, :]
    gap1 = row[:, None] + 64 - np.arange(192)[None, :]
    band = np.concatenate([gap0, gap1], axis=1)
    w["band_mask"] = np.where((band < 0) | (band > 64), -1e30, 0.0).astype(bf16)
    pad = lambda m, axis: np.concatenate([m, np.zeros(m.shape[:axis] + (43,) + m.shape[axis + 1:], np.float32)], axis=axis)
    w1 = a["L2_ffn_w1"]
    w["L2_ffn_w1"] = np.concatenate([pad(w1[:, :, :341], 2), pad(w1[:, :, 341:], 2)], axis=2)
    b1 = a["L2_ffn_b1"]
    w["L2_ffn_b1"] = np.concatenate([pad(b1[:, :341], 1), pad(b1[:, 341:], 1)], axis=1).reshape(2, 6, 128).transpose(0, 2, 1)
    w["L2_ffn_w2"] = pad(a["L2_ffn_w2"], 1)
    w["L2_ffn_b2"] = a["L2_ffn_b2"]
    w["L2_ffn_ln_g"] = a["L2_ffn_ln_g"][:, :, None]
    w["L2_ffn_ln_b"] = a["L2_ffn_ln_b"][:, :, None]
    w["row_before"] = np.eye(128, k=1, dtype=np.float32)
    corner = np.zeros((128, 128), np.float32)
    corner[127, 0] = 1.0
    w["row_before_tile"] = corner
    w["causal_mask"] = np.where(row[None, :] > row[:, None], -1e30, 0.0).astype(bf16)
    w["ident16"] = np.eye(128).astype(bf16)
    for n in ("w_disp", "w_val", "w_cproj", "b_val", "b_cproj", "b_bond_out"):
        w[f"L1_attn_{n}"] = a[f"L1_attn_{n}"]

    def per_head(m):
        o = np.zeros((8, 16, 8, 16), np.float32)
        for h in range(8):
            o[h, :, h, :] = m
        return o.reshape(128, 128)

    def out_columns(v):
        o = np.zeros((8, 16, 16, 8, 16), np.float32)
        for h in range(8):
            for k in range(16):
                o[h, :, k, h, k] = v[:, 0]
        return o.reshape(128, 16, 128)

    small = [a[f"L1_attn_w_{n}"] for n in ("state", "strain", "state_i", "state_j", "damage", "strain")]
    w["L1_attn_w_small"] = np.stack([per_head(m) for m in small], axis=1)
    w["L1_attn_w_bond"] = out_columns(a["L1_attn_w_bond_out"])
    w["L1_attn_w_damage_out"] = out_columns(a["L1_attn_w_damage_out"])
    heads8 = lambda v: np.tile(v, 8)
    w["L1_attn_biases"] = np.stack([a["L1_attn_b_disp"][:128], a["L1_attn_b_disp"][128:], heads8(a["L1_attn_b_state"]),
                                    heads8(a["L1_attn_b_strain"]), heads8(a["L1_attn_b_damage"]),
                                    np.repeat(a["L1_attn_b_damage_out"], 128)], axis=1)
    w["L1_attn_w_pos"] = np.tile(a["L1_attn_w_pos"], (1, 8))
    w["L1_attn_rel_emb"] = a["L1_attn_rel_pos_emb"].T
    key = at[:, None] - 31 + np.arange(32)[None, :]
    w["L1_attn_mask"] = np.where(key < 0, -1e30, 0.0).reshape(2, 128, 32).transpose(1, 0, 2).astype(np.float32)
    gap = at[None, :] - at[:, None]
    mean = ((gap >= 0) & (gap < 32)) / np.minimum(at + 1, 32)[None, :]
    w["L1_attn_mean_w"] = mean.reshape(2, 128, 256).transpose(1, 0, 2).astype(np.float32)
    return a["L0_attn_x"].reshape(-1, 128), {k: np.ascontiguousarray(v) for k, v in w.items()}


def kernel(**inputs):
    import numpy as np
    import concourse.bacc as bacc
    from concourse.bass_utils import run_bass_kernel_spmd

    x, w = layout(inputs)
    nc = bacc.Bacc("TRN2", target_bir_lowering=False, num_devices=1)
    arrays = {"x": np.ascontiguousarray(x), **w}
    aps = {n: nc.dram_tensor(n, a.shape, mybir.dt.from_np(a.dtype), kind="ExternalInput").ap() for n, a in arrays.items()}
    out = nc.dram_tensor("out", x.shape, F32, kind="ExternalOutput").ap()
    program(nc, aps["x"], aps, out, 32, ORDER)
    r = run_bass_kernel_spmd(nc, [arrays], core_ids=[0])
    return r.results[0]["out"].reshape(32, SEQ, P)
```
